# Optimizing a Trainium2 kernel written in Bass

```python
import numpy as np
import jax
import jax.numpy as jnp

def _softmax(x, axis=-1):
    return jax.nn.softmax(x, axis=axis)

def _gelu(x):
    return jax.nn.gelu(x, approximate=True)

def _silu(x):
    return jax.nn.silu(x)

def _sigmoid(x):
    return jax.nn.sigmoid(x)

def _layernorm(x, axis=-1, eps=1e-05):
    m = jnp.mean(x, axis=axis, keepdims=True)
    v = jnp.var(x, axis=axis, keepdims=True)
    return (x - m) / jnp.sqrt(v + eps)

def _scatter_add(tgt, idx, src, axis=0):
    return tgt.at[idx].add(src)

def _segment_sum(src, seg, n):
    return jax.ops.segment_sum(src, seg, n)
kernel_name = 'mk_adaln_ffn_d4_seqx_r8_61a915'

def setup_inputs(seed: int=0):
    np.random.seed(seed)
    _w = jnp.asarray

    def _rec_inputs():
        import jax
        import jax.numpy as jnp
        _rk = jax.random.key(seed)
        x = -0.000125 + 0.9999 * jax.random.normal(jax.random.fold_in(_rk, 1), (64, 32, 128), jnp.float32)
        _lenS = 32 - jax.random.randint(jax.random.fold_in(_rk, 7), (64,), 0, max(1, 32 // 4) + 1, jnp.int32)
        _lenS2 = 32 - jax.random.randint(jax.random.fold_in(_rk, 8), (64,), 0, max(1, 32 // 4) + 1, jnp.int32)
        cond_1024 = -0.00493535 + 1.00056 * jax.random.normal(jax.random.fold_in(_rk, 11), (64, 128), jnp.float32)
        return (x, cond_1024)
    x, cond_1024 = _rec_inputs()

    def _L0_cond_setup():
        import jax, jax.numpy as jnp
        import numpy as np
        N, T, D, H = (64, 64, 128, 128)
        key = jax.random.key(seed)
        k1, k2, k3, k4 = jax.random.split(key, 4)
        x = jax.random.normal(k1, (N, T, D), dtype=jnp.float32)
        h0 = jax.random.normal(k2, (N, H), dtype=jnp.float32)
        Wx = jax.random.normal(k3, (D, H), dtype=jnp.float32) / np.sqrt(D)
        Wh = jax.random.normal(k4, (H, H), dtype=jnp.float32) / np.sqrt(H)
        b = jnp.zeros((H,), dtype=jnp.float32)
        return {'x': x, 'h0': h0, 'Wx': Wx, 'Wh': Wh, 'b': b}
    _L0_cond_all = _L0_cond_setup()
    _L0_cond_in = {k: v for k, v in _L0_cond_all.items() if k in ('Wx', 'Wh', 'b')}
    del _L0_cond_all

    def _L0_ffn_setup():
        import jax, jax.numpy as jnp
        import numpy as np
        import math
        D_MODEL, D_FF, N_EXPERTS, TOP_K, N_SHARED = (128, 512, 8, 2, 1)
        B, T = (4, 128)
        SCALE = 1.0 / math.sqrt(N_SHARED + TOP_K / N_EXPERTS)
        key = jax.random.key(seed)
        ks = jax.random.split(key, 10)
        s1 = 1.0 / math.sqrt(D_MODEL)
        s2 = 1.0 / math.sqrt(D_FF)
        return {'x': jax.random.normal(ks[0], (B, T, D_MODEL), dtype=jnp.float32), 'w_router': jax.random.normal(ks[1], (N_EXPERTS, D_MODEL), dtype=jnp.float32) * s1, 'W1': jax.random.normal(ks[2], (N_EXPERTS, D_FF, D_MODEL), dtype=jnp.float32) * s1, 'b1': jax.random.normal(ks[3], (N_EXPERTS, D_FF), dtype=jnp.float32) * 0.02, 'W2': jax.random.normal(ks[4], (N_EXPERTS, D_MODEL, D_FF), dtype=jnp.float32) * s2, 'b2': jax.random.normal(ks[5], (N_EXPERTS, D_MODEL), dtype=jnp.float32) * 0.02, 'Ws1': jax.random.normal(ks[6], (D_FF, D_MODEL), dtype=jnp.float32) * s1, 'bs1': jax.random.normal(ks[7], (D_FF,), dtype=jnp.float32) * 0.02, 'Ws2': jax.random.normal(ks[8], (D_MODEL, D_FF), dtype=jnp.float32) * s2, 'bs2': jax.random.normal(ks[9], (D_MODEL,), dtype=jnp.float32) * 0.02}
    _L0_ffn_all = _L0_ffn_setup()
    _L0_ffn_in = {k: v for k, v in _L0_ffn_all.items() if k in ('w_router', 'W1', 'b1', 'W2', 'b2', 'Ws1', 'bs1', 'Ws2', 'bs2')}
    del _L0_ffn_all

    def _L1_cond_setup():
        import jax, jax.numpy as jnp
        import numpy as np
        N, T, D, H = (64, 64, 128, 128)

        def lstm_scan(x, h0, Wx, Wh, b):
            xW = jnp.einsum('ntd,dg->ntg', x, Wx) + b
            Hdim = h0.shape[1]
            c0 = jnp.zeros_like(h0)

            def step(carry, xw_t):
                prev_h, prev_c = carry
                a = xw_t + prev_h @ Wh
                i = jax.nn.sigmoid(a[:, :Hdim])
                f = jax.nn.sigmoid(a[:, Hdim:2 * Hdim])
                o = jax.nn.sigmoid(a[:, 2 * Hdim:3 * Hdim])
                g = jnp.tanh(a[:, 3 * Hdim:])
                next_c = f * prev_c + i * g
                next_h = o * jnp.tanh(next_c)
                return ((next_h, next_c), next_h)
            _, hs = jax.lax.scan(step, (h0, c0), jnp.swapaxes(xW, 0, 1))
            return jnp.swapaxes(hs, 0, 1)
        key = jax.random.key(seed)
        k1, k2, k3, k4 = jax.random.split(key, 4)
        x = jax.random.normal(k1, (N, T, D), dtype=jnp.float32)
        h0 = jax.random.normal(k2, (N, H), dtype=jnp.float32)
        Wx = jax.random.normal(k3, (D, 4 * H), dtype=jnp.float32) / np.sqrt(D)
        Wh = jax.random.normal(k4, (H, 4 * H), dtype=jnp.float32) / np.sqrt(H)
        b = jnp.zeros((4 * H,), dtype=jnp.float32)
        return {'x': x, 'h0': h0, 'Wx': Wx, 'Wh': Wh, 'b': b}
    _L1_cond_all = _L1_cond_setup()
    _L1_cond_in = {k: v for k, v in _L1_cond_all.items() if k in ('Wx', 'Wh', 'b')}
    del _L1_cond_all

    def _L1_ffn_setup():
        import jax, jax.numpy as jnp
        import numpy as np
        D_MODEL = 128
        D1, D2 = (32, 32)
        F1, F2 = (64, 64)
        E = 64
        TOP_K = 2

        def kmoe(x_flat, W_router, A, B, scale, bias, d_in1, d_in2, d_out1, d_out2, top_k):
            logits = x_flat @ W_router.T
            vals, idx = jax.lax.top_k(logits, top_k)
            probs = jax.nn.softmax(vals, axis=-1)
            xs = x_flat.reshape(-1, d_in1, d_in2)
            Ag = A[idx]
            Bg = B[idx]
            Y = jnp.einsum('nkoi,nij,nkpj->nkop', Ag, xs, Bg)
            out = jnp.einsum('nkop,nk->nop', Y, probs).reshape(-1, d_out1 * d_out2)
            return out * scale + bias
        key = jax.random.key(seed)
        ks = jax.random.split(key, 12)
        s = 0.02
        return {'x': jax.random.normal(ks[0], (4, 256, D_MODEL), dtype=jnp.float32), 'W_up': jax.random.normal(ks[1], (E, D1 * D2), dtype=jnp.float32) * s, 'A_up': jax.random.normal(ks[2], (E, F1, D1), dtype=jnp.float32) * s, 'B_up': jax.random.normal(ks[3], (E, F2, D2), dtype=jnp.float32) * s, 'scale_up': jnp.ones((1,), dtype=jnp.float32), 'bias_up': jnp.zeros((F1 * F2,), dtype=jnp.float32), 'W_down': jax.random.normal(ks[4], (E, F1 * F2), dtype=jnp.float32) * s, 'A_down': jax.random.normal(ks[5], (E, D1, F1), dtype=jnp.float32) * s, 'B_down': jax.random.normal(ks[6], (E, D2, F2), dtype=jnp.float32) * s, 'scale_down': jnp.ones((1,), dtype=jnp.float32), 'bias_down': jnp.zeros((D1 * D2,), dtype=jnp.float32)}
    _L1_ffn_all = _L1_ffn_setup()
    _L1_ffn_in = {k: v for k, v in _L1_ffn_all.items() if k in ('W_up', 'A_up', 'B_up', 'scale_up', 'bias_up', 'W_down', 'A_down', 'B_down', 'scale_down', 'bias_down')}
    del _L1_ffn_all

    def _L2_cond_setup():
        import jax, jax.numpy as jnp
        import numpy as np
        EPS = 1e-08
        key = jax.random.key(seed)
        ks = jax.random.split(key, 8)
        B, S, D, H = (8, 256, 128, 128)
        scale = 1.0 / np.sqrt(D)
        return {'input_seq': jax.random.normal(ks[0], (B, S, D), dtype=jnp.float32), 'initial_hidden': jax.random.normal(ks[1], (B, H), dtype=jnp.float32), 'W_f': jax.random.normal(ks[2], (H, D), dtype=jnp.float32) * scale, 'b_f': jnp.zeros((H,), dtype=jnp.float32), 'W_i': jax.random.normal(ks[3], (H, D), dtype=jnp.float32) * scale, 'b_i': jnp.zeros((H,), dtype=jnp.float32), 'W_h': jax.random.normal(ks[4], (H, D), dtype=jnp.float32) * scale, 'b_h': jnp.zeros((H,), dtype=jnp.float32)}
    _L2_cond_all = _L2_cond_setup()
    _L2_cond_in = {k: v for k, v in _L2_cond_all.items() if k in ('W_f', 'b_f', 'W_i', 'b_i', 'W_h', 'b_h')}
    del _L2_cond_all

    def _L2_ffn_setup():
        import jax, jax.numpy as jnp
        import numpy as np
        S, B, H, I, E = (64, 2, 128, 352, 8)
        key = jax.random.key(seed)
        ks = jax.random.split(key, 5)
        return {'hidden_states': jax.random.normal(ks[0], (S, B, H), dtype=jnp.float32), 'router_w': jax.random.normal(ks[1], (E, H), dtype=jnp.float32) * 0.02, 'gate_w': jax.random.normal(ks[2], (E, I, H), dtype=jnp.float32) * 0.02, 'up_w': jax.random.normal(ks[3], (E, I, H), dtype=jnp.float32) * 0.02, 'down_w': jax.random.normal(ks[4], (E, H, I), dtype=jnp.float32) * 0.02}
    _L2_ffn_all = _L2_ffn_setup()
    _L2_ffn_in = {k: v for k, v in _L2_ffn_all.items() if k in ('router_w', 'gate_w', 'up_w', 'down_w')}
    del _L2_ffn_all

    def _L3_cond_setup():
        import jax, jax.numpy as jnp
        import numpy as np
        B, T, D_IN, V_IN, E = (64, 128, 128, 128, 128)
        key = jax.random.key(seed)
        ks = jax.random.split(key, 16)
        s = 0.01
        return {'video': jax.random.normal(ks[0], (B, V_IN), jnp.float32), 'seq': jax.random.normal(ks[1], (B, T, D_IN), jnp.float32), 'W_z': jax.random.normal(ks[2], (D_IN, E), jnp.float32) * s, 'U_z': jax.random.normal(ks[3], (E, E), jnp.float32) * s, 'C_z': jax.random.normal(ks[4], (V_IN, E), jnp.float32) * s, 'b_z': jnp.zeros((E,), jnp.float32), 'W_r': jax.random.normal(ks[5], (D_IN, E), jnp.float32) * s, 'U_r': jax.random.normal(ks[6], (E, E), jnp.float32) * s, 'C_r': jax.random.normal(ks[7], (V_IN, E), jnp.float32) * s, 'b_r': jnp.zeros((E,), jnp.float32), 'W': jax.random.normal(ks[8], (D_IN, E), jnp.float32) * s, 'U': jax.random.normal(ks[9], (E, E), jnp.float32) * s, 'C': jax.random.normal(ks[10], (V_IN, E), jnp.float32) * s, 'b': jnp.zeros((E,), jnp.float32)}
    _L3_cond_all = _L3_cond_setup()
    _L3_cond_in = {k: v for k, v in _L3_cond_all.items() if k in ('W_z', 'U_z', 'C_z', 'b_z', 'W_r', 'U_r', 'C_r', 'b_r', 'W', 'U', 'C', 'b')}
    del _L3_cond_all

    def _L3_ffn_setup():
        import jax, jax.numpy as jnp
        import numpy as np
        D_MODEL = 128
        H_SHARED = 256
        H_ROUTED = 128
        N_EXPERTS = 8
        TOP_K = 2
        key = jax.random.key(seed)
        ks = jax.random.split(key, 8)
        B, T = (2, 256)
        sc_d = 1.0 / np.sqrt(D_MODEL)
        sc_hs = 1.0 / np.sqrt(H_SHARED)
        sc_hr = 1.0 / np.sqrt(H_ROUTED)
        return {'x': jax.random.normal(ks[0], (B, T, D_MODEL), dtype=jnp.float32), 'router_w': jax.random.normal(ks[1], (N_EXPERTS, D_MODEL), dtype=jnp.float32) * sc_d, 'router_bias': jnp.zeros((N_EXPERTS,), dtype=jnp.float32), 'sw1': jax.random.normal(ks[2], (D_MODEL, H_SHARED), dtype=jnp.float32) * sc_d, 'sw3': jax.random.normal(ks[3], (D_MODEL, H_SHARED), dtype=jnp.float32) * sc_d, 'sw2': jax.random.normal(ks[4], (H_SHARED, D_MODEL), dtype=jnp.float32) * sc_hs, 'ew1': jax.random.normal(ks[5], (N_EXPERTS, D_MODEL, H_ROUTED), dtype=jnp.float32) * sc_d, 'ew2': jax.random.normal(ks[6], (N_EXPERTS, H_ROUTED, D_MODEL), dtype=jnp.float32) * sc_hr}
    _L3_ffn_all = _L3_ffn_setup()
    _L3_ffn_in = {k: v for k, v in _L3_ffn_all.items() if k in ('router_w', 'router_bias', 'sw1', 'sw3', 'sw2', 'ew1', 'ew2')}
    del _L3_ffn_all
    return {'x': x, 'cond_1024': cond_1024, 'L0_cond_Wx': _L0_cond_in['Wx'], 'L0_cond_Wh': _L0_cond_in['Wh'], 'L0_cond_b': _L0_cond_in['b'], 'L0_ffn_w_router': _L0_ffn_in['w_router'], 'L0_ffn_W1': _L0_ffn_in['W1'], 'L0_ffn_b1': _L0_ffn_in['b1'], 'L0_ffn_W2': _L0_ffn_in['W2'], 'L0_ffn_b2': _L0_ffn_in['b2'], 'L0_ffn_Ws1': _L0_ffn_in['Ws1'], 'L0_ffn_bs1': _L0_ffn_in['bs1'], 'L0_ffn_Ws2': _L0_ffn_in['Ws2'], 'L0_ffn_bs2': _L0_ffn_in['bs2'], 'L1_cond_Wx': _L1_cond_in['Wx'], 'L1_cond_Wh': _L1_cond_in['Wh'], 'L1_cond_b': _L1_cond_in['b'], 'L1_ffn_W_up': _L1_ffn_in['W_up'], 'L1_ffn_A_up': _L1_ffn_in['A_up'], 'L1_ffn_B_up': _L1_ffn_in['B_up'], 'L1_ffn_scale_up': _L1_ffn_in['scale_up'], 'L1_ffn_bias_up': _L1_ffn_in['bias_up'], 'L1_ffn_W_down': _L1_ffn_in['W_down'], 'L1_ffn_A_down': _L1_ffn_in['A_down'], 'L1_ffn_B_down': _L1_ffn_in['B_down'], 'L1_ffn_scale_down': _L1_ffn_in['scale_down'], 'L1_ffn_bias_down': _L1_ffn_in['bias_down'], 'L2_cond_W_f': _L2_cond_in['W_f'], 'L2_cond_b_f': _L2_cond_in['b_f'], 'L2_cond_W_i': _L2_cond_in['W_i'], 'L2_cond_b_i': _L2_cond_in['b_i'], 'L2_cond_W_h': _L2_cond_in['W_h'], 'L2_cond_b_h': _L2_cond_in['b_h'], 'L2_ffn_router_w': _L2_ffn_in['router_w'], 'L2_ffn_gate_w': _L2_ffn_in['gate_w'], 'L2_ffn_up_w': _L2_ffn_in['up_w'], 'L2_ffn_down_w': _L2_ffn_in['down_w'], 'L3_cond_W_z': _L3_cond_in['W_z'], 'L3_cond_U_z': _L3_cond_in['U_z'], 'L3_cond_C_z': _L3_cond_in['C_z'], 'L3_cond_b_z': _L3_cond_in['b_z'], 'L3_cond_W_r': _L3_cond_in['W_r'], 'L3_cond_U_r': _L3_cond_in['U_r'], 'L3_cond_C_r': _L3_cond_in['C_r'], 'L3_cond_b_r': _L3_cond_in['b_r'], 'L3_cond_W': _L3_cond_in['W'], 'L3_cond_U': _L3_cond_in['U'], 'L3_cond_C': _L3_cond_in['C'], 'L3_cond_b': _L3_cond_in['b'], 'L3_ffn_router_w': _L3_ffn_in['router_w'], 'L3_ffn_router_bias': _L3_ffn_in['router_bias'], 'L3_ffn_sw1': _L3_ffn_in['sw1'], 'L3_ffn_sw3': _L3_ffn_in['sw3'], 'L3_ffn_sw2': _L3_ffn_in['sw2'], 'L3_ffn_ew1': _L3_ffn_in['ew1'], 'L3_ffn_ew2': _L3_ffn_in['ew2']}

def reference(x, cond_1024, L0_cond_Wx, L0_cond_Wh, L0_cond_b, L0_ffn_w_router, L0_ffn_W1, L0_ffn_b1, L0_ffn_W2, L0_ffn_b2, L0_ffn_Ws1, L0_ffn_bs1, L0_ffn_Ws2, L0_ffn_bs2, L1_cond_Wx, L1_cond_Wh, L1_cond_b, L1_ffn_W_up, L1_ffn_A_up, L1_ffn_B_up, L1_ffn_scale_up, L1_ffn_bias_up, L1_ffn_W_down, L1_ffn_A_down, L1_ffn_B_down, L1_ffn_scale_down, L1_ffn_bias_down, L2_cond_W_f, L2_cond_b_f, L2_cond_W_i, L2_cond_b_i, L2_cond_W_h, L2_cond_b_h, L2_ffn_router_w, L2_ffn_gate_w, L2_ffn_up_w, L2_ffn_down_w, L3_cond_W_z, L3_cond_U_z, L3_cond_C_z, L3_cond_b_z, L3_cond_W_r, L3_cond_U_r, L3_cond_C_r, L3_cond_b_r, L3_cond_W, L3_cond_U, L3_cond_C, L3_cond_b, L3_ffn_router_w, L3_ffn_router_bias, L3_ffn_sw1, L3_ffn_sw3, L3_ffn_sw2, L3_ffn_ew1, L3_ffn_ew2):
    import jax
    import jax.numpy as jnp

    def _L0_cond_ref(x, h0, Wx, Wh, b):
        import jax, jax.numpy as jnp
        import numpy as np
        N, T, D, H = (64, 64, 128, 128)
        xw = jnp.einsum('ntd,dh->nth', x, Wx) + b

        def step(prev_h, xw_t):
            next_h = jnp.tanh(prev_h @ Wh + xw_t)
            return (next_h, next_h)
        _, hs = jax.lax.scan(step, h0, jnp.swapaxes(xw, 0, 1))
        return jnp.swapaxes(hs, 0, 1)

    def _L0_ffn_ref(x, w_router, W1, b1, W2, b2, Ws1, bs1, Ws2, bs2):
        import jax, jax.numpy as jnp
        import numpy as np
        import math
        D_MODEL, D_FF, N_EXPERTS, TOP_K, N_SHARED = (128, 512, 8, 2, 1)
        B, T = (4, 128)
        SCALE = 1.0 / math.sqrt(N_SHARED + TOP_K / N_EXPERTS)
        logits = jnp.einsum('btd,ed->bte', x, w_router)
        probs = jax.nn.softmax(logits, axis=-1)
        vals, idx = jax.lax.top_k(probs, TOP_K)
        gates = jnp.sum(jax.nn.one_hot(idx, N_EXPERTS, dtype=x.dtype) * vals[..., None], axis=-2)
        hs = jax.nn.gelu(jnp.einsum('btd,fd->btf', x, Ws1) + bs1)
        acc = jnp.einsum('btf,df->btd', hs, Ws2) + bs2
        h = jax.nn.gelu(jnp.einsum('btd,efd->btef', x, W1) + b1)
        y = jnp.einsum('btef,edf->bted', h, W2) + b2
        acc = acc + jnp.einsum('bted,bte->btd', y, gates)
        return SCALE * acc

    def _L1_cond_ref(x, h0, Wx, Wh, b):
        import jax, jax.numpy as jnp
        import numpy as np
        N, T, D, H = (64, 64, 128, 128)

        def lstm_scan(x, h0, Wx, Wh, b):
            xW = jnp.einsum('ntd,dg->ntg', x, Wx) + b
            Hdim = h0.shape[1]
            c0 = jnp.zeros_like(h0)

            def step(carry, xw_t):
                prev_h, prev_c = carry
                a = xw_t + prev_h @ Wh
                i = jax.nn.sigmoid(a[:, :Hdim])
                f = jax.nn.sigmoid(a[:, Hdim:2 * Hdim])
                o = jax.nn.sigmoid(a[:, 2 * Hdim:3 * Hdim])
                g = jnp.tanh(a[:, 3 * Hdim:])
                next_c = f * prev_c + i * g
                next_h = o * jnp.tanh(next_c)
                return ((next_h, next_c), next_h)
            _, hs = jax.lax.scan(step, (h0, c0), jnp.swapaxes(xW, 0, 1))
            return jnp.swapaxes(hs, 0, 1)
        return lstm_scan(x, h0, Wx, Wh, b)

    def _L1_ffn_ref(x, W_up, A_up, B_up, scale_up, bias_up, W_down, A_down, B_down, scale_down, bias_down):
        import jax, jax.numpy as jnp
        import numpy as np
        D_MODEL = 128
        D1, D2 = (32, 32)
        F1, F2 = (64, 64)
        E = 64
        TOP_K = 2

        def kmoe(x_flat, W_router, A, B, scale, bias, d_in1, d_in2, d_out1, d_out2, top_k):
            logits = x_flat @ W_router.T
            vals, idx = jax.lax.top_k(logits, top_k)
            probs = jax.nn.softmax(vals, axis=-1)
            xs = x_flat.reshape(-1, d_in1, d_in2)
            Ag = A[idx]
            Bg = B[idx]
            Y = jnp.einsum('nkoi,nij,nkpj->nkop', Ag, xs, Bg)
            out = jnp.einsum('nkop,nk->nop', Y, probs).reshape(-1, d_out1 * d_out2)
            return out * scale + bias
        orig_shape = x.shape
        x_flat = x.reshape(-1, D1 * D2)
        h = kmoe(x_flat, W_up, A_up, B_up, scale_up, bias_up, D1, D2, F1, F2, TOP_K)
        h = jax.nn.gelu(h, approximate=False)
        y = kmoe(h, W_down, A_down, B_down, scale_down, bias_down, F1, F2, D1, D2, TOP_K)
        return y.reshape(*orig_shape[:-1], D_MODEL)

    def _L2_cond_ref(input_seq, initial_hidden, W_f, b_f, W_i, b_i, W_h, b_h):
        import jax, jax.numpy as jnp
        import numpy as np
        EPS = 1e-08
        forget_gate = jax.nn.sigmoid(jnp.einsum('bsd,hd->bsh', input_seq, W_f) + b_f)
        input_gate = jax.nn.sigmoid(jnp.einsum('bsd,hd->bsh', input_seq, W_i) + b_i)
        gate_sum = forget_gate + input_gate + EPS
        forget_norm = forget_gate / gate_sum
        input_norm = input_gate / gate_sum
        candidate = jnp.einsum('bsd,hd->bsh', input_seq, W_h) + b_h
        new_info = input_norm * candidate
        log_ret = jnp.log(forget_norm + EPS)
        log_cumprod = jnp.cumsum(log_ret, axis=1)
        B, _, H = log_cumprod.shape
        padded = jnp.concatenate([jnp.zeros((B, 1, H), dtype=log_cumprod.dtype), log_cumprod], axis=1)
        scaling = jnp.exp(log_cumprod[:, -1:, :] - padded[:, :-1, :])
        hidden = jnp.cumsum(scaling * new_info, axis=1)
        hidden = hidden + jnp.exp(log_cumprod) * initial_hidden[:, None, :]
        return hidden

    def _L2_ffn_ref(hidden_states, router_w, gate_w, up_w, down_w):
        import jax, jax.numpy as jnp
        import numpy as np
        S, B, H, I, E = (64, 2, 128, 352, 8)
        router_logits = jnp.einsum('sbh,eh->sbe', hidden_states, router_w)
        routing_indices = jnp.argmax(router_logits, axis=-1)
        out = jnp.zeros_like(hidden_states)
        for e in range(E):
            mask = (routing_indices == e)[..., None]
            xe = jnp.where(mask, hidden_states, 0.0)
            g = jnp.einsum('sbh,ih->sbi', xe, gate_w[e])
            u = jnp.einsum('sbh,ih->sbi', xe, up_w[e])
            ye = jnp.einsum('sbi,hi->sbh', jax.nn.silu(g) * u, down_w[e])
            out = out + jnp.where(mask, ye, 0.0)
        return out

    def _L3_cond_ref(video, seq, W_z, U_z, C_z, b_z, W_r, U_r, C_r, b_r, W, U, C, b):
        import jax, jax.numpy as jnp
        import numpy as np
        B, T, D_IN, V_IN, E = (64, 128, 128, 128, 128)
        vz = video @ C_z + b_z
        vr = video @ C_r + b_r
        vh = video @ C + b
        xz = jnp.einsum('btd,de->bte', seq, W_z)
        xr = jnp.einsum('btd,de->bte', seq, W_r)
        xh = jnp.einsum('btd,de->bte', seq, W)

        def step(h, xs):
            xzt, xrt, xht = xs
            z = jax.nn.sigmoid(xzt + h @ U_z + vz)
            r = jax.nn.sigmoid(xrt + h @ U_r + vr)
            hh = jnp.tanh(xht + r * h @ U + vh)
            h_new = (1.0 - z) * h + z * hh
            return (h_new, h_new)
        h0 = jnp.zeros((seq.shape[0], U.shape[0]), seq.dtype)
        xs = (jnp.swapaxes(xz, 0, 1), jnp.swapaxes(xr, 0, 1), jnp.swapaxes(xh, 0, 1))
        _, out_t = jax.lax.scan(step, h0, xs)
        return jnp.swapaxes(out_t, 0, 1)

    def _L3_ffn_ref(x, router_w, router_bias, sw1, sw3, sw2, ew1, ew2):
        import jax, jax.numpy as jnp
        import numpy as np
        D_MODEL = 128
        H_SHARED = 256
        H_ROUTED = 128
        N_EXPERTS = 8
        TOP_K = 2
        B, T, C = x.shape
        xf = x.reshape(-1, C)
        shared_out = jax.nn.silu(xf @ sw1) * (xf @ sw3) @ sw2
        s = jax.nn.sigmoid((xf @ router_w.T).astype(jnp.float32))
        sel_scores = s + router_bias.astype(jnp.float32)
        _, topk_idx = jax.lax.top_k(sel_scores, TOP_K)
        s_sel = jnp.take_along_axis(s, topk_idx, axis=1)
        denom = s_sel.sum(axis=1, keepdims=True)
        gates = jnp.where(denom > 1e-09, s_sel / (denom + 1e-09), 1.0 / TOP_K).astype(x.dtype)
        one_hot = jax.nn.one_hot(topk_idx, N_EXPERTS, dtype=x.dtype)
        comb = jnp.einsum('nke,nk->ne', one_hot, gates)
        h = jax.nn.gelu(jnp.einsum('nd,edh->neh', xf, ew1), approximate=False)
        y = jnp.einsum('neh,ehd->ned', h, ew2)
        routed_out = jnp.einsum('ned,ne->nd', y, comb)
        return (shared_out + routed_out).reshape(B, T, C)
    x = x + _L0_ffn_ref(_L0_cond_ref(x, cond_1024, L0_cond_Wx, L0_cond_Wh, L0_cond_b), L0_ffn_w_router, L0_ffn_W1, L0_ffn_b1, L0_ffn_W2, L0_ffn_b2, L0_ffn_Ws1, L0_ffn_bs1, L0_ffn_Ws2, L0_ffn_bs2)
    x = x + _L1_ffn_ref(_L1_cond_ref(x, cond_1024, L1_cond_Wx, L1_cond_Wh, L1_cond_b), L1_ffn_W_up, L1_ffn_A_up, L1_ffn_B_up, L1_ffn_scale_up, L1_ffn_bias_up, L1_ffn_W_down, L1_ffn_A_down, L1_ffn_B_down, L1_ffn_scale_down, L1_ffn_bias_down)
    x = x + _L2_ffn_ref(_L2_cond_ref(x, cond_1024, L2_cond_W_f, L2_cond_b_f, L2_cond_W_i, L2_cond_b_i, L2_cond_W_h, L2_cond_b_h), L2_ffn_router_w, L2_ffn_gate_w, L2_ffn_up_w, L2_ffn_down_w)
    x = x + _L3_ffn_ref(_L3_cond_ref(cond_1024, x, L3_cond_W_z, L3_cond_U_z, L3_cond_C_z, L3_cond_b_z, L3_cond_W_r, L3_cond_U_r, L3_cond_C_r, L3_cond_b_r, L3_cond_W, L3_cond_U, L3_cond_C, L3_cond_b), L3_ffn_router_w, L3_ffn_router_bias, L3_ffn_sw1, L3_ffn_sw3, L3_ffn_sw2, L3_ffn_ew1, L3_ffn_ew2)
    return x

_drawn_inputs = setup_inputs


def setup_inputs(seed=0):
    import zlib

    import numpy as np

    out = dict(_drawn_inputs(seed))
    spreads = {'L0_cond_b': (0.0, 0.1),
     'L1_cond_b': (0.0, 0.8),
     'L1_ffn_bias_up': (0.0, 0.8),
     'L1_ffn_bias_down': (0.0, 0.1),
     'L2_cond_b_f': (0.0, 0.8),
     'L2_cond_b_i': (0.0, 0.8),
     'L2_cond_b_h': (0.0, 0.8),
     'L3_cond_b_z': (0.0, 0.8),
     'L3_cond_b_r': (0.0, 0.8),
     'L3_cond_b': (0.0, 0.1),
     'L3_ffn_router_bias': (0.0, 0.8)}
    factors = {'L0_ffn_b1': 8.0,
     'L0_ffn_b2': 8.0,
     'L0_ffn_bs1': 5.427,
     'L0_ffn_bs2': 3.043,
     'L1_cond_Wx': 8.0,
     'L1_cond_Wh': 8.0,
     'L1_ffn_W_up': 8.0,
     'L1_ffn_A_up': 8.0,
     'L1_ffn_B_up': 8.0,
     'L1_ffn_W_down': 8.0,
     'L1_ffn_A_down': 8.0,
     'L1_ffn_B_down': 8.0,
     'L2_cond_W_f': 8.0,
     'L2_cond_W_i': 8.0,
     'L2_cond_W_h': 8.0,
     'L2_ffn_router_w': 8.0,
     'L2_ffn_gate_w': 8.0,
     'L2_ffn_up_w': 8.0,
     'L2_ffn_down_w': 8.0,
     'L3_cond_W_z': 8.0,
     'L3_cond_U_z': 8.0,
     'L3_cond_C_z': 8.0,
     'L3_cond_W_r': 8.0,
     'L3_cond_U_r': 40.825,
     'L3_cond_C_r': 8.0,
     'L3_cond_U': 8.0,
     'L3_ffn_router_w': 20.709,
     'L3_ffn_sw1': 4.809,
     'L3_ffn_sw3': 4.567,
     'L3_ffn_sw2': 4.496,
     'L3_ffn_ew1': 5.785,
     'L3_ffn_ew2': 5.608}
    for name, (base, spread) in spreads.items():
        noise = np.random.default_rng([zlib.crc32(name.encode()), seed]).standard_normal(out[name].shape)
        drawn = base * np.exp(spread * noise) if base else spread * noise
        out[name] = jnp.asarray(drawn.astype(out[name].dtype))
    for name, factor in factors.items():
        out[name] = (out[name] * factor).astype(out[name].dtype)
    return out
```

```python
from contextlib import ExitStack

import numpy as np
import concourse.bass as bass
from concourse import mybir

F32 = mybir.dt.float32
BF16 = mybir.dt.bfloat16
U32 = mybir.dt.uint32
ACT = mybir.ActivationFunctionType
ALU = mybir.AluOpType
AX = mybir.AxisListType.X

P = 128
T = 32
N = 64
TOK = T * N
TILE = 512
NT = TOK // TILE
G = TOK // P
BANK = 512
L0_SCALE = 1.0 / float(np.sqrt(1 + 2 / 8))


def chain(eng, sem, start=0):
    count = [start]

    def link(ins):
        count[0] += 1
        ins.then_inc(sem, 1)
        eng.wait_ge(sem, count[0])
        return count[0]

    return link


class Memory:

    semaphores = None

    def __init__(self, nc, tag):
        self.nc, self.tag, self.ctx = nc, tag, ExitStack()

    def __enter__(self):
        self.ctx.__enter__()
        return self

    def __exit__(self, *a):
        return self.ctx.__exit__(*a)

    def sb(self, name, shape, dt=F32):
        return self.ctx.enter_context(self.nc.sbuf_tensor(f"{self.tag}_{name}", shape, dt))

    def ps(self, name, shape, dt=F32):
        return self.ctx.enter_context(self.nc.psum_tensor(f"{self.tag}_{name}", shape, dt))

    def sem(self, name):
        return Memory.semaphores.enter_context(self.nc.semaphore(f"{self.tag}_{name}"))

    def block(self):
        return self.ctx.enter_context(self.nc.Block())


def load_state(nc, x, d, S):
    with Memory(nc, "load") as m:
        s_in, s_zero, s_id = m.sem("in"), m.sem("zero"), m.sem("id")
        block = m.block()

        @block.sync
        def _(sp):
            sp.dma_start(x[:], d["xT"]).then_inc(s_in, 16)
            sp.dma_start(S["cond"][:], d["condT"]).then_inc(s_in, 16)
            sp.wait_ge(s_in, 32)

        @block.gpsimd
        def _(pool):
            pool.memset(S["ident"][:], 0.0).then_inc(s_zero, 1)
            pool.wait_ge(s_zero, 1)
            pool.affine_select(out=S["ident"][:], in_=S["ident"][:], compare_op=ALU.not_equal, fill=1.0,
                               base=0, pattern=[[-1, P]], channel_multiplier=1).then_inc(s_id, 1)
            pool.wait_ge(s_id, 1)


def store_state(nc, x, out):
    with Memory(nc, "store") as m:
        s_out = m.sem("out")
        block = m.block()

        @block.sync
        def _(sp):
            sp.dma_start(out, x[:]).then_inc(s_out, 16)
            sp.wait_ge(s_out, 16)


def rnn(nc, x, h, d, S):
    with Memory(nc, "rnn") as m:
        wx, wh, b, warm = m.sb("wx", [P, P]), m.sb("wh", [P, P]), m.sb("b", [P, 1]), m.sb("warm", [P, 1])
        pre = m.ps("pre", [P, 2, BANK])
        s_w, s_pre, s_h = m.sem("w"), m.sem("pre"), m.sem("h")
        block = m.block()

        @block.sync
        def _(sp):
            sp.dma_start(wx[:], d["l0_wx"]).then_inc(s_w, 16)
            sp.dma_start(wh[:], d["l0_wh"]).then_inc(s_w, 16)
            sp.dma_start(b[:], d["l0_b"]).then_inc(s_w, 16)

        @block.vector
        def _(dve):
            nc.vector.tensor_copy(h[:, 0, :], S["cond"][:]).then_inc(s_h, 1)

        @block.tensor
        def _(pe):
            pe.wait_ge(s_w, 48)
            with pe.Fori(0, T // 2) as i:
                for j in range(2):
                    t = i * 2 + j
                    nc.tensor.matmul(pre[:, j, 0:N], wx[:], x[:, t, :], start=True, stop=False)
                    pe.wait_ge(s_h, t + 1)
                    nc.tensor.matmul(pre[:, j, 0:N], wh[:], h[:, t, :], start=False, stop=True).then_inc(s_pre, 1)

        @block.scalar
        def _(act):
            act.wait_ge(s_w, 48)
            nc.scalar.activation(warm[:], b[:], ACT.Tanh)
            with act.Fori(0, T // 2) as i:
                for j in range(2):
                    t = i * 2 + j
                    act.wait_ge(s_pre, t + 1)
                    nc.scalar.activation(h[:, t + 1, :], pre[:, j, 0:N], ACT.Tanh, bias=b[:]).then_inc(s_h, 1)


def lstm(nc, x, h, d, S):
    with Memory(nc, "lstm") as m:
        wx, wh, b = m.sb("wx", [P, 4, P]), m.sb("wh", [P, 4, P]), m.sb("b", [P, 4])
        bias, warm = m.sb("bias", [P, 4, N]), m.sb("warm", [P, 4])
        c, sig, g, fc, ig, tc = (m.sb(k, [P, w, N]) for k, w in
                                 (("c", 1), ("sig", 3), ("g", 1), ("fc", 1), ("ig", 1), ("tc", 1)))
        pre = m.ps("pre", [P, 2, BANK])
        s_w, s_bias, s_pre, s_gates, s_own, s_c, s_tc, s_h = (
            m.sem(k) for k in ("w", "bias", "pre", "gates", "own", "c", "tc", "h"))
        block = m.block()

        @block.sync
        def _(sp):
            sp.dma_start(wx[:], d["l1_wx"]).then_inc(s_w, 16)
            sp.dma_start(wh[:], d["l1_wh"]).then_inc(s_w, 16)
            sp.dma_start(b[:], d["l1_b"]).then_inc(s_w, 16)

        @block.tensor
        def _(pe):
            pe.wait_ge(s_w, 48)
            pe.wait_ge(s_bias, 1)
            with pe.Fori(0, T // 2) as i:
                for j in range(2):
                    t = i * 2 + j
                    nc.tensor.matmul(pre[:, j, 0:4 * N], S["ident"][:], bias[:].rearrange("p k n -> p (k n)"),
                                     start=True, stop=False)
                    for k in range(4):
                        nc.tensor.matmul(pre[:, j, k * N:(k + 1) * N], wx[:, k, :], x[:, t, :],
                                         start=False, stop=False)
                    pe.wait_ge(s_h, t + 1)
                    for k in range(4):
                        last = nc.tensor.matmul(pre[:, j, k * N:(k + 1) * N], wh[:, k, :], h[:, t, :],
                                                start=False, stop=(k == 3))
                    last.then_inc(s_pre, 1)

        @block.scalar
        def _(act):
            act.wait_ge(s_w, 48)
            nc.scalar.activation(warm[:], b[:], ACT.Sigmoid)
            with act.Fori(0, T // 2) as i:
                for j in range(2):
                    t = i * 2 + j
                    act.wait_ge(s_pre, t + 1)
                    nc.scalar.activation(sig[:].rearrange("p k n -> p (k n)"), pre[:, j, 0:3 * N], ACT.Sigmoid)
                    nc.scalar.activation(g[:, 0, :], pre[:, j, 3 * N:4 * N], ACT.Tanh).then_inc(s_gates, 1)
                    act.wait_ge(s_c, t + 1)
                    nc.scalar.activation(tc[:, 0, :], c[:, 0, :], ACT.Tanh).then_inc(s_tc, 1)

        @block.vector
        def _(dve):
            nc.vector.tensor_copy(h[:, 0, :], S["cond"][:]).then_inc(s_h, 1)
            nc.vector.memset(c[:], 0.0)
            dve.wait_ge(s_w, 48)
            nc.vector.tensor_copy(bias[:], b[:].rearrange("p (k o) -> p k o", o=1).to_broadcast([P, 4, N])).then_inc(s_bias, 1)
            dve.wait_ge(s_bias, 1)
            with dve.Fori(0, T // 2) as i:
                for j in range(2):
                    t = i * 2 + j
                    dve.wait_ge(s_gates, t + 1)
                    nc.vector.tensor_tensor(fc[:], sig[:, 1:2, :], c[:], ALU.mult).then_inc(s_own, 1)
                    nc.vector.tensor_tensor(ig[:], sig[:, 0:1, :], g[:], ALU.mult).then_inc(s_own, 1)
                    dve.wait_ge(s_own, t * 2 + 2)
                    nc.vector.tensor_tensor(c[:], fc[:], ig[:], ALU.add).then_inc(s_c, 1)
                    dve.wait_ge(s_tc, t + 1)
                    nc.vector.tensor_tensor(h[:, t + 1, :], sig[:, 2, :], tc[:, 0, :], ALU.mult).then_inc(s_h, 1)


E64 = 64
TB = T // 8
BLK = TB * N // 4


class Turns:

    def __init__(self, depth):
        self.depth = depth

    def run(self, eng, step):
        for s in range(4):
            step(s, s % 2)
        with eng.Fori(2, BLK // 2) as i:
            for j in range(2):
                step(i * 2 + j, j)
        for s in range(BLK, BLK + self.depth):
            step(s, s % 2)


def live(v):
    return not isinstance(v, int) or 0 <= v < BLK


def freed(eng, sem, v):
    if not isinstance(v, int) or v >= 2:
        eng.wait_ge(sem, v - 1)


def split_tables(nc, d, K):
    with Memory(nc, "split") as m:
        tab = [m.sb(f"t{i}", [P, 2048]) for i in range(4)]
        mid = [m.sb(f"m{i}", [E64, 2048], BF16) for i in range(4)]
        s_in = [m.sem(f"in{i}") for i in range(4)]
        s_act, s_dve, s_pool = m.sem("act"), m.sem("dve"), m.sem("pool")
        block = m.block()

        @block.sync
        def _(sp):
            for i in range(4):
                sp.dma_start(tab[i][:], d["k_tab"][i]).then_inc(s_in[i], 16)
            for i in range(4):
                sp.wait_ge(s_in[i], 16)

        @block.scalar
        def _(act):
            for i in range(4):
                act.wait_ge(s_in[i], 16)
                nc.scalar.copy(K["hm"][i][:], tab[i][:]).then_inc(s_act, 1)
            for i in range(4):
                act.wait_ge(s_dve, i + 1)
                nc.scalar.copy(mid[i][:], tab[i][0:E64, :]).then_inc(s_act, 1)
                nc.scalar.copy(K["hm"][i][E64:P, :], tab[i][E64:P, :]).then_inc(s_act, 1)

        @block.vector
        def _(dve):
            for i in range(4):
                dve.wait_ge(s_act, i + 1)
                nc.vector.tensor_tensor(tab[i][:], tab[i][:], K["hm"][i][:], ALU.subtract).then_inc(s_dve, 1)
            for i in range(4):
                dve.wait_ge(s_act, 4 + 2 * i + 1)
                nc.vector.tensor_tensor(K["lo"][i][:], tab[i][0:E64, :], mid[i][:], ALU.subtract).then_inc(s_dve, 1)


def pick_two(nc, pick, link, logits, K, halves):
    top, idx, idxf, hot = pick
    for r in range(2):
        link(nc.vector.tensor_copy(halves[:, r, :], logits(r)))
        link(nc.vector.max(top[:, r, :], halves[:, r, :]))
        link(nc.vector.max_index(idx[:, r, :], top[:, r, :], halves[:, r, :]))
    link(nc.vector.tensor_copy(idxf[:], idx[:]))
    for r in range(2):
        for k in range(2):
            link(nc.vector.tensor_scalar(hot[:, r, k, :], K["iota"], idxf[:, r, k:k + 1], None, ALU.is_equal))


def kron_route(nc, tag, mats, d, K, hotT, prob, probs_dram, cls, scale_key):
    with Memory(nc, tag) as m:
        bankL = m.ps("logits", [P, 2, BANK])
        psT = m.ps("hotT", [P, 2, 2, 2 * BANK], BF16)
        halves = m.sb("halves", [P, 2, E64])
        pr = m.sb("pr", [P, 2, 2])
        diff = m.sb("diff", [P, 2, 2])
        NBK = 8 * BLK // cls
        pb = m.sb("pb", [P, NBK])
        top, idx, idxf = m.sb("top", [P, 2, 8]), m.sb("idx", [P, 2, 8], U32), m.sb("idxf", [P, 2, 8])
        hot = m.sb("hot", [P, 2, 2, P], BF16)
        sc = m.sb("sc", [P, 1])
        s_logits, s_own, s_hot, s_T, s_diff, s_pr, s_dram, s_pb, s_sc, s_hotT = (
            m.sem(k) for k in ("logits", "own", "hot", "T", "diff", "pr", "dram", "pb", "sc", "hotT"))
        block = m.block()
        @block.sync
        def _(sp):
            sp.dma_start(sc[:], d[scale_key]).then_inc(s_sc, 16)
            sp.wait_ge(s_pr, 1)
            for r in range(2):
                if cls == 4:
                    dst = probs_dram.rearrange("c (b k) -> b c k", k=2)[r * BLK // 2:(r + 1) * BLK // 2, :, :]
                else:
                    dst = probs_dram.rearrange("c (b k) -> c b k", k=2)[r, :, :]
                sp.dma_start(dst, pr[:, r, :]).then_inc(s_dram, 16)
            sp.wait_ge(s_dram, 32)
            w = P // cls
            for c in range(cls):
                sp.dma_start(pb[c * w:(c + 1) * w, :], probs_dram[c:c + 1, :].to_broadcast([w, NBK])).then_inc(s_pb, 16)

        @block.tensor
        def _(pe):
            for r in range(2):
                mats(pe, r, lambda *a, **k: nc.tensor.matmul(bankL[:, r, 0:E64], *a, **k)).then_inc(s_logits, 1)
            pe.wait_ge(s_hot, 1)
            for r in range(2):
                for k in range(2):
                    nc.tensor.transpose(psT[:, r, k, 0:P], hot[:, r, k, :], K["identb"][:]).then_inc(s_T, 1)

        @block.vector
        def _(dve):
            link = chain(dve, s_own)
            dve.wait_ge(s_logits, 2)
            pick_two(nc, (top, idx, idxf, hot), link, lambda r: bankL[:, r, 0:E64], K, halves)
            nc.vector.tensor_tensor(diff[:, :, 0:1], top[:, :, 0:1], top[:, :, 1:2], ALU.subtract).then_inc(s_hot, 1)
            nc.vector.tensor_tensor(diff[:, :, 1:2], top[:, :, 1:2], top[:, :, 0:1], ALU.subtract).then_inc(s_diff, 1)
            dve.wait_ge(s_T, 4)
            for r in range(2):
                for k in range(2):
                    src = psT[:, r, k, 0:P]
                    if cls == 4:
                        dst = hotT[:].rearrange("p c (b k) -> p k b c", k=2)[:, k, r * BLK // 2:(r + 1) * BLK // 2, :]
                        src = src.rearrange("p (b c) -> p b c", c=4)
                    else:
                        dst = hotT[:].rearrange("p c (b k) -> p c k b", k=2)[:, r, k, :]
                    nc.vector.tensor_copy(dst, src).then_inc(s_hotT, 1)
            dve.wait_ge(s_pb, 16 * cls)
            dve.wait_ge(s_sc, 16)
            link(nc.vector.tensor_scalar(pb[:], pb[:], sc[:], None, ALU.mult))
            for q in range(2):
                link(nc.vector.tensor_scalar(prob[:, :, q], pb[:], K["half4" if cls == 4 else "half2"][:, q:q + 1], None, ALU.mult))

        @block.scalar
        def _(act):
            act.wait_ge(s_diff, 1)
            act.wait_ge(s_hot, 1)
            nc.scalar.activation(pr[:], diff[:], ACT.Sigmoid).then_inc(s_pr, 1)


def kron_gather(nc, tag, K, tabs, hotT, dst, cls):
    w = P // cls
    PER = P // w
    COLS = BANK // PER
    TURNS = 2048 // P
    with Memory(nc, tag) as m:
        hm = [m.sb(f"hm{j}", [P, 2, P], BF16) for j in range(2)]
        lo = [m.sb(f"lo{j}", [E64, 2, P], BF16) for j in range(2)]
        out = m.ps("out", [P, 2, 2, BANK])
        s_stage, s_pick, s_gotA, s_gotB = (m.sem(k) for k in ("stage", "pick", "gotA", "gotB"))
        block = m.block()

        def loop(eng, turn):
            for v in range(2):
                turn(v, v)
            with eng.Fori(1, TURNS // 2) as i:
                for j in range(2):
                    turn(i * 2 + j, j)

        @block.gpsimd
        def _(pool):
            def turn(v, j):
                freed(pool, s_pick, v)
                for t in range(2):
                    c = bass.ds(v * P, P)
                    nc.gpsimd.tensor_copy(hm[j][:, t, :], K["hm"][tabs[t]][:, c]).then_inc(s_stage, 1)
                    nc.gpsimd.tensor_copy(lo[j][:, t, :], K["lo"][tabs[t]][:, c]).then_inc(s_stage, 1)
            loop(pool, turn)

        @block.tensor
        def _(pe):
            def turn(v, j):
                pe.wait_ge(s_stage, v * 4 + 4)
                freed(pe, s_gotA, v)
                freed(pe, s_gotB, v)
                for t in range(2):
                    for o in range(PER):
                        for c in range(cls):
                            at = out[c * w:(c + 1) * w, j, t, o * COLS:(o + 1) * COLS]
                            nc.tensor.matmul(at, hm[j][:, t, o * w:(o + 1) * w], hotT[:, c, :], start=True, stop=False)
                            last = nc.tensor.matmul(at, lo[j][:, t, o * w:(o + 1) * w], hotT[0:E64, c, :], start=False, stop=True)
                last.then_inc(s_pick, 1)
            loop(pe, turn)

        def put(t, v):
            return dst[t][:].rearrange("p c o -> p o c")[:, bass.ds(v * PER, PER), :]

        @block.scalar
        def _(act):
            def turn(v, j):
                act.wait_ge(s_pick, v + 1)
                nc.scalar.copy(put(0, v), out[:, j, 0, :].rearrange("p (o c) -> p o c", o=PER)).then_inc(s_gotA, 1)
            loop(act, turn)

        @block.vector
        def _(dve):
            def turn(v, j):
                dve.wait_ge(s_pick, v + 1)
                nc.vector.tensor_copy(put(1, v), out[:, j, 1, :].rearrange("p (o c) -> p o c", o=PER)).then_inc(s_gotB, 1)
            loop(dve, turn)


def kron_up(nc, d, K, rows, GA, GB, prob, H):
    with Memory(nc, "up") as m:
        xm = m.sb("xm", [P, 2, P])
        xd = m.sb("xd", [P, 2, P])
        vd = m.sb("vd", [P, 2, 2, P])
        gb = m.sb("gb", [P, 2, 2, E64])
        bias = m.sb("bias", [P, E64])
        warm = m.sb("warm", [P, 1])
        px, pv = m.ps("px", [P, 2, BANK]), m.ps("pv", [P, 2, BANK])
        ph = m.ps("ph", [P, 2, 2, BANK])
        s_b, s_xm, s_px, s_xd, s_pv, s_vd, s_ph, s_h, s_gb = (
            m.sem(k) for k in ("b", "xm", "px", "xd", "pv", "vd", "ph", "h", "gb"))
        block = m.block()
        turns = Turns(2)

        @block.sync
        def _(sp):
            sp.dma_start(bias[:], d["k_bias_up"]).then_inc(s_b, 16)

        @block.gpsimd
        def _(pool):
            def step(s, j):
                if live(s):
                    freed(pool, s_px, s)
                    x4 = rows[:, bass.ds(s * 32, 32)].rearrange("p (n o t) -> p n o t", n=4, o=1).to_broadcast([P, 4, 4, 8])
                    nc.gpsimd.tensor_tensor(xm[:, j, :].rearrange("p (n q t) -> p n q t", n=4, q=4), x4,
                                            K["mq"].rearrange("p (n q t) -> p n q t", n=4, q=4), ALU.mult).then_inc(s_xm, 1)
            turns.run(pool, step)

        @block.tensor
        def _(pe):
            pe.wait_ge(s_b, 16)

            def step(s, j):
                if live(s):
                    pe.wait_ge(s_xm, s + 1)
                    freed(pe, s_xd, s)
                    nc.tensor.matmul(px[:, j, 0:32], xm[:, j, :], K["fold"], start=True, stop=True).then_inc(s_px, 1)
                v, i = s - 1, (j + 1) % 2
                if live(v):
                    pe.wait_ge(s_xd, v + 1)
                    freed(pe, s_vd, v)
                    nc.tensor.matmul(pv[:, i, 0:P], xd[:, i, :], GA[:, bass.ds(v * 2, 2), :],
                                     start=True, stop=True).then_inc(s_pv, 1)
                v = s - 2
                if live(v):
                    pe.wait_ge(s_vd, v + 1)
                    pe.wait_ge(s_gb, v + 1)
                    freed(pe, s_h, v)
                    for q in range(2):
                        at = ph[:, j, q, 0:E64]
                        rows64 = slice(E64 * q, E64 * (q + 1))
                        nc.tensor.matmul(at, K["ident"][:], bias[:], start=True, stop=False)
                        for k in range(2):
                            last = nc.tensor.matmul(at, vd[rows64, j, k, :], gb[rows64, j, k, :],
                                                    start=False, stop=(k == 1))
                    last.then_inc(s_ph, 1)
            turns.run(pe, step)

        @block.vector
        def _(dve):
            def step(s, j):
                if live(s):
                    dve.wait_ge(s_px, s + 1)
                    freed(dve, s_pv, s)
                    nc.vector.tensor_tensor(xd[:, j, :].rearrange("p (n j) -> p n j", n=4),
                                            px[:, j, 0:32].rearrange("p (o j) -> p o j", o=1).to_broadcast([P, 4, 32]),
                                            K["mn"].rearrange("p (n j) -> p n j", n=4), ALU.mult).then_inc(s_xd, 1)
                v, i = s - 1, (j + 1) % 2
                if live(v):
                    dve.wait_ge(s_pv, v + 1)
                    freed(dve, s_ph, v)
                    nc.vector.tensor_tensor(
                        vd[:, i, :, :].rearrange("p k (m o) -> p k m o", m=2),
                        pv[:, i, 0:P].rearrange("p (k m o) -> p k m o", k=2, m=1).to_broadcast([P, 2, 2, E64]),
                        prob[:, bass.ds(v * 2, 2), :].rearrange("p k (m o) -> p k m o", o=1).to_broadcast([P, 2, 2, E64]),
                        ALU.mult).then_inc(s_vd, 1)
            turns.run(dve, step)

        @block.scalar
        def _(act):
            nc.scalar.activation(warm[:], K["ident"][:, 0:1], ACT.Gelu)

            def step(s, j):
                v, i = s - 1, (j + 1) % 2
                if live(v):
                    freed(act, s_ph, v)
                    nc.scalar.copy(gb[:, i, :, :], GB[:, bass.ds(v * 2, 2), :]).then_inc(s_gb, 1)
                v = s - 2
                if live(v):
                    act.wait_ge(s_ph, v + 1)
                    nc.scalar.activation(H[:, bass.ds(v, 1), :, :].rearrange("p b q o -> p (b q) o"),
                                         ph[:, j, :, 0:E64], ACT.Gelu).then_inc(s_h, 1)
            turns.run(act, step)


def kron_down(nc, d, K, x, GA, GB, prob, H, y):
    with Memory(nc, "down") as m:
        hd = m.sb("hd", [P, 2, 2, P])
        vd = m.sb("vd", [P, 2, 4, E64])
        gb = m.sb("gb", [P, 2, 4, 32])
        ym = m.sb("ym", [P, 2, P])
        bias = m.sb("bias", [P, 8])
        pv, py, pr = m.ps("pv", [P, 2, BANK]), m.ps("py", [P, 2, BANK]), m.ps("pr", [P, 2, BANK])
        s_b, s_hd, s_pv, s_vd, s_py, s_ym, s_pr, s_y, s_x, s_gb = (
            m.sem(k) for k in ("b", "hd", "pv", "vd", "py", "ym", "pr", "y", "x", "gb"))
        block = m.block()
        turns = Turns(2)

        @block.sync
        def _(sp):
            sp.dma_start(bias[:], d["k_bias_down"]).then_inc(s_b, 16)

        @block.gpsimd
        def _(pool):
            def step(s, j):
                if live(s):
                    freed(pool, s_pv, s)
                    for q in range(2):
                        nc.gpsimd.tensor_tensor(
                            hd[:, j, q, :].rearrange("p (m j) -> p m j", m=2),
                            H[:, bass.ds(s, 1), q, :].to_broadcast([P, 2, E64]),
                            K["mn2"].rearrange("p (m j) -> p m j", m=2), ALU.mult).then_inc(s_hd, 1)
            turns.run(pool, step)

        @block.tensor
        def _(pe):
            def step(s, j):
                if live(s):
                    pe.wait_ge(s_hd, 2 * s + 2)
                    freed(pe, s_vd, s)
                    for q in range(2):
                        last = nc.tensor.matmul(pv[:, j, q * E64:(q + 1) * E64], hd[:, j, q, :],
                                                GA[:, bass.ds(s * 4 + q * 2, 2), :], start=True, stop=True)
                    last.then_inc(s_pv, 1)
                v, i = s - 1, (j + 1) % 2
                if live(v):
                    pe.wait_ge(s_vd, v + 1)
                    pe.wait_ge(s_gb, v + 1)
                    freed(pe, s_ym, v)
                    for q in range(2):
                        for k in range(2):
                            last = nc.tensor.matmul(py[E64 * q:E64 * (q + 1), i, 0:32], vd[:, i, 2 * q + k, :],
                                                    gb[:, i, 2 * q + k, :], start=(k == 0), stop=(k == 1))
                    last.then_inc(s_py, 1)
                v = s - 2
                if live(v):
                    pe.wait_ge(s_ym, v + 1)
                    freed(pe, s_y, v)
                    nc.tensor.matmul(pr[:, j, 0:32], ym[:, j, :], K["gatherT"], start=True, stop=True).then_inc(s_pr, 1)
            turns.run(pe, step)

        @block.vector
        def _(dve):
            def step(s, j):
                if live(s):
                    dve.wait_ge(s_pv, s + 1)
                    freed(dve, s_py, s)
                    nc.vector.tensor_tensor(
                        vd[:, j, :, :].rearrange("p k (m o) -> p k m o", m=2),
                        pv[:, j, 0:P].rearrange("p (k m o) -> p k m o", k=4, m=1).to_broadcast([P, 4, 2, 32]),
                        prob[:, bass.ds(s * 4, 4), :].rearrange("p k (m o) -> p k m o", o=1).to_broadcast([P, 4, 2, 32]),
                        ALU.mult).then_inc(s_vd, 1)
                v, i = s - 1, (j + 1) % 2
                if live(v):
                    dve.wait_ge(s_py, v + 1)
                    freed(dve, s_pr, v)
                    nc.vector.tensor_tensor(ym[:, i, :].rearrange("p (c j) -> p c j", c=4),
                                            py[:, i, 0:32].rearrange("p (o j) -> p o j", o=1).to_broadcast([P, 4, 32]),
                                            K["mc"].rearrange("p (c j) -> p c j", c=4), ALU.mult).then_inc(s_ym, 1)
            turns.run(dve, step)
            dve.wait_ge(s_y, BLK)
            dve.wait_ge(s_b, 16)
            for tb in range(TB):
                v = y[:, tb * BANK:(tb + 1) * BANK].rearrange("p (n t) -> p t n", t=8)
                xs = x[:, tb * 8:(tb + 1) * 8, :]
                nc.vector.tensor_tensor(xs, xs, v, ALU.add).then_inc(s_x, 1)
            dve.wait_ge(s_x, TB)
            for tb in range(TB):
                xs = x[:, tb * 8:(tb + 1) * 8, :]
                nc.vector.tensor_tensor(xs, xs, bias[:].rearrange("p (t o) -> p t o", o=1).to_broadcast([P, 8, N]), ALU.add).then_inc(s_x, 1)

        @block.scalar
        def _(act):
            def step(s, j):
                if live(s):
                    freed(act, s_py, s)
                    nc.scalar.copy(gb[:, j, :, :], GB[:, bass.ds(s * 4, 4), :]).then_inc(s_gb, 1)
                v = s - 2
                if live(v):
                    act.wait_ge(s_pr, v + 1)
                    nc.scalar.copy(y[:, bass.ds(v * 32, 32)], pr[:, j, 0:32]).then_inc(s_y, 1)
            turns.run(act, step)


def kron_moe(nc, x, h, d, S, scratch):
    with Memory(nc, "kron") as m:
        cst = m.sb("cst", [P, 800])
        K = {"ident": S["ident"], "identb": m.sb("identb", [P, P], BF16)}
        at = 0
        for k, n in (("mq", P), ("mn", P), ("mn2", P), ("mc", P), ("iota", P), ("fold", 32), ("gatherT", 32),
                     ("half4", 2), ("half2", 2)):
            K[k] = cst[:, at:at + n]
            at += n
        K["hm"] = [m.sb(f"hm{i}", [P, 2048], BF16) for i in range(4)]
        K["lo"] = [m.sb(f"lo{i}", [E64, 2048], BF16) for i in range(4)]
        rows = m.sb("rows", [P, TOK])
        wup, wdown = m.sb("wup", [P, 8, E64]), m.sb("wdown", [P, E64, E64])
        split_tables(nc, d, K)
        with Memory(nc, "kstart") as q:
            s_c, s_r = q.sem("c"), q.sem("r")
            block = q.block()

            @block.sync
            def _(sp):
                sp.dma_start(cst[:, 0:at], d["k_cst"]).then_inc(s_c, 16)
                sp.dma_start(wup[:], d["k_wup"]).then_inc(s_c, 16)
                sp.dma_start(wdown[:], d["k_wdown"]).then_inc(s_c, 16)
                sp.wait_ge(s_c, 48)

            @block.vector
            def _(dve):
                nc.vector.tensor_copy(K["identb"][:], S["ident"][:]).then_inc(s_r, 1)
                for tb in range(TB):
                    nc.vector.tensor_copy(rows[:, tb * BANK:(tb + 1) * BANK].rearrange("p (n t) -> p n t", t=8),
                                          h[:, 1 + tb * 8:1 + (tb + 1) * 8, :].rearrange("p t n -> p n t")).then_inc(s_r, 1)
                dve.wait_ge(s_r, 1 + TB)

        H = m.sb("H", [P, BLK, 2, E64])
        hotT = m.sb("hotT4", [P, 4, 2 * BLK], BF16)
        hotT2 = m.sb("hotT2", [P, 2, 4 * BLK], BF16)
        prob = m.sb("prob4", [P, 2 * BLK, 2])
        prob2 = m.sb("prob2", [P, 4 * BLK, 2])
        GA, GB = m.sb("GA", [P, 2 * BLK, E64]), m.sb("GB", [P, 2 * BLK, E64])

        def mats_up(pe, r, emit):
            for t8 in range(8):
                last = emit(rows[:].rearrange("p (r t) -> p r t", t=8)[:, r * P:(r + 1) * P, t8],
                            wup[:, t8, :], start=(t8 == 0), stop=(t8 == 7))
            return last

        kron_route(nc, "ru", mats_up, d, K, hotT, prob, scratch[0], 4, "k_scale_up")
        kron_gather(nc, "gu", K, (0, 1), hotT, (GA, GB), 4)
        kron_up(nc, d, K, rows, GA, GB, prob, H)

        def mats_down(pe, r, emit):
            half = slice(E64 * r, E64 * (r + 1))
            for p in range(E64):
                last = emit(H[half, :, :, p].rearrange("p b q -> p (b q)"), wdown[half, p, :],
                            start=(p == 0), stop=(p == E64 - 1))
            return last

        kron_route(nc, "rd", mats_down, d, K, hotT2, prob2, scratch[1], 2, "k_scale_down")
        GAd = GA[:].rearrange("p c o -> p (c o)").rearrange("p (c o) -> p c o", o=32)
        GBd = GB[:].rearrange("p c o -> p (c o)").rearrange("p (c o) -> p c o", o=32)
        kron_gather(nc, "gd", K, (2, 3), hotT2, (GAd, GBd), 2)
        kron_down(nc, d, K, x, GAd, GBd, prob2, H, rows)


def gated_scan(nc, x, hid, d, S):
    C = TILE // T
    with Memory(nc, "scan") as m:
        w, b = m.sb("w", [P, 3, P]), m.sb("b", [P, 3])
        keep = m.sb("keep", [P, N, T])
        f, i_, cand, r = (m.sb(k, [P, N, T]) for k in ("f", "i", "cand", "r"))
        pre = m.ps("pre", [P, 3, 2, BANK])
        s_w, s_keep, s_pre, s_act, s_own, s_ratio, s_log, s_exp, s_diff, s_exp2 = (
            m.sem(k) for k in ("w", "keep", "pre", "act", "own", "ratio", "log", "exp", "diff", "exp2"))
        block = m.block()
        flat = lambda a: a[:].rearrange("p n t -> p (n t)")

        @block.sync
        def _(sp):
            sp.dma_start(w[:], d["l2_w"]).then_inc(s_w, 16)
            sp.dma_start(b[:], d["l2_b"]).then_inc(s_w, 16)

        @block.gpsimd
        def _(pool):
            pool.memset(keep[:], 1.0).then_inc(s_keep, 1)
            pool.wait_ge(s_keep, 1)
            pool.memset(keep[:, :, 0:1], 0.0).then_inc(s_keep, 1)

        @block.tensor
        def _(pe):
            pe.wait_ge(s_w, 32)
            for tile in range(NT):
                if tile >= 2:
                    pe.wait_ge(s_act, 3 * (tile - 1))
                for k in range(3):
                    nc.tensor.matmul(pre[:, k, tile % 2, :], w[:, k, :],
                                     x[:].rearrange("p t n -> p n t")[:, tile * C:(tile + 1) * C, :],
                                     start=True, stop=True).then_inc(s_pre, 1)

        @block.scalar
        def _(act):
            act.wait_ge(s_w, 32)
            for tile in range(NT):
                for k, (dst, fn) in enumerate(((f, ACT.Sigmoid), (i_, ACT.Sigmoid), (cand, ACT.Identity))):
                    act.wait_ge(s_pre, 3 * tile + k + 1)
                    nc.scalar.activation(flat(dst)[:, tile * TILE:(tile + 1) * TILE], pre[:, k, tile % 2, :], fn,
                                         bias=b[:, k:k + 1]).then_inc(s_act, 1)
            act.wait_ge(s_ratio, 1)
            nc.scalar.activation(flat(f), flat(f), ACT.Ln).then_inc(s_log, 1)
            act.wait_ge(s_diff, 1)
            nc.scalar.activation(flat(i_), flat(i_), ACT.Exp).then_inc(s_exp, 1)
            nc.scalar.activation(flat(f), flat(f), ACT.Exp).then_inc(s_exp, 1)

        @block.vector
        def _(dve):
            link = chain(dve, s_own)
            dve.wait_ge(s_act, 3 * NT)
            link(nc.vector.scalar_tensor_tensor(flat(r), flat(f), 1e-8, flat(i_), ALU.add, ALU.add))
            link(nc.vector.reciprocal(flat(r), flat(r)))
            link(nc.vector.tensor_tensor(flat(f), flat(f), flat(r), ALU.mult))
            nc.vector.tensor_scalar(flat(f), flat(f), 1e-8, None, ALU.add).then_inc(s_ratio, 1)
            link(nc.vector.tensor_tensor(flat(i_), flat(i_), flat(r), ALU.mult))
            link(nc.vector.tensor_tensor(flat(cand), flat(cand), flat(i_), ALU.mult))
            dve.wait_ge(s_log, 1)
            dve.wait_ge(s_keep, 2)
            link(nc.vector.tensor_tensor_scan(flat(r), flat(keep), flat(f), 0.0, ALU.mult, ALU.add))
            link(nc.vector.tensor_copy(i_[:, :, 0:1], r[:, :, T - 1:T]))
            link(nc.vector.tensor_tensor(i_[:, :, 1:T], r[:, :, T - 1:T].to_broadcast([P, N, T - 1]), r[:, :, 0:T - 1], ALU.subtract))
            nc.vector.tensor_copy(flat(f), flat(r)).then_inc(s_diff, 1)
            dve.wait_ge(s_exp, 2)
            link(nc.vector.tensor_tensor(flat(cand), flat(cand), flat(i_), ALU.mult))
            link(nc.vector.tensor_tensor_scan(flat(r), flat(keep), flat(cand), 0.0, ALU.mult, ALU.add))
            link(nc.vector.tensor_tensor(f[:], f[:], S["cond"][:].rearrange("p (n o) -> p n o", o=1).to_broadcast([P, N, T]), ALU.mult))
            link(nc.vector.tensor_tensor(flat(hid), flat(f), flat(r), ALU.add))


def gru(nc, x, h, d, S):
    with Memory(nc, "gru") as m:
        w, u, cv, b = (m.sb(k, [P, 3, P]) for k in ("w", "u", "cv", "b_"))
        b = m.sb("b", [P, 3])
        vid = m.sb("vid", [P, 3, N])
        zr, rh, hh, dd, zd = m.sb("zr", [P, 2, N]), m.sb("rh", [P, N]), m.sb("hh", [P, N]), m.sb("dd", [P, N]), m.sb("zd", [P, N])
        warm = m.sb("warm", [P, 3])
        pzr = m.ps("pzr", [P, 2, BANK])
        phh = m.ps("phh", [P, 2, BANK])
        s_w, s_v, s_vid, s_zr_pre, s_zr, s_rh, s_hh_pre, s_hh, s_own, s_h = (
            m.sem(k) for k in ("w", "v", "vid", "zr_pre", "zr", "rh", "hh_pre", "hh", "own", "h"))
        block = m.block()
        pair = lambda a: a.rearrange("p k n -> p (k n)")

        @block.sync
        def _(sp):
            for dst, src in ((w, "l3_w"), (u, "l3_u"), (cv, "l3_c"), (b, "l3_b")):
                sp.dma_start(dst[:], d[src]).then_inc(s_w, 16)

        @block.tensor
        def _(pe):
            pe.wait_ge(s_w, 64)
            for k in range(3):
                nc.tensor.matmul(pzr[:, 0, k * N:(k + 1) * N], cv[:, k, :], S["cond"][:], start=True, stop=True).then_inc(s_v, 1)
            pe.wait_ge(s_vid, 3)
            with pe.Fori(0, T // 2) as i:
                for j in range(2):
                    t = i * 2 + j
                    nc.tensor.matmul(pzr[:, j, 0:2 * N], S["ident"][:], pair(vid[:, 0:2, :]), start=True, stop=False)
                    for k in range(2):
                        nc.tensor.matmul(pzr[:, j, k * N:(k + 1) * N], w[:, k, :], x[:, t, :], start=False, stop=False)
                    nc.tensor.matmul(phh[:, j, 0:N], S["ident"][:], vid[:, 2, :], start=True, stop=False)
                    nc.tensor.matmul(phh[:, j, 0:N], w[:, 2, :], x[:, t, :], start=False, stop=False)
                    pe.wait_ge(s_h, t + 1)
                    for k in (1, 0):
                        last = nc.tensor.matmul(pzr[:, j, k * N:(k + 1) * N], u[:, k, :], h[:, t, :],
                                                start=False, stop=(k == 0))
                    last.then_inc(s_zr_pre, 1)
                    pe.wait_ge(s_rh, t + 1)
                    nc.tensor.matmul(phh[:, j, 0:N], u[:, 2, :], rh[:], start=False, stop=True).then_inc(s_hh_pre, 1)

        @block.scalar
        def _(act):
            act.wait_ge(s_w, 64)
            nc.scalar.activation(warm[:], b[:], ACT.Sigmoid)
            with act.Fori(0, T // 2) as i:
                for j in range(2):
                    t = i * 2 + j
                    act.wait_ge(s_zr_pre, t + 1)
                    nc.scalar.activation(pair(zr[:]), pzr[:, j, 0:2 * N], ACT.Sigmoid).then_inc(s_zr, 1)
                    act.wait_ge(s_hh_pre, t + 1)
                    nc.scalar.activation(hh[:], phh[:, j, 0:N], ACT.Tanh).then_inc(s_hh, 1)

        @block.vector
        def _(dve):
            nc.vector.memset(h[:, 0, :], 0.0).then_inc(s_h, 1)
            dve.wait_ge(s_w, 64)
            dve.wait_ge(s_v, 3)
            for k in range(3):
                nc.vector.tensor_scalar(vid[:, k, :], pzr[:, 0, k * N:(k + 1) * N], b[:, k:k + 1], None, ALU.add).then_inc(s_vid, 1)
            dve.wait_ge(s_h, 1)
            with dve.Fori(0, T // 2) as i:
                for j in range(2):
                    t = i * 2 + j
                    dve.wait_ge(s_zr, t + 1)
                    nc.vector.tensor_tensor(rh[:], zr[:, 1, :], h[:, t, :], ALU.mult).then_inc(s_rh, 1)
                    dve.wait_ge(s_hh, t + 1)
                    nc.vector.tensor_tensor(dd[:], hh[:], h[:, t, :], ALU.subtract).then_inc(s_own, 1)
                    dve.wait_ge(s_own, t * 2 + 1)
                    nc.vector.tensor_tensor(zd[:], zr[:, 0, :], dd[:], ALU.mult).then_inc(s_own, 1)
                    dve.wait_ge(s_own, t * 2 + 2)
                    nc.vector.tensor_tensor(h[:, t + 1, :], zd[:], h[:, t, :], ALU.add).then_inc(s_h, 1)


def router(nc, tag, tokens, d, S, gates_dram, mode, EG):
    E = 8
    with Memory(nc, tag) as m:
        w = m.sb("w", [P, E])
        code = m.sb("code", [P, E])
        bias = m.sb("bias", [P, E])
        v = {k: m.sb(k, [P, G, E]) for k in ("score", "value", "eq", "one", "two", "tmp")}
        red = {k: m.sb(k, [P, G]) for k in ("mx", "sum", "rec")}
        gates = m.sb("gates", [P, G, EG])
        logits = m.ps("logits", [P, G * E])
        gT = m.ps("gT", [EG, NT, BANK])
        s_w, s_logits, s_own, s_gates, s_gT, s_rows, s_out, s_code = (
            m.sem(k) for k in ("w", "logits", "own", "gates", "gT", "rows", "out", "code"))
        s_in, s_exp = (m.sem("in"), m.sem("exp")) if mode != "argmax" else (None, None)
        nd = 2 if mode == "sigmoid" else 1
        block = m.block()
        wide = lambda a: a[:].rearrange("p (g o) -> p g o", o=1).to_broadcast([P, G, E])
        per = lambda a: a[:].rearrange("p (o e) -> p o e", o=1).to_broadcast([P, G, E])

        @block.sync
        def _(sp):
            sp.dma_start(w[:], d[f"{tag}_w"]).then_inc(s_w, 16)
            if mode == "sigmoid":
                sp.dma_start(bias[:], d[f"{tag}_bias"]).then_inc(s_w, 16)
            sp.wait_ge(s_rows, NT)
            sp.dma_start(gates_dram, S["gates"][0:EG, :]).then_inc(s_out, 16)
            sp.wait_ge(s_out, 16)

        @block.gpsimd
        def _(pool):
            for e in range(E):
                pool.memset(code[:, e:e + 1], float(E - e)).then_inc(s_code, 1)

        @block.tensor
        def _(pe):
            pe.wait_ge(s_w, 16 * nd)
            for g in range(G):
                last = nc.tensor.matmul(logits[:, g * E:(g + 1) * E], tokens(g), w[:], start=True, stop=True)
            last.then_inc(s_logits, 1)
            pe.wait_ge(s_gates, 1)
            for g in range(G):
                nc.tensor.transpose(gT[:, g // 4, (g % 4) * P:(g % 4 + 1) * P], gates[:, g, :], S["ident"][:]).then_inc(s_gT, 1)

        @block.scalar
        def _(act):
            if mode == "softmax":
                act.wait_ge(s_in, 1)
                nc.scalar.activation(v["value"][:], v["value"][:], ACT.Exp).then_inc(s_exp, 1)
            if mode == "sigmoid":
                act.wait_ge(s_in, 1)
                nc.scalar.activation(v["value"][:], v["value"][:], ACT.Sigmoid).then_inc(s_exp, 1)
            for k in range(NT):
                act.wait_ge(s_gT, 4 * (k + 1))
                nc.scalar.activation(S["gates"][0:EG, k * TILE:(k + 1) * TILE], gT[:, k, :], ACT.Copy).then_inc(s_rows, 1)

        @block.vector
        def _(dve):
            link = chain(dve, s_own)
            tt = nc.vector.tensor_tensor
            lg = logits[:].rearrange("p (g e) -> p g e", e=E)
            value, score, eq, tmp = v["value"], v["score"], v["eq"], v["tmp"]

            def pick(one, src):
                link(nc.vector.tensor_reduce(red["mx"][:], src, AX, ALU.max))
                link(tt(eq[:], src, wide(red["mx"]), ALU.is_ge))
                link(tt(eq[:], eq[:], per(code), ALU.mult))
                link(nc.vector.tensor_reduce(red["mx"][:], eq[:], AX, ALU.max))
                link(tt(one[:], eq[:], wide(red["mx"]), ALU.is_equal))

            dve.wait_ge(s_code, E)
            dve.wait_ge(s_logits, 1)
            if mode == "softmax":
                link(nc.vector.tensor_reduce(red["mx"][:], lg, AX, ALU.max))
                tt(value[:], lg, wide(red["mx"]), ALU.subtract).then_inc(s_in, 1)
                dve.wait_ge(s_exp, 1)
                link(nc.vector.tensor_reduce(red["sum"][:], value[:], AX, ALU.add))
                link(nc.vector.reciprocal(red["rec"][:], red["sum"][:]))
                link(tt(value[:], value[:], wide(red["rec"]), ALU.mult))
                link(nc.vector.tensor_copy(score[:], value[:]))
            elif mode == "sigmoid":
                nc.vector.tensor_copy(value[:], lg).then_inc(s_in, 1)
                dve.wait_ge(s_exp, 1)
                link(tt(score[:], value[:], per(bias), ALU.add))
            else:
                link(nc.vector.tensor_copy(score[:], lg))
            pick(v["one"], score[:])
            out = gates[:, :, 0:E]
            if mode != "argmax":
                link(nc.vector.scalar_tensor_tensor(tmp[:], v["one"][:], -1e30, score[:], ALU.mult, ALU.add))
                pick(v["two"], tmp[:])
                link(tt(v["one"][:], v["one"][:], v["two"][:], ALU.add))
            if mode == "argmax":
                last = nc.vector.tensor_copy(out, v["one"][:])
            elif mode == "softmax":
                last = tt(out, v["one"][:], value[:], ALU.mult)
            else:
                link(tt(value[:], v["one"][:], value[:], ALU.mult))
                link(nc.vector.tensor_reduce(red["sum"][:], value[:], AX, ALU.add))
                link(nc.vector.tensor_scalar(red["mx"][:], red["sum"][:], 1e-9, None, ALU.is_gt))
                link(nc.vector.tensor_scalar(red["sum"][:], red["sum"][:], 1e-9, None, ALU.add))
                link(nc.vector.reciprocal(red["rec"][:], red["sum"][:]))
                link(tt(value[:], value[:], wide(red["rec"]), ALU.mult))
                link(nc.vector.tensor_scalar(v["two"][:], v["one"][:], 0.5, None, ALU.mult))
                link(tt(value[:], value[:], v["two"][:], ALU.subtract))
                link(tt(value[:], value[:], wide(red["mx"]), ALU.mult))
                last = tt(out, value[:], v["two"][:], ALU.add)
            if EG > E:
                link(last)
                last = nc.vector.memset(gates[:, :, E:EG], 1.0)
            last.then_inc(s_gates, 1)


def experts(nc, tag, tokens, resid, result, d, S, gates_dram, *, E, chunks, kind, act_fn, wcols, shared=None,
            out_view=lambda a: a):
    glu = kind == "glu"
    NCH = len(chunks)
    U = NT * NCH
    NB = 4
    with Memory(nc, tag) as m:
        w = [m.sb(f"w{i}", [P, wcols]) for i in range(2)]
        gate = [m.sb(f"gate{i}", [P, TOK]) for i in range(2)]
        xe = m.sb("xe", [P, 2, NT, TILE]) if glu else None
        a = m.sb("a", [P, NB, TILE])
        hb = m.sb("h", [P, NB, TILE])
        sw = m.sb("sw", [P, shared["cols"]]) if shared else None
        b2 = m.sb("b2", [E, P]) if result == "scaled" else None
        warm = m.sb("warm", [P, 1])
        acc = m.ps("acc", [P, NT, BANK])
        up = m.ps("up", [P, 4, BANK])
        s_up, s_act, s_hid, s_down, s_fin = (m.sem(k) for k in ("up", "act", "hid", "down", "fin"))
        s_b2 = m.sem("b2") if b2 is not None else None
        s_sw = m.sem("sw") if shared else None
        s_xe = m.sem("xe") if glu else None
        s_w = [m.sem(f"w{i}") for i in range(2)]
        s_gate = [m.sem(f"gate{i}") for i in range(2)]
        SH = shared["units"] if shared else 0
        PAIRS = (E - 1) // 2
        TAIL = E - 2 * PAIRS
        block = m.block()

        def expert_list(run):
            def body(eng):
                with eng.Fori(0, PAIRS) as i:
                    for j in range(2):
                        run(SH + (i * 2 + j) * U, i, j, False)
                for k in range(TAIL):
                    run(SH + (2 * PAIRS + k) * U, PAIRS, k, k == TAIL - 1)
            return body

        def sh_unit(u):
            return u // shared["nch"], u % shared["nch"]

        @block.sync
        def _(sp):
            if b2 is not None:
                sp.dma_start(b2[:], d[f"{tag}_b2"]).then_inc(s_b2, 16)
            if shared:
                sp.dma_start(sw[:], d[f"{tag}_sw"]).then_inc(s_sw, 16)

            def fetch(e, j):
                sp.dma_start(w[j][:], d[f"{tag}_wp"][e, :, :]).then_inc(s_w[j], 16)
                sp.dma_start(gate[j][:], gates_dram[e, :, :].to_broadcast([P, TOK])).then_inc(s_gate[j], 16)

            fetch(0, 0)
            fetch(1, 1)
            with sp.Fori(1, PAIRS) as i:
                for j in range(2):
                    sp.wait_ge(s_down, SH + ((i - 1) * 2 + j + 1) * U)
                    fetch(i * 2 + j, j)
            for k in range(TAIL):
                e = 2 * PAIRS + k
                sp.wait_ge(s_down, SH + (e - 1) * U)
                fetch(e, k)

        @block.tensor
        def _(pe):
            if b2 is not None:
                pe.wait_ge(s_b2, 16)
            for k in range(NT):
                if b2 is not None:
                    nc.tensor.matmul(acc[:, k, :], b2[:], S["gates"][0:E, k * TILE:(k + 1) * TILE], start=True, stop=False)
                else:
                    nc.tensor.matmul(acc[:, k, :], S["ident"][:], resid(k), start=True, stop=False)
            if shared:
                pe.wait_ge(s_sw, 16)
                H = shared["nch"] * P
                for u in range(SH + 2):
                    if u < SH:
                        tile, c = sh_unit(u)
                        if u >= 2:
                            pe.wait_ge(s_hid, u - 1)
                        nc.tensor.matmul(up[:, u % 2, :], sw[:, c * P:(c + 1) * P], tokens(tile), start=True, stop=True)
                        nc.tensor.matmul(up[:, 2 + u % 2, :], sw[:, H + c * P:H + (c + 1) * P], tokens(tile),
                                         start=True, stop=True).then_inc(s_up, 1)
                    if u >= 2:
                        tile, c = sh_unit(u - 2)
                        pe.wait_ge(s_hid, u - 1)
                        nc.tensor.matmul(acc[:, tile, :], sw[:, 2 * H + c * P:2 * H + (c + 1) * P], hb[:, (u - 2) % NB, :],
                                         start=False, stop=False).then_inc(s_down, 1)

            def run(base, i, j, is_last):
                pe.wait_ge(s_w[j], (i + 1) * 16)
                for u in range(U + 2):
                    if u < U:
                        tile, c = u // NCH, u % NCH
                        f0, fw = chunks[c]
                        if u >= 2:
                            pe.wait_ge(s_hid, base + u - 1)
                        if glu:
                            if c == 0:
                                pe.wait_ge(s_xe, (i * 2 + j) * NT + tile + 1)
                            rhs = xe[:, j, tile, :]
                            nc.tensor.matmul(up[0:fw, u % 2, :], w[j][:, f0:f0 + fw], rhs, start=True, stop=True)
                            F = sum(x[1] for x in chunks)
                            nc.tensor.matmul(up[0:fw, 2 + u % 2, :], w[j][:, F + f0:F + f0 + fw], rhs,
                                             start=True, stop=True).then_inc(s_up, 1)
                        else:
                            nc.tensor.matmul(up[0:fw, u % 2, :], w[j][:, f0:f0 + fw], tokens(tile),
                                             start=True, stop=True).then_inc(s_up, 1)
                    if u >= 2:
                        v = u - 2
                        tile, c = v // NCH, v % NCH
                        fw = chunks[c][1]
                        F = sum(x[1] for x in chunks) * (2 if glu else 1)
                        pe.wait_ge(s_hid, base + v + 1)
                        ins = nc.tensor.matmul(acc[:, tile, :], w[j][0:fw, F + c * P:F + (c + 1) * P], hb[0:fw, v % NB, :],
                                               start=False, stop=is_last and c == NCH - 1)
                        ins.then_inc(s_down, 1)
            expert_list(run)(pe)

        @block.scalar
        def _(act):
            if shared:
                for u in range(SH):
                    act.wait_ge(s_up, u + 1)
                    if u >= NB:
                        act.wait_ge(s_hid, u - NB + 1)
                    nc.scalar.activation(a[:, u % NB, :], up[:, u % 2, :], ACT.Silu).then_inc(s_act, 1)
            else:
                nc.scalar.activation(warm[:], S["ident"][:, 0:1], act_fn)

            def run(base, i, j, is_last):
                if not glu:
                    act.wait_ge(s_w[j], (i + 1) * 16)
                for u in range(U):
                    fw = chunks[u % NCH][1]
                    act.wait_ge(s_up, base + u + 1)
                    if u >= NB:
                        act.wait_ge(s_hid, base + u - NB + 1)
                    bias = 0.0
                    if kind == "gelu" and wcols > 2 * NCH * P:
                        bias = w[j][0:fw, 2 * NCH * P + u % NCH:2 * NCH * P + u % NCH + 1]
                    nc.scalar.activation(a[0:fw, u % NB, :], up[0:fw, u % 2, :], act_fn, bias=bias).then_inc(s_act, 1)
            if shared:
                nc.scalar.activation(warm[:], S["ident"][:, 0:1], act_fn)
            expert_list(run)(act)

        @block.vector
        def _(dve):
            if shared:
                for u in range(SH):
                    dve.wait_ge(s_act, u + 1)
                    if u >= NB:
                        dve.wait_ge(s_down, u - NB + 1)
                    nc.vector.tensor_tensor(hb[:, u % NB, :], up[:, 2 + u % 2, :], a[:, u % NB, :], ALU.mult).then_inc(s_hid, 1)

            def run(base, i, j, is_last):
                dve.wait_ge(s_gate[j], (i + 1) * 16)
                if glu:
                    for tile in range(NT):
                        nc.vector.tensor_tensor(xe[:, j, tile, :], tokens(tile), gate[j][:, tile * TILE:(tile + 1) * TILE],
                                                ALU.mult).then_inc(s_xe, 1)
                for u in range(U):
                    tile, c = u // NCH, u % NCH
                    fw = chunks[c][1]
                    dve.wait_ge(s_act, base + u + 1)
                    if u >= NB:
                        dve.wait_ge(s_down, base + u - NB + 1)
                    other = up[0:fw, 2 + u % 2, :] if glu else gate[j][0:fw, tile * TILE:(tile + 1) * TILE]
                    nc.vector.tensor_tensor(hb[0:fw, u % NB, :], a[0:fw, u % NB, :], other, ALU.mult).then_inc(s_hid, 1)
            expert_list(run)(dve)
            dve.wait_ge(s_down, SH + E * U)
            for k in range(NT):
                if result == "scaled":
                    nc.vector.scalar_tensor_tensor(resid(k), acc[:, k, :], L0_SCALE, resid(k), ALU.mult, ALU.add).then_inc(s_fin, 1)
                else:
                    nc.vector.tensor_copy(result(k), out_view(acc[:, k, :])).then_inc(s_fin, 1)


LAYERS = [0, 1, 2, 3]


def build(nc, d, out, scratch, probs_up, probs_down, layers):
    with ExitStack() as x_ctx, ExitStack() as Memory.semaphores:
        sb = lambda name, shape: x_ctx.enter_context(nc.sbuf_tensor(name, shape, F32))
        x = sb("x", [P, T, N])
        h = sb("h", [P, T + 1, N])
        S = {"cond": sb("cond", [P, N]), "ident": sb("ident", [P, P]), "gates": sb("gates", [9, TOK])}
        load_state(nc, x, d, S)
        xf = x[:].rearrange("p t n -> p (t n)")
        hf = h[:, 1:, :].rearrange("p t n -> p (t n)")
        x_tile = lambda k: xf[:, k * TILE:(k + 1) * TILE]
        h_tile = lambda k: hf[:, k * TILE:(k + 1) * TILE]
        h_group = lambda g: hf[:, g * P:(g + 1) * P]
        if 0 in layers:
            rnn(nc, x, h, d, S)
            router(nc, "r0", h_group, d, S, scratch[:, 0, :], "softmax", 9)
            experts(nc, "e0", h_tile, x_tile, "scaled", d, S, scratch, E=9,
                    chunks=[(c * P, P) for c in range(4)], kind="gelu", act_fn=ACT.Gelu_apprx_tanh, wcols=8 * P + 4)
        if 1 in layers:
            lstm(nc, x, h, d, S)
            kron_moe(nc, x, h, d, S, (probs_up, probs_down))
        if 2 in layers:
            hid = h[:, 1:, :].rearrange("p t n -> p (t n)").rearrange("p (n t) -> p n t", n=N)
            gated_scan(nc, x, hid, d, S)
            router(nc, "r2", h_group, d, S, scratch[0:8, 0, :], "argmax", 8)
            C = TILE // T
            xn = lambda k: x[:].rearrange("p t n -> p n t")[:, k * C:(k + 1) * C, :]
            experts(nc, "e2", h_tile, xn, xn, d, S, scratch, E=8,
                    chunks=[(0, 128), (128, 128), (256, 96)], kind="glu", act_fn=ACT.Silu, wcols=2 * 352 + 3 * P,
                    out_view=lambda a: a.rearrange("p (n t) -> p n t", t=T))
        if 3 in layers:
            gru(nc, x, h, d, S)
            router(nc, "r3", h_group, d, S, scratch[0:8, 0, :], "sigmoid", 8)
            experts(nc, "e3", h_tile, x_tile, x_tile, d, S, scratch, E=8, chunks=[(0, 128)], kind="gelu",
                    act_fn=ACT.Gelu, wcols=2 * P, shared={"cols": 3 * 2 * P, "nch": 2, "units": 2 * NT})
        store_state(nc, x, out)


def lay_out(i):
    t = lambda a, *axes: np.ascontiguousarray(np.transpose(a, axes))
    cat, pad = np.concatenate, np.pad
    col = lambda *bs: np.ascontiguousarray(np.stack(bs, 1))
    a = {"xT": t(i["x"], 2, 1, 0), "condT": t(i["cond_1024"], 1, 0)}
    a["l0_wx"], a["l0_wh"], a["l0_b"] = i["L0_cond_Wx"], i["L0_cond_Wh"], i["L0_cond_b"][:, None]
    a["r0_w"] = t(i["L0_ffn_w_router"], 1, 0)
    w1 = t(cat([i["L0_ffn_W1"], i["L0_ffn_Ws1"][None]]), 0, 2, 1)
    w2 = cat([i["L0_ffn_W2"], i["L0_ffn_Ws2"][None]]).reshape(9, P, 4, P).transpose(0, 3, 2, 1).reshape(9, P, 4 * P)
    b1 = cat([i["L0_ffn_b1"], i["L0_ffn_bs1"][None]]).reshape(9, 4, P).transpose(0, 2, 1)
    a["e0_wp"] = np.ascontiguousarray(cat([w1, w2, b1], 2))
    a["e0_b2"] = cat([i["L0_ffn_b2"], i["L0_ffn_bs2"][None]])
    a["l1_wx"] = i["L1_cond_Wx"].reshape(P, 4, P)
    a["l1_wh"] = i["L1_cond_Wh"].reshape(P, 4, P)
    a["l1_b"] = t(i["L1_cond_b"].reshape(4, P), 1, 0)
    a["l2_w"] = col(*(i[f"L2_cond_W_{k}"].T for k in "fih"))
    a["l2_b"] = col(*(i[f"L2_cond_b_{k}"] for k in "fih"))
    a["r2_w"] = t(i["L2_ffn_router_w"], 1, 0)
    dw = pad(t(i["L2_ffn_down_w"], 0, 2, 1), ((0, 0), (0, 32), (0, 0))).reshape(8, 3, P, P).transpose(0, 2, 1, 3)
    a["e2_wp"] = np.ascontiguousarray(cat([t(i["L2_ffn_gate_w"], 0, 2, 1), t(i["L2_ffn_up_w"], 0, 2, 1),
                                           dw.reshape(8, P, 3 * P)], 2))
    a["l3_w"] = col(i["L3_cond_W_z"], i["L3_cond_W_r"], i["L3_cond_W"])
    a["l3_u"] = col(i["L3_cond_U_z"], i["L3_cond_U_r"], i["L3_cond_U"])
    a["l3_c"] = col(i["L3_cond_C_z"], i["L3_cond_C_r"], i["L3_cond_C"])
    a["l3_b"] = col(i["L3_cond_b_z"], i["L3_cond_b_r"], i["L3_cond_b"])
    a["r3_w"] = t(i["L3_ffn_router_w"], 1, 0)
    a["r3_bias"] = np.ascontiguousarray(np.broadcast_to(i["L3_ffn_router_bias"], (P, 8)))
    a["e3_sw"] = cat([i["L3_ffn_sw1"], i["L3_ffn_sw3"],
                      i["L3_ffn_sw2"].reshape(2, P, P).transpose(1, 0, 2).reshape(P, 2 * P)], 1)
    a["e3_wp"] = cat([i["L3_ffn_ew1"], i["L3_ffn_ew2"]], 2)
    tab = (i["L1_ffn_A_up"].reshape(64, 64, 8, 4).transpose(0, 1, 3, 2), i["L1_ffn_B_up"],
           i["L1_ffn_A_down"], i["L1_ffn_B_down"])
    a["k_tab"] = np.stack([cat([v.reshape(64, 2048)] * 2) for v in tab])
    a["k_wup"] = i["L1_ffn_W_up"].reshape(64, 8, P).transpose(2, 1, 0)
    a["k_wdown"] = cat([i["L1_ffn_W_down"].reshape(64, 64, 64).transpose(1, 2, 0)] * 2)
    a["k_bias_up"] = cat([i["L1_ffn_bias_up"].reshape(64, 64)] * 2)
    a["k_bias_down"] = i["L1_ffn_bias_down"].reshape(8, P).T
    a["k_scale_up"] = np.broadcast_to(i["L1_ffn_scale_up"][None], (P, 1))
    a["k_scale_down"] = np.broadcast_to(i["L1_ffn_scale_down"][None], (P, 1))
    a["k_cst"] = patterns()
    return {k: np.ascontiguousarray(v) for k, v in a.items()}


def patterns():
    p, c = np.arange(P)[:, None], np.arange(P)[None, :]
    parts = [
        p // 32 == c // 8 % 4,
        p // 32 == c // 32,
        p // 64 == c // 64,
        p % 4 == c // 32,
        np.broadcast_to(c % 64, (P, P)),
        p % 32 == c[:, :32],
        p // 4 == c[:, :32],
        p // 32 % 2 == c[:, :2],
        p // 64 == c[:, :2],
    ]
    return np.concatenate([v.astype(np.float32) for v in parts], 1)


def kernel(**inputs):
    import concourse.bacc as bacc
    from concourse.bass_utils import run_bass_kernel_spmd as run

    arrays = lay_out({k: np.asarray(v) for k, v in inputs.items()})
    nc = bacc.Bacc("TRN2", target_bir_lowering=False, num_devices=1)
    d = {k: nc.dram_tensor("in_" + k, v.shape, mybir.dt.from_np(v.dtype), kind="ExternalInput").ap() for k, v in arrays.items()}
    out = nc.dram_tensor("out_x", (P, T, N), F32, kind="ExternalOutput").ap()
    scratch = nc.dram_tensor("gate_rows", (9, 1, TOK), F32, kind="Internal").ap()
    probs_up = nc.dram_tensor("probs_up", (4, 2 * BLK), F32, kind="Internal").ap()
    probs_down = nc.dram_tensor("probs_down", (2, 4 * BLK), F32, kind="Internal").ap()
    build(nc, d, out, scratch, probs_up, probs_down, LAYERS)
    r = run(nc, [{"in_" + k: v for k, v in arrays.items()}], core_ids=[0])
    return np.ascontiguousarray(np.transpose(r.results[0]["out_x"], (2, 1, 0)))
```

```python
from contextlib import ExitStack

import numpy as np
import concourse.bass as bass
from concourse import mybir

F32 = mybir.dt.float32
F32R = mybir.dt.float32r
BF16 = mybir.dt.bfloat16
U32 = mybir.dt.uint32
ACT = mybir.ActivationFunctionType
ALU = mybir.AluOpType
AX = mybir.AxisListType.X

P = 128
T = 32
N = 64
TOK = T * N
TILE = 512
NT = TOK // TILE
G = TOK // P
BANK = 512
L0_SCALE = 1.0 / float(np.sqrt(1 + 2 / 8))


def chain(eng, sem, start=0):
    count = [start]

    def link(ins):
        count[0] += 1
        ins.then_inc(sem, 1)
        eng.wait_ge(sem, count[0])
        return count[0]

    return link


class Memory:

    semaphores = None

    def __init__(self, nc, tag):
        self.nc, self.tag, self.ctx = nc, tag, ExitStack()

    def __enter__(self):
        self.ctx.__enter__()
        return self

    def __exit__(self, *a):
        return self.ctx.__exit__(*a)

    def sb(self, name, shape, dt=F32):
        return self.ctx.enter_context(self.nc.sbuf_tensor(f"{self.tag}_{name}", shape, dt))

    def ps(self, name, shape, dt=F32):
        return self.ctx.enter_context(self.nc.psum_tensor(f"{self.tag}_{name}", shape, dt))

    def sem(self, name):
        return Memory.semaphores.enter_context(self.nc.semaphore(f"{self.tag}_{name}"))

    def block(self):
        return self.ctx.enter_context(self.nc.Block())


def load_state(nc, x, d, S):
    with Memory(nc, "load") as m:
        s_in, s_zero, s_id = m.sem("in"), m.sem("zero"), m.sem("id")
        block = m.block()

        @block.sync
        def _(sp):
            sp.dma_start(x[:], d["xT"]).then_inc(s_in, 16)
            sp.dma_start(S["cond"][:], d["condT"]).then_inc(s_in, 16)
            sp.wait_ge(s_in, 32)

        @block.gpsimd
        def _(pool):
            pool.memset(S["ident"][:], 0.0).then_inc(s_zero, 1)
            pool.wait_ge(s_zero, 1)
            pool.affine_select(out=S["ident"][:], in_=S["ident"][:], compare_op=ALU.not_equal, fill=1.0,
                               base=0, pattern=[[-1, P]], channel_multiplier=1).then_inc(s_id, 1)
            pool.wait_ge(s_id, 1)
            pool.memset(S["zero"][:], 0.0).then_inc(s_zero, 1)
            for e in range(8):
                pool.memset(S["code"][:, e:e + 1], float(8 - e)).then_inc(s_zero, 1)


def store_state(nc, x, out):
    with Memory(nc, "store") as m:
        s_out = m.sem("out")
        block = m.block()

        @block.sync
        def _(sp):
            sp.dma_start(out, x[:]).then_inc(s_out, 16)
            sp.wait_ge(s_out, 16)


H2 = P // 2


def halves_product(nc, out, w, right, start, stop):
    for m in range(2):
        half = slice(m * H2, (m + 1) * H2)
        last = nc.tensor.matmul(out[half], w[:, half], right, start=start, stop=stop)
    return last


def over_steps(eng, step):
    with eng.Fori(0, T // 2 - 1) as i:
        for j in range(2):
            step(i * 2 + j, j, True)
    for j in range(2):
        step(T - 2 + j, j, False)


def rnn(nc, x, h, d, S):
    with Memory(nc, "rnn") as m:
        wx, wh, b, warm = m.sb("wx", [P, P]), m.sb("wh", [P, P]), m.sb("b", [P, 1]), m.sb("warm", [P, 1])
        state, xs = m.sb("state", [P, 2, N]), m.sb("xs", [P, 2, N])
        pre = m.ps("pre", [P, 2, BANK])
        s_w, s_x, s_pre, s_h, s_copied = (m.sem(k) for k in ("w", "x", "pre", "h", "copied"))
        block = m.block()

        @block.sync
        def _(sp):
            sp.dma_start(wx[:], d["l0_wx"]).then_inc(s_w, 16)
            sp.dma_start(wh[:], d["l0_wh"]).then_inc(s_w, 16)
            sp.dma_start(b[:], d["l0_b"]).then_inc(s_w, 16)

        @block.vector
        def _(dve):
            for t in range(2):
                nc.vector.tensor_copy(xs[:, t, :], x[:, t, :]).then_inc(s_x, 1)
            nc.vector.tensor_copy(state[:, 0, :], S["cond"][:]).then_inc(s_copied, 1)

            def step(t, j, more):
                dve.wait_ge(s_h, t + 1)
                if more:
                    nc.vector.tensor_copy(xs[:, j, :], x[:, t + 2, :]).then_inc(s_x, 1)
                nc.vector.tensor_copy(h[:, t + 1, :], state[:, 1 - j, :]).then_inc(s_copied, 1)
            over_steps(dve, step)

        @block.tensor
        def _(pe):
            def input_part(t, j):
                pe.wait_ge(s_x, t + 1)
                halves_product(nc, pre[:, j, 0:N], wx, xs[:, j, :], True, False)

            pe.wait_ge(s_w, 48)
            input_part(0, 0)
            pe.wait_ge(s_copied, 1)
            halves_product(nc, pre[:, 0, 0:N], wh, state[:, 0, :], False, True).then_inc(s_pre, 1)

            def step(t, j, more):
                if more or j == 0:
                    input_part(t + 1, 1 - j)
                    pe.wait_ge(s_h, t + 1)
                    halves_product(nc, pre[:, 1 - j, 0:N], wh, state[:, 1 - j, :], False, True).then_inc(s_pre, 1)
            over_steps(pe, step)

        @block.scalar
        def _(act):
            act.wait_ge(s_w, 48)
            nc.scalar.activation(warm[:], b[:], ACT.Tanh)

            def step(t, j, more):
                act.wait_ge(s_pre, t + 1)
                act.wait_ge(s_copied, t + 1)
                nc.scalar.activation(state[:, 1 - j, :], pre[:, j, 0:N], ACT.Tanh, bias=b[:]).then_inc(s_h, 1)
            over_steps(act, step)


def lstm(nc, x, h, d, S):
    I, FORGET, O, CAND = range(4)
    ORDER = (CAND, I, FORGET, O)
    with Memory(nc, "lstm") as m:
        wx, wh, b = m.sb("wx", [P, 4, P]), m.sb("wh", [P, 4, P]), m.sb("b", [P, 4])
        warm, gates = m.sb("warm", [P, 4]), m.sb("gates", [P, 4, N])
        c, fc, ig, tc = (m.sb(k, [P, N]) for k in ("c", "fc", "ig", "tc"))
        state, xs = m.sb("state", [P, 2, N]), m.sb("xs", [P, 2, N])
        pre = m.ps("pre", [P, 2, 4, BANK])
        s_w, s_x, s_pre, s_gates, s_own, s_c, s_tc, s_h = (
            m.sem(k) for k in ("w", "x", "pre", "gates", "own", "c", "tc", "h"))
        block = m.block()

        @block.sync
        def _(sp):
            sp.dma_start(wx[:], d["l1_wx"]).then_inc(s_w, 16)
            sp.dma_start(wh[:], d["l1_wh"]).then_inc(s_w, 16)
            sp.dma_start(b[:], d["l1_b"]).then_inc(s_w, 16)

        @block.tensor
        def _(pe):
            pe.wait_ge(s_w, 48)

            def input_part(t, j):
                pe.wait_ge(s_x, t + 1)
                for k in ORDER:
                    halves_product(nc, pre[:, j, k, 0:N], wx[:, k, :], xs[:, j, :], True, False)

            def state_part(j):
                for k in ORDER:
                    halves_product(nc, pre[:, j, k, 0:N], wh[:, k, :], state[:, j, :], False, True).then_inc(s_pre, 1)

            input_part(0, 0)
            pe.wait_ge(s_h, 1)
            state_part(0)

            def step(t, j, more):
                if more or j == 0:
                    input_part(t + 1, 1 - j)
                    pe.wait_ge(s_h, t + 2)
                    state_part(1 - j)
            over_steps(pe, step)

        @block.scalar
        def _(act):
            act.wait_ge(s_w, 48)
            nc.scalar.activation(warm[:], b[:], ACT.Sigmoid)

            def step(t, j, more):
                for n, k in enumerate(ORDER):
                    act.wait_ge(s_pre, t * 4 + n + 1)
                    nc.scalar.activation(gates[:, k, :], pre[:, j, k, 0:N], ACT.Tanh if k == CAND else ACT.Sigmoid,
                                         bias=b[:, k:k + 1]).then_inc(s_gates, 1)
                act.wait_ge(s_c, t + 2)
                nc.scalar.activation(tc[:], c[:], ACT.Tanh).then_inc(s_tc, 1)
            over_steps(act, step)

        @block.vector
        def _(dve):
            nc.vector.tensor_copy(state[:, 0, :], S["cond"][:]).then_inc(s_h, 1)
            for t in range(2):
                nc.vector.tensor_copy(xs[:, t, :], x[:, t, :]).then_inc(s_x, 1)
            nc.vector.memset(c[:], 0.0).then_inc(s_c, 1)
            dve.wait_ge(s_c, 1)

            def step(t, j, more):
                dve.wait_ge(s_gates, t * 4 + 2)
                nc.vector.tensor_tensor(ig[:], gates[:, I, :], gates[:, CAND, :], ALU.mult).then_inc(s_own, 1)
                dve.wait_ge(s_gates, t * 4 + 3)
                nc.vector.tensor_tensor(fc[:], gates[:, FORGET, :], c[:], ALU.mult).then_inc(s_own, 1)
                dve.wait_ge(s_own, t * 2 + 2)
                nc.vector.tensor_tensor(c[:], fc[:], ig[:], ALU.add).then_inc(s_c, 1)
                dve.wait_ge(s_gates, t * 4 + 4)
                if more:
                    nc.vector.tensor_copy(xs[:, j, :], x[:, t + 2, :]).then_inc(s_x, 1)
                dve.wait_ge(s_tc, t + 1)
                nc.vector.tensor_tensor(state[:, 1 - j, :], gates[:, O, :], tc[:], ALU.mult).then_inc(s_h, 1)
                dve.wait_ge(s_h, t + 2)
                nc.vector.tensor_copy(h[:, t + 1, :], state[:, 1 - j, :])
            over_steps(dve, step)


E64 = 64
TB = T // 8
BLK = TB * N // 4
BPT = 4


class Turns:

    COUNT = BLK // BPT

    def __init__(self, depth):
        self.depth = depth

    def run(self, eng, step):
        for s in range(4):
            step(s, s % 2)
        with eng.Fori(2, self.COUNT // 2) as i:
            for j in range(2):
                step(i * 2 + j, j)
        for s in range(self.COUNT, self.COUNT + self.depth):
            step(s, s % 2)


def live(v):
    return not isinstance(v, int) or 0 <= v < Turns.COUNT


def freed(eng, sem, v):
    if not isinstance(v, int) or v >= 2:
        eng.wait_ge(sem, v - 1)


def split_tables(nc, d, K, space):
    with Memory(nc, "split") as m:
        tab = [space[:, i * 2048:(i + 1) * 2048] for i in range(4)]
        mid = [m.sb(f"m{i}", [E64, 2048], BF16) for i in range(4)]
        s_in = [m.sem(f"in{i}") for i in range(2)]
        s_act, s_dve, s_pool = m.sem("act"), m.sem("dve"), m.sem("pool")
        block = m.block()

        @block.sync
        def _(sp):
            for i in range(4):
                sp.dma_start(tab[i], d["k_tab"][i]).then_inc(s_in[i // 2], 16)
            for i in range(2):
                sp.wait_ge(s_in[i], 32)

        @block.scalar
        def _(act):
            for i in range(4):
                act.wait_ge(s_in[i // 2], 32)
                nc.scalar.copy(K["hm"][i][:], tab[i]).then_inc(s_act, 1)
            for i in range(4):
                act.wait_ge(s_dve, i + 1)
                nc.scalar.copy(mid[i][:], tab[i][0:E64, :]).then_inc(s_act, 1)
                nc.scalar.copy(K["hm"][i][E64:P, :], tab[i][E64:P, :]).then_inc(s_act, 1)

        @block.vector
        def _(dve):
            for i in range(4):
                dve.wait_ge(s_act, i + 1)
                nc.vector.tensor_tensor(tab[i], tab[i], K["hm"][i][:], ALU.subtract).then_inc(s_dve, 1)
            for i in range(4):
                dve.wait_ge(s_act, 4 + 2 * i + 1)
                nc.vector.tensor_tensor(K["lo"][i][:], tab[i][0:E64, :], mid[i][:], ALU.subtract).then_inc(s_dve, 1)


def pick_two(nc, pick, link, logits, K, halves):
    top, idx, idxf, hot = pick
    for r in range(2):
        link(nc.vector.tensor_copy(halves[:, r, :], logits(r)))
        link(nc.vector.max(top[:, r, :], halves[:, r, :]))
        link(nc.vector.max_index(idx[:, r, :], top[:, r, :], halves[:, r, :]))
    link(nc.vector.tensor_copy(idxf[:], idx[:]))
    for r in range(2):
        for k in range(2):
            link(nc.vector.tensor_scalar(hot[:, r, k, :], K["iota"], idxf[:, r, k:k + 1], None, ALU.is_equal))


def kron_route(nc, tag, mats, d, K, hotT, prob, probs_dram, cls, scale_key, fetch=None):
    with Memory(nc, tag) as m:
        bankL = m.ps("logits", [P, 2, BANK])
        psT = m.ps("hotT", [P, 2, 2, 2 * BANK], BF16)
        halves = m.sb("halves", [P, 2, E64])
        pr = m.sb("pr", [P, 2, 2])
        diff = m.sb("diff", [P, 2, 2])
        NBK = 8 * BLK // cls
        pb = m.sb("pb", [P, NBK])
        top, idx, idxf = m.sb("top", [P, 2, 8]), m.sb("idx", [P, 2, 8], U32), m.sb("idxf", [P, 2, 8])
        hot = m.sb("hot", [P, 2, 2, P], BF16)
        sc = m.sb("sc", [P, 1])
        s_logits, s_own, s_hot, s_T, s_diff, s_pr, s_dram, s_pb, s_sc, s_hotT = (
            m.sem(k) for k in ("logits", "own", "hot", "T", "diff", "pr", "dram", "pb", "sc", "hotT"))
        s_fetch = m.sem("fetch") if fetch else None
        block = m.block()
        @block.sync
        def _(sp):
            sp.dma_start(sc[:], d[scale_key]).then_inc(s_sc, 16)
            if fetch:
                sp.dma_start(fetch[0][:], d[fetch[1]]).then_inc(s_fetch, 16)
            sp.wait_ge(s_pr, 1)
            for r in range(2):
                if cls == 4:
                    dst = probs_dram.rearrange("c (b k) -> b c k", k=2)[r * BLK // 2:(r + 1) * BLK // 2, :, :]
                else:
                    dst = probs_dram.rearrange("c (b k) -> c b k", k=2)[r, :, :]
                sp.dma_start(dst, pr[:, r, :]).then_inc(s_dram, 16)
            sp.wait_ge(s_dram, 32)
            w = P // cls
            for c in range(cls):
                sp.dma_start(pb[c * w:(c + 1) * w, :], probs_dram[c:c + 1, :].to_broadcast([w, NBK])).then_inc(s_pb, 16)

        @block.tensor
        def _(pe):
            if fetch:
                pe.wait_ge(s_fetch, 16)
            for r in range(2):
                def emit(left, right, **flags):
                    for n in range(2):
                        half = slice(E64 * n, E64 * (n + 1))
                        last = nc.tensor.matmul(bankL[half, r, 0:E64], left[:, half], right, **flags)
                    return last
                mats(pe, r, emit).then_inc(s_logits, 1)
            pe.wait_ge(s_hot, 1)
            for r in range(2):
                for k in range(2):
                    nc.tensor.transpose(psT[:, r, k, 0:P], hot[:, r, k, :], K["identb"][:]).then_inc(s_T, 1)

        @block.vector
        def _(dve):
            link = chain(dve, s_own)
            dve.wait_ge(s_logits, 2)
            pick_two(nc, (top, idx, idxf, hot), link, lambda r: bankL[:, r, 0:E64], K, halves)
            nc.vector.tensor_tensor(diff[:, :, 0:1], top[:, :, 0:1], top[:, :, 1:2], ALU.subtract).then_inc(s_hot, 1)
            nc.vector.tensor_tensor(diff[:, :, 1:2], top[:, :, 1:2], top[:, :, 0:1], ALU.subtract).then_inc(s_diff, 1)
            dve.wait_ge(s_T, 4)
            for r in range(2):
                for k in range(2):
                    src = psT[:, r, k, 0:P]
                    if cls == 4:
                        dst = hotT[:].rearrange("p c (b k) -> p k b c", k=2)[:, k, r * BLK // 2:(r + 1) * BLK // 2, :]
                        src = src.rearrange("p (b c) -> p b c", c=4)
                    else:
                        dst = hotT[:].rearrange("p c (b k) -> p c k b", k=2)[:, r, k, :]
                    nc.vector.tensor_copy(dst, src).then_inc(s_hotT, 1)
            dve.wait_ge(s_pb, 16 * cls)
            dve.wait_ge(s_sc, 16)
            link(nc.vector.tensor_scalar(pb[:], pb[:], sc[:], None, ALU.mult))
            for q in range(2):
                link(nc.vector.tensor_scalar(prob[:, :, q], pb[:], K["half4" if cls == 4 else "half2"][:, q:q + 1], None, ALU.mult))

        @block.scalar
        def _(act):
            act.wait_ge(s_diff, 1)
            act.wait_ge(s_hot, 1)
            nc.scalar.activation(pr[:], diff[:], ACT.Sigmoid).then_inc(s_pr, 1)


def kron_gather(nc, tag, K, tabs, hotT, dst, cls):
    w = P // cls
    PER = P // w
    COLS = BANK // PER
    TURNS = 2048 // P
    with Memory(nc, tag) as m:
        hm = [m.sb(f"hm{j}", [P, 2, P], BF16) for j in range(2)]
        lo = [m.sb(f"lo{j}", [E64, 2, P], BF16) for j in range(2)]
        out = m.ps("out", [P, 2, 2, BANK])
        s_stage, s_pick, s_gotA, s_gotB = (m.sem(k) for k in ("stage", "pick", "gotA", "gotB"))
        block = m.block()

        def loop(eng, turn):
            for v in range(2):
                turn(v, v)
            with eng.Fori(1, TURNS // 2) as i:
                for j in range(2):
                    turn(i * 2 + j, j)

        @block.gpsimd
        def _(pool):
            def turn(v, j):
                freed(pool, s_pick, v)
                for t in range(2):
                    c = bass.ds(v * P, P)
                    nc.gpsimd.tensor_copy(hm[j][:, t, :], K["hm"][tabs[t]][:, c]).then_inc(s_stage, 1)
                    nc.gpsimd.tensor_copy(lo[j][:, t, :], K["lo"][tabs[t]][:, c]).then_inc(s_stage, 1)
            loop(pool, turn)

        @block.tensor
        def _(pe):
            def turn(v, j):
                pe.wait_ge(s_stage, v * 4 + 4)
                freed(pe, s_gotA, v)
                freed(pe, s_gotB, v)
                for t in range(2):
                    for o in range(PER):
                        for c in range(cls):
                            at = out[c * w:(c + 1) * w, j, t, o * COLS:(o + 1) * COLS]
                            nc.tensor.matmul(at, hm[j][:, t, o * w:(o + 1) * w], hotT[:, c, :], start=True, stop=False)
                            last = nc.tensor.matmul(at, lo[j][:, t, o * w:(o + 1) * w], hotT[0:E64, c, :], start=False, stop=True)
                last.then_inc(s_pick, 1)
            loop(pe, turn)

        def put(t, v):
            return dst[t][:].rearrange("p c o -> p o c")[:, bass.ds(v * PER, PER), :]

        @block.scalar
        def _(act):
            def turn(v, j):
                act.wait_ge(s_pick, v + 1)
                nc.scalar.copy(put(0, v), out[:, j, 0, :].rearrange("p (o c) -> p o c", o=PER)).then_inc(s_gotA, 1)
            loop(act, turn)

        @block.vector
        def _(dve):
            def turn(v, j):
                dve.wait_ge(s_pick, v + 1)
                nc.vector.tensor_copy(put(1, v), out[:, j, 1, :].rearrange("p (o c) -> p o c", o=PER)).then_inc(s_gotB, 1)
            loop(dve, turn)


def kron_up(nc, d, K, rows, GA, GB, prob, H):
    with Memory(nc, "up") as m:
        xm = m.sb("xm", [P, 2, BPT, P])
        xd = m.sb("xd", [P, 2, BPT, P])
        vd = m.sb("vd", [P, 2, BPT, 2, P])
        ga = m.sb("ga", [P, 2, BPT, P])
        gb = m.sb("gb", [P, 2, BPT, P])
        bias = m.sb("bias", [P, BPT * P])
        warm = m.sb("warm", [P, 1])
        px, pv = m.ps("px", [P, 2, BANK]), m.ps("pv", [P, 2, BANK])
        ph = m.ps("ph", [P, 2, BANK])
        s_b, s_xm, s_px, s_xd, s_pv, s_vd, s_ph, s_h, s_ga, s_gb = (
            m.sem(k) for k in ("b", "xm", "px", "xd", "pv", "vd", "ph", "h", "ga", "gb"))
        block = m.block()
        turns = Turns(2)
        W = 2 * BPT

        @block.sync
        def _(sp):
            sp.dma_start(bias[:], d["k_bias_up"]).then_inc(s_b, 16)

        @block.gpsimd
        def _(pool):
            def step(s, j):
                if live(s):
                    freed(pool, s_px, s)
                    nc.gpsimd.tensor_tensor(
                        xm[:, j, :, :].rearrange("p b (n q t) -> p (b n) q t", n=4, q=4),
                        rows[:, bass.ds(s * 32 * BPT, 32 * BPT)].rearrange("p (r o t) -> p r o t", o=1, t=8)
                        .to_broadcast([P, 4 * BPT, 4, 8]),
                        K["mq"][:, 0:32].rearrange("p (o q t) -> p o q t", o=1, q=4).to_broadcast([P, 4 * BPT, 4, 8]),
                        ALU.mult).then_inc(s_xm, 1)
            turns.run(pool, step)

        @block.tensor
        def _(pe):
            pe.wait_ge(s_b, 16)

            def step(s, j):
                if live(s):
                    pe.wait_ge(s_xm, s + 1)
                    freed(pe, s_xd, s)
                    for b in range(BPT):
                        for q in range(2):
                            half = slice(E64 * q, E64 * (q + 1))
                            last = nc.tensor.matmul(px[half, j, b * 32:(b + 1) * 32], xm[:, j, b, half], K["fold"], start=True, stop=True)
                    last.then_inc(s_px, 1)
                v, i = s - 1, (j + 1) % 2
                if live(v):
                    pe.wait_ge(s_xd, v + 1)
                    pe.wait_ge(s_ga, v + 1)
                    freed(pe, s_vd, v)
                    for b in range(BPT):
                        last = nc.tensor.matmul(pv[:, i, b * P:(b + 1) * P], xd[:, i, b, :], ga[:, i, b, :],
                                                start=True, stop=True)
                    last.then_inc(s_pv, 1)
                v = s - 2
                if live(v):
                    pe.wait_ge(s_vd, v + 1)
                    pe.wait_ge(s_gb, v + 1)
                    freed(pe, s_h, v)
                    nc.tensor.matmul(ph[:, j, :], K["ident"][:], bias[:], start=True, stop=False)
                    for b in range(BPT):
                        for q in range(2):
                            half = slice(E64 * q, E64 * (q + 1))
                            for k in range(2):
                                last = nc.tensor.matmul(ph[half, j, b * P:(b + 1) * P], gb[half, j, b, k * E64:(k + 1) * E64],
                                                        vd[half, j, b, k, :], start=False, stop=(b, k) == (BPT - 1, 1))
                    last.then_inc(s_ph, 1)
            turns.run(pe, step)

        @block.vector
        def _(dve):
            def step(s, j):
                if live(s):
                    dve.wait_ge(s_px, s + 1)
                    freed(dve, s_pv, s)
                    nc.vector.tensor_tensor(
                        xd[:, j, :, :].rearrange("p b (n j) -> p b n j", n=4),
                        px[:, j, 0:32 * BPT].rearrange("p (b o j) -> p b o j", b=BPT, o=1).to_broadcast([P, BPT, 4, 32]),
                        K["mn"].rearrange("p (o n j) -> p o n j", o=1, n=4).to_broadcast([P, BPT, 4, 32]),
                        ALU.mult).then_inc(s_xd, 1)
                v, i = s - 1, (j + 1) % 2
                if live(v):
                    dve.wait_ge(s_pv, v + 1)
                    freed(dve, s_ph, v)
                    nc.vector.tensor_tensor(
                        vd[:, i, :, :, :].rearrange("p b k (m o) -> p (b k) m o", m=2),
                        pv[:, i, :].rearrange("p (w m o) -> p w m o", w=W, m=1).to_broadcast([P, W, 2, E64]),
                        prob[:, bass.ds(v * W, W), :].rearrange("p k (m o) -> p k m o", o=1).to_broadcast([P, W, 2, E64]),
                        ALU.mult).then_inc(s_vd, 1)
            turns.run(dve, step)

        @block.scalar
        def _(act):
            nc.scalar.activation(warm[:], K["ident"][:, 0:1], ACT.Gelu)

            def step(s, j):
                if live(s):
                    freed(act, s_pv, s)
                    nc.scalar.copy(ga[:, j, :, :].rearrange("p b c -> p (b c)"),
                                   GA[:, bass.ds(s * W, W), :].rearrange("p c o -> p (c o)")).then_inc(s_ga, 1)
                v, i = s - 1, (j + 1) % 2
                if live(v):
                    freed(act, s_ph, v)
                    nc.scalar.copy(gb[:, i, :, :].rearrange("p b c -> p (b c)"),
                                   GB[:, bass.ds(v * W, W), :].rearrange("p c o -> p (c o)")).then_inc(s_gb, 1)
                v = s - 2
                if live(v):
                    act.wait_ge(s_ph, v + 1)
                    nc.scalar.activation(H[:, bass.ds(v * BPT, BPT), :, :].rearrange("p b n o -> p (b n o)"), ph[:, j, :],
                                         ACT.Gelu).then_inc(s_h, 1)
            turns.run(act, step)


def kron_down(nc, d, K, x, GA, GB, prob, H, y):
    with Memory(nc, "down") as m:
        hd = m.sb("hd", [P, 2, 2 * BPT, P])
        vd = m.sb("vd", [P, 2, 4 * BPT, E64])
        ym = m.sb("ym", [P, 2, BPT, 4, 32])
        ga = m.sb("ga", [P, 2, 2 * BPT, E64])
        gb = m.sb("gb", [P, 2, 4 * BPT, 32])
        bias = m.sb("bias", [P, 8])
        pv, py, pr = m.ps("pv", [P, 2, BANK]), m.ps("py", [P, 2, BANK]), m.ps("pr", [P, 2, BANK])
        s_b, s_hd, s_pv, s_vd, s_py, s_ym, s_pr, s_y, s_x, s_ga, s_gb = (
            m.sem(k) for k in ("b", "hd", "pv", "vd", "py", "ym", "pr", "y", "x", "ga", "gb"))
        block = m.block()
        turns = Turns(3)
        W = 4 * BPT

        @block.sync
        def _(sp):
            sp.dma_start(bias[:], d["k_bias_down"]).then_inc(s_b, 16)

        @block.gpsimd
        def _(pool):
            def step(s, j):
                if live(s):
                    freed(pool, s_pv, s)
                    nc.gpsimd.tensor_tensor(
                        hd[:, j, :, :].rearrange("p w (m j) -> p w m j", m=2),
                        H[:, bass.ds(s * BPT, BPT), :, :].rearrange("p b q (m j) -> p (b q) m j", m=1)
                        .to_broadcast([P, 2 * BPT, 2, E64]),
                        K["mn2"].rearrange("p (o m j) -> p o m j", o=1, m=2).to_broadcast([P, 2 * BPT, 2, E64]),
                        ALU.mult).then_inc(s_hd, 1)
            turns.run(pool, step)

        @block.tensor
        def _(pe):
            def step(s, j):
                if live(s):
                    pe.wait_ge(s_hd, s + 1)
                    pe.wait_ge(s_ga, s + 1)
                    freed(pe, s_vd, s)
                    for w in range(2 * BPT):
                        for n in range(2):
                            half = slice(E64 * n, E64 * (n + 1))
                            last = nc.tensor.matmul(pv[half, j, w * E64:(w + 1) * E64], hd[:, j, w, half], ga[:, j, w, :],
                                                    start=True, stop=True)
                    last.then_inc(s_pv, 1)
                v, i = s - 1, (j + 1) % 2
                if live(v):
                    pe.wait_ge(s_vd, v + 1)
                    pe.wait_ge(s_gb, v + 1)
                    freed(pe, s_ym, v)
                    for b in range(BPT):
                        for q in range(2):
                            for k in range(2):
                                w = 4 * b + 2 * q + k
                                last = nc.tensor.matmul(py[E64 * q:E64 * (q + 1), i, b * 32:(b + 1) * 32], vd[:, i, w, :],
                                                        gb[:, i, w, :], start=(k == 0), stop=(k == 1))
                    last.then_inc(s_py, 1)
                v = s - 2
                if live(v):
                    pe.wait_ge(s_ym, v + 1)
                    freed(pe, s_y, v)
                    for c in range(4):
                        last = nc.tensor.matmul(pr[c * 32:(c + 1) * 32, j, 0:32 * BPT], K["fold"],
                                                ym[:, j, :, :, :].rearrange("p b n (t c) -> p (b n t) c", c=4)[:, :, c],
                                                start=True, stop=True)
                    last.then_inc(s_pr, 1)
            turns.run(pe, step)

        @block.vector
        def _(dve):
            def step(s, j):
                if live(s):
                    dve.wait_ge(s_pv, s + 1)
                    freed(dve, s_py, s)
                    nc.vector.tensor_tensor(
                        vd[:, j, :, :].rearrange("p k (m o) -> p k m o", m=2),
                        pv[:, j, :].rearrange("p (w m o) -> p w m o", w=W, m=1).to_broadcast([P, W, 2, 32]),
                        prob[:, bass.ds(s * W, W), :].rearrange("p k (m o) -> p k m o", o=1).to_broadcast([P, W, 2, 32]),
                        ALU.mult).then_inc(s_vd, 1)
                v, i = s - 1, (j + 1) % 2
                if live(v):
                    dve.wait_ge(s_py, v + 1)
                    freed(dve, s_pr, v)
                    nc.vector.tensor_tensor(
                        ym[:, i, :, :, :],
                        py[:, i, 0:32 * BPT].rearrange("p (b o j) -> p b o j", b=BPT, o=1).to_broadcast([P, BPT, 4, 32]),
                        K["mns"].rearrange("p (o c j) -> p o c j", o=1, c=4).to_broadcast([P, BPT, 4, 32]),
                        ALU.mult).then_inc(s_ym, 1)
            turns.run(dve, step)
            dve.wait_ge(s_y, Turns.COUNT)
            dve.wait_ge(s_b, 16)
            for tb in range(TB):
                v = y[:, tb * BANK:(tb + 1) * BANK].rearrange("p (n t) -> p t n", t=8)
                xs = x[:, tb * 8:(tb + 1) * 8, :]
                nc.vector.tensor_tensor(xs, xs, v, ALU.add).then_inc(s_x, 1)
            dve.wait_ge(s_x, TB)
            for tb in range(TB):
                xs = x[:, tb * 8:(tb + 1) * 8, :]
                nc.vector.tensor_tensor(xs, xs, bias[:].rearrange("p (t o) -> p t o", o=1).to_broadcast([P, 8, N]), ALU.add).then_inc(s_x, 1)

        @block.scalar
        def _(act):
            def step(s, j):
                if live(s):
                    freed(act, s_pv, s)
                    nc.scalar.copy(ga[:, j, :, :].rearrange("p w o -> p (w o)"),
                                   GA[:, bass.ds(s * W, W), :].rearrange("p c o -> p (c o)")).then_inc(s_ga, 1)
                    freed(act, s_py, s)
                    nc.scalar.copy(gb[:, j, :, :].rearrange("p w o -> p (w o)"),
                                   GB[:, bass.ds(s * W, W), :].rearrange("p c o -> p (c o)")).then_inc(s_gb, 1)
                v, i = s - 3, (j + 1) % 2
                if live(v):
                    act.wait_ge(s_pr, v + 1)
                    nc.scalar.copy(y[:, bass.ds(v * 32 * BPT, 32 * BPT)], pr[:, i, 0:32 * BPT]).then_inc(s_y, 1)
            turns.run(act, step)


def kron_moe(nc, x, h, d, S, scratch):
    with Memory(nc, "kron") as m:
        cst = m.sb("cst", [P, 800])
        K = {"ident": S["ident"], "identb": m.sb("identb", [P, P], BF16)}
        at = 0
        for k, n in (("mq", P), ("mn", P), ("mn2", P), ("mns", P), ("iota", P), ("fold", 32),
                     ("half4", 2), ("half2", 2)):
            K[k] = cst[:, at:at + n]
            at += n
        rows = m.sb("rows", [P, TOK])
        H = m.sb("H", [P, BLK, 2, E64])
        GA, GB = m.sb("GA", [P, 2 * BLK, E64]), m.sb("GB", [P, 2 * BLK, E64])
        hotT = m.sb("hotT4", [P, 4, 2 * BLK], BF16)
        hotT2 = m.sb("hotT2", [P, 2, 4 * BLK], BF16)
        prob = m.sb("prob4", [P, 2 * BLK, 2])
        prob2 = m.sb("prob2", [P, 4 * BLK, 2])
        down = [(m.sb(f"hm{i}", [P, 2048], BF16), m.sb(f"lo{i}", [E64, 2048], BF16)) for i in (2, 3)]

        with Memory(nc, "kup") as q:
            up = [(q.sb(f"hm{i}", [P, 2048], BF16), q.sb(f"lo{i}", [E64, 2048], BF16)) for i in (0, 1)]
            K["hm"], K["lo"] = zip(*(up + down))
            wup = q.sb("wup", [P, 8, E64])
            split_tables(nc, d, K, H[:].rearrange("p b q o -> p (b q o)"))
            kron_start(nc, d, K, S, h, rows, cst, at, wup)

            def mats_up(pe, r, emit):
                for t8 in range(8):
                    last = emit(rows[:].rearrange("p (r t) -> p r t", t=8)[:, r * P:(r + 1) * P, t8],
                                wup[:, t8, :], start=(t8 == 0), stop=(t8 == 7))
                return last

            kron_route(nc, "ru", mats_up, d, K, hotT, prob, scratch[0], 4, "k_scale_up")
            kron_gather(nc, "gu", K, (0, 1), hotT, (GA, GB), 4)
        kron_up(nc, d, K, rows, GA, GB, prob, H)
        with Memory(nc, "kdn") as q:
            wdown = q.sb("wdown", [P, E64, E64])

            def mats_down(pe, r, emit):
                half = slice(E64 * r, E64 * (r + 1))
                for o in range(E64):
                    last = emit(H[half, :, :, o].rearrange("p b n -> p (b n)"), wdown[half, o, :],
                                start=(o == 0), stop=(o == E64 - 1))
                return last

            kron_route(nc, "rd", mats_down, d, K, hotT2, prob2, scratch[1], 2, "k_scale_down", (wdown, "k_wdown"))
        GAd = GA[:].rearrange("p c o -> p (c o)").rearrange("p (c o) -> p c o", o=32)
        GBd = GB[:].rearrange("p c o -> p (c o)").rearrange("p (c o) -> p c o", o=32)
        kron_gather(nc, "gd", K, (3, 2), hotT2, (GAd, GBd), 2)
        kron_down(nc, d, K, x, GAd, GBd, prob2, H, rows)


def kron_start(nc, d, K, S, h, rows, cst, width, wup):
    with Memory(nc, "kstart") as q:
        s_c = q.sem("c")
        block = q.block()

        @block.sync
        def _(sp):
            sp.dma_start(cst[:, 0:width], d["k_cst"]).then_inc(s_c, 16)
            sp.dma_start(wup[:], d["k_wup"]).then_inc(s_c, 16)
            sp.wait_ge(s_c, 32)

        @block.vector
        def _(dve):
            nc.vector.tensor_copy(K["identb"][:], S["ident"][:])
            for tb in range(TB):
                nc.vector.tensor_copy(rows[:, tb * BANK:(tb + 1) * BANK].rearrange("p (n t) -> p t n", t=8),
                                      h[:, 1 + tb * 8:1 + (tb + 1) * 8, :])


def gated_scan(nc, x, hid, d, S):
    C = TILE // T
    with Memory(nc, "scan") as m:
        w, b = m.sb("w", [P, 3, P]), m.sb("b", [P, 3])
        keep = m.sb("keep", [P, N, T])
        f, i_, cand, r = (m.sb(k, [P, N, T]) for k in ("f", "i", "cand", "r"))
        pre = m.ps("pre", [P, 3, 2, BANK])
        s_w, s_keep, s_pre, s_act, s_own, s_ratio, s_log, s_exp, s_diff, s_exp2 = (
            m.sem(k) for k in ("w", "keep", "pre", "act", "own", "ratio", "log", "exp", "diff", "exp2"))
        block = m.block()
        flat = lambda a: a[:].rearrange("p n t -> p (n t)")

        @block.sync
        def _(sp):
            sp.dma_start(w[:], d["l2_w"]).then_inc(s_w, 16)
            sp.dma_start(b[:], d["l2_b"]).then_inc(s_w, 16)

        @block.gpsimd
        def _(pool):
            pool.memset(keep[:], 1.0).then_inc(s_keep, 1)
            pool.wait_ge(s_keep, 1)
            pool.memset(keep[:, :, 0:1], 0.0).then_inc(s_keep, 1)

        @block.tensor
        def _(pe):
            pe.wait_ge(s_w, 32)
            for tile in range(NT):
                if tile >= 2:
                    pe.wait_ge(s_act, 3 * (tile - 1))
                for k in range(3):
                    nc.tensor.matmul(pre[:, k, tile % 2, :], w[:, k, :],
                                     x[:].rearrange("p t n -> p n t")[:, tile * C:(tile + 1) * C, :],
                                     start=True, stop=True).then_inc(s_pre, 1)

        @block.scalar
        def _(act):
            act.wait_ge(s_w, 32)
            for tile in range(NT):
                for k, (dst, fn) in enumerate(((f, ACT.Sigmoid), (i_, ACT.Sigmoid), (cand, ACT.Identity))):
                    act.wait_ge(s_pre, 3 * tile + k + 1)
                    nc.scalar.activation(flat(dst)[:, tile * TILE:(tile + 1) * TILE], pre[:, k, tile % 2, :], fn,
                                         bias=b[:, k:k + 1]).then_inc(s_act, 1)
            act.wait_ge(s_ratio, 1)
            nc.scalar.activation(flat(f), flat(f), ACT.Ln).then_inc(s_log, 1)
            act.wait_ge(s_diff, 1)
            nc.scalar.activation(flat(i_), flat(i_), ACT.Exp).then_inc(s_exp, 1)
            nc.scalar.activation(flat(f), flat(f), ACT.Exp).then_inc(s_exp, 1)

        @block.vector
        def _(dve):
            link = chain(dve, s_own)
            dve.wait_ge(s_act, 3 * NT)
            link(nc.vector.scalar_tensor_tensor(flat(r), flat(f), 1e-8, flat(i_), ALU.add, ALU.add))
            link(nc.vector.reciprocal(flat(r), flat(r)))
            link(nc.vector.tensor_tensor(flat(f), flat(f), flat(r), ALU.mult))
            nc.vector.tensor_scalar(flat(f), flat(f), 1e-8, None, ALU.add).then_inc(s_ratio, 1)
            link(nc.vector.tensor_tensor(flat(i_), flat(i_), flat(r), ALU.mult))
            link(nc.vector.tensor_tensor(flat(cand), flat(cand), flat(i_), ALU.mult))
            dve.wait_ge(s_log, 1)
            dve.wait_ge(s_keep, 2)
            link(nc.vector.tensor_tensor_scan(flat(r), flat(keep), flat(f), 0.0, ALU.mult, ALU.add))
            link(nc.vector.tensor_copy(i_[:, :, 0:1], r[:, :, T - 1:T]))
            link(nc.vector.tensor_tensor(i_[:, :, 1:T], r[:, :, T - 1:T].to_broadcast([P, N, T - 1]), r[:, :, 0:T - 1], ALU.subtract))
            nc.vector.tensor_copy(flat(f), flat(r)).then_inc(s_diff, 1)
            dve.wait_ge(s_exp, 2)
            link(nc.vector.tensor_tensor(flat(cand), flat(cand), flat(i_), ALU.mult))
            link(nc.vector.tensor_tensor_scan(flat(r), flat(keep), flat(cand), 0.0, ALU.mult, ALU.add))
            link(nc.vector.tensor_tensor(f[:], f[:], S["cond"][:].rearrange("p (n o) -> p n o", o=1).to_broadcast([P, N, T]), ALU.mult))
            link(nc.vector.tensor_tensor(flat(hid), flat(f), flat(r), ALU.add))


def gru(nc, x, h, d, S):
    ZRC = ((1,), (0,), (2,))
    with Memory(nc, "gru") as m:
        w, u, cv, b = m.sb("w", [P, 3, P]), m.sb("u", [P, 3, P]), m.sb("cv", [P, 3, P]), m.sb("b", [P, 3])
        vid = m.sb("vid", [P, 3, N])
        z, keep, r, rh, hh, kept, new = (m.sb(k, [P, N]) for k in ("z", "keep", "r", "rh", "hh", "kept", "new"))
        warm, state, xs = m.sb("warm", [P, 3]), m.sb("state", [P, 2, N]), m.sb("xs", [P, 2, N])
        pre = m.ps("pre", [P, 2, 3, BANK])
        s_w, s_v, s_vid, s_x, s_pre, s_gate, s_rh, s_hh, s_own, s_h = (
            m.sem(k) for k in ("w", "v", "vid", "x", "pre", "gate", "rh", "hh", "own", "h"))
        block = m.block()

        @block.sync
        def _(sp):
            for dst, src in ((w, "l3_w"), (u, "l3_u"), (cv, "l3_c"), (b, "l3_b")):
                sp.dma_start(dst[:], d[src]).then_inc(s_w, 16)

        @block.tensor
        def _(pe):
            pe.wait_ge(s_w, 64)
            for k in range(3):
                nc.tensor.matmul(pre[:, 1, 0, k * N:(k + 1) * N], cv[:, k, :], S["cond"][:], start=True, stop=True).then_inc(s_v, 1)
            pe.wait_ge(s_vid, 3)

            def input_part(t, j, banks):
                for bank in banks:
                    k = ZRC[bank][0]
                    halves_product(nc, pre[:, j, bank, 0:N], S["ident"], vid[:, k, :], True, False)
                    halves_product(nc, pre[:, j, bank, 0:N], w[:, k, :], xs[:, j, :], False, False)

            def gate_part(j):
                for bank in range(2):
                    halves_product(nc, pre[:, j, bank, 0:N], u[:, ZRC[bank][0], :], state[:, j, :], False, True).then_inc(s_pre, 1)

            pe.wait_ge(s_x, 1)
            input_part(0, 0, range(3))
            pe.wait_ge(s_h, 1)
            gate_part(0)

            def step(t, j, more):
                if more or j == 0:
                    pe.wait_ge(s_x, t + 2)
                    input_part(t + 1, 1 - j, (0, 1))
                pe.wait_ge(s_rh, t + 1)
                halves_product(nc, pre[:, j, 2, 0:N], u[:, 2, :], rh[:], False, True).then_inc(s_pre, 1)
                if more or j == 0:
                    input_part(t + 1, 1 - j, (2,))
                    pe.wait_ge(s_h, t + 2)
                    gate_part(1 - j)
            over_steps(pe, step)

        @block.scalar
        def _(act):
            act.wait_ge(s_w, 64)
            nc.scalar.activation(warm[:], b[:], ACT.Sigmoid)

            def step(t, j, more):
                act.wait_ge(s_pre, t * 3 + 1)
                nc.scalar.activation(r[:], pre[:, j, 0, 0:N], ACT.Sigmoid).then_inc(s_gate, 1)
                act.wait_ge(s_pre, t * 3 + 2)
                nc.scalar.activation(keep[:], pre[:, j, 1, 0:N], ACT.Sigmoid, scale=-1.0).then_inc(s_gate, 1)
                nc.scalar.activation(z[:], pre[:, j, 1, 0:N], ACT.Sigmoid).then_inc(s_gate, 1)
                act.wait_ge(s_pre, t * 3 + 3)
                nc.scalar.activation(hh[:], pre[:, j, 2, 0:N], ACT.Tanh).then_inc(s_hh, 1)
            over_steps(act, step)

        @block.vector
        def _(dve):
            nc.vector.memset(state[:, 0, :], 0.0).then_inc(s_h, 1)
            for t in range(2):
                nc.vector.tensor_copy(xs[:, t, :], x[:, t, :]).then_inc(s_x, 1)
            dve.wait_ge(s_w, 64)
            dve.wait_ge(s_v, 3)
            for k in range(3):
                nc.vector.tensor_scalar(vid[:, k, :], pre[:, 1, 0, k * N:(k + 1) * N], b[:, k:k + 1], None, ALU.add).then_inc(s_vid, 1)
            dve.wait_ge(s_h, 1)

            def step(t, j, more):
                dve.wait_ge(s_gate, t * 3 + 1)
                nc.vector.tensor_tensor(rh[:], r[:], state[:, j, :], ALU.mult).then_inc(s_rh, 1)
                dve.wait_ge(s_gate, t * 3 + 2)
                nc.vector.tensor_tensor(kept[:], keep[:], state[:, j, :], ALU.mult).then_inc(s_own, 1)
                dve.wait_ge(s_gate, t * 3 + 3)
                dve.wait_ge(s_hh, t + 1)
                nc.vector.tensor_tensor(new[:], z[:], hh[:], ALU.mult).then_inc(s_own, 1)
                if more:
                    nc.vector.tensor_copy(xs[:, j, :], x[:, t + 2, :]).then_inc(s_x, 1)
                dve.wait_ge(s_own, t * 2 + 2)
                nc.vector.tensor_tensor(state[:, 1 - j, :], new[:], kept[:], ALU.add).then_inc(s_h, 1)
                dve.wait_ge(s_h, t + 2)
                nc.vector.tensor_copy(h[:, t + 1, :], state[:, 1 - j, :])
            over_steps(dve, step)


def router(nc, tag, tokens, d, S, gates_dram, mode, EG):
    E = 8
    with Memory(nc, tag) as m:
        w = m.sb("w", [P, E])
        code = S["code"]
        bias = m.sb("bias", [P, E])
        v = {k: m.sb(k, [P, G, E]) for k in ("score", "value", "eq", "one", "two", "tmp")}
        red = {k: m.sb(k, [P, G]) for k in ("mx", "sum", "rec")}
        gates = m.sb("gates", [P, G, EG])
        logits = m.ps("logits", [P, G * E])
        gT = m.ps("gT", [EG, NT, BANK])
        s_w, s_logits, s_own, s_gates, s_gT, s_rows, s_out = (
            m.sem(k) for k in ("w", "logits", "own", "gates", "gT", "rows", "out"))
        s_in, s_exp = (m.sem("in"), m.sem("exp")) if mode != "argmax" else (None, None)
        nd = 2 if mode == "sigmoid" else 1
        block = m.block()
        wide = lambda a: a[:].rearrange("p (g o) -> p g o", o=1).to_broadcast([P, G, E])
        per = lambda a: a[:].rearrange("p (o e) -> p o e", o=1).to_broadcast([P, G, E])

        @block.sync
        def _(sp):
            sp.dma_start(w[:], d[f"{tag}_w"]).then_inc(s_w, 16)
            if mode == "sigmoid":
                sp.dma_start(bias[:], d[f"{tag}_bias"]).then_inc(s_w, 16)
            sp.wait_ge(s_rows, NT)
            sp.dma_start(gates_dram, S["gates"][0:EG, :]).then_inc(s_out, 16)
            sp.wait_ge(s_out, 16)

        @block.tensor
        def _(pe):
            pe.wait_ge(s_w, 16 * nd)
            for g in range(G):
                last = nc.tensor.matmul(logits[:, g * E:(g + 1) * E], tokens(g), w[:], start=True, stop=True)
            last.then_inc(s_logits, 1)
            pe.wait_ge(s_gates, 1)
            for g in range(G):
                nc.tensor.transpose(gT[:, g // 4, (g % 4) * P:(g % 4 + 1) * P], gates[:, g, :], S["ident"][:]).then_inc(s_gT, 1)

        @block.scalar
        def _(act):
            if mode == "softmax":
                act.wait_ge(s_in, 1)
                nc.scalar.activation(v["value"][:], v["value"][:], ACT.Exp).then_inc(s_exp, 1)
            if mode == "sigmoid":
                act.wait_ge(s_in, 1)
                nc.scalar.activation(v["value"][:], v["value"][:], ACT.Sigmoid).then_inc(s_exp, 1)
            for k in range(NT):
                act.wait_ge(s_gT, 4 * (k + 1))
                nc.scalar.activation(S["gates"][0:EG, k * TILE:(k + 1) * TILE], gT[:, k, :], ACT.Copy).then_inc(s_rows, 1)

        @block.vector
        def _(dve):
            link = chain(dve, s_own)
            tt = nc.vector.tensor_tensor
            lg = logits[:].rearrange("p (g e) -> p g e", e=E)
            value, score, eq, tmp = v["value"], v["score"], v["eq"], v["tmp"]

            def pick(one, src):
                link(nc.vector.tensor_reduce(red["mx"][:], src, AX, ALU.max))
                link(tt(eq[:], src, wide(red["mx"]), ALU.is_ge))
                link(tt(eq[:], eq[:], per(code), ALU.mult))
                link(nc.vector.tensor_reduce(red["mx"][:], eq[:], AX, ALU.max))
                link(tt(one[:], eq[:], wide(red["mx"]), ALU.is_equal))

            dve.wait_ge(s_logits, 1)
            if mode == "softmax":
                link(nc.vector.tensor_reduce(red["mx"][:], lg, AX, ALU.max))
                tt(value[:], lg, wide(red["mx"]), ALU.subtract).then_inc(s_in, 1)
                dve.wait_ge(s_exp, 1)
                link(nc.vector.tensor_reduce(red["sum"][:], value[:], AX, ALU.add))
                link(nc.vector.reciprocal(red["rec"][:], red["sum"][:]))
                link(tt(value[:], value[:], wide(red["rec"]), ALU.mult))
                link(nc.vector.tensor_copy(score[:], value[:]))
            elif mode == "sigmoid":
                nc.vector.tensor_copy(value[:], lg).then_inc(s_in, 1)
                dve.wait_ge(s_exp, 1)
                link(tt(score[:], value[:], per(bias), ALU.add))
            else:
                link(nc.vector.tensor_copy(score[:], lg))
            pick(v["one"], score[:])
            out = gates[:, :, 0:E]
            if mode != "argmax":
                link(nc.vector.scalar_tensor_tensor(tmp[:], v["one"][:], -1e30, score[:], ALU.mult, ALU.add))
                pick(v["two"], tmp[:])
                link(tt(v["one"][:], v["one"][:], v["two"][:], ALU.add))
            if mode == "argmax":
                last = nc.vector.tensor_copy(out, v["one"][:])
            elif mode == "softmax":
                last = tt(out, v["one"][:], value[:], ALU.mult)
            else:
                link(tt(value[:], v["one"][:], value[:], ALU.mult))
                link(nc.vector.tensor_reduce(red["sum"][:], value[:], AX, ALU.add))
                link(nc.vector.tensor_scalar(red["mx"][:], red["sum"][:], 1e-9, None, ALU.is_gt))
                link(nc.vector.tensor_scalar(red["sum"][:], red["sum"][:], 1e-9, None, ALU.add))
                link(nc.vector.reciprocal(red["rec"][:], red["sum"][:]))
                link(tt(value[:], value[:], wide(red["rec"]), ALU.mult))
                link(nc.vector.tensor_scalar(v["two"][:], v["one"][:], 0.5, None, ALU.mult))
                link(tt(value[:], value[:], v["two"][:], ALU.subtract))
                link(tt(value[:], value[:], wide(red["mx"]), ALU.mult))
                last = tt(out, value[:], v["two"][:], ALU.add)
            if EG > E:
                link(last)
                last = nc.vector.memset(gates[:, :, E:EG], 1.0)
            last.then_inc(s_gates, 1)


def experts(nc, tag, tokens, resid, result, d, S, gates_dram, *, E, chunks, kind, act_fn, wcols, shared=None, bufs=2,
            out_view=lambda a: a):
    glu = kind == "glu"
    NCH = len(chunks)
    F = sum(w for _, w in chunks)
    DOWN = F * (2 if glu else 1)
    WMM = DOWN + NCH * P
    U = NT * NCH
    NB = NT
    SKEW = 2 if glu else 3
    with Memory(nc, tag) as m:
        w = [m.sb(f"w{i}", [P, wcols]) for i in range(bufs)]
        whi, wlo = ([m.sb(f"{k}{i}", [P, WMM], F32R) for i in range(bufs)] for k in ("whi", "wlo"))
        gate = [m.sb(f"gate{i}", [P, TOK]) for i in range(bufs)]
        thi, tlo = m.sb("thi", [P, NT, TILE], F32R), m.sb("tlo", [P, NT, TILE], F32R)
        if glu:
            xhi, xlo = m.sb("xhi", [P, bufs, NT, TILE], F32R), m.sb("xlo", [P, bufs, NT, TILE], F32R)
        a = m.sb("a", [P, NB, TILE])
        hb = m.sb("h", [P, NB, TILE])
        hhi, hlo = m.sb("hhi", [P, NB, TILE], F32R), m.sb("hlo", [P, NB, TILE], F32R)
        if shared:
            sw = m.sb("sw", [P, shared["cols"]])
            swhi, swlo = m.sb("swhi", [P, shared["cols"]], F32R), m.sb("swlo", [P, shared["cols"]], F32R)
        b2 = m.sb("b2", [E, P]) if result == "scaled" else None
        warm = m.sb("warm", [P, 1])
        acc = m.ps("acc", [P, NT, BANK])
        up = m.ps("up", [P, 4, BANK])
        s_up, s_act, s_mul, s_high, s_hid, s_down, s_whi, s_wsplit, s_xsplit = (
            m.sem(k) for k in ("up", "act", "mul", "high", "hid", "down", "whi", "wsplit", "xsplit"))
        s_b2 = m.sem("b2") if b2 is not None else None
        s_sw, s_swsplit = (m.sem("sw"), m.sem("swsplit")) if shared else (None, None)
        s_masked = m.sem("masked") if glu else None
        s_w = [m.sem(f"w{i}") for i in range(bufs)]
        SH = shared["units"] if shared else 0
        TURNS = (E - 1) // bufs if E > 2 * bufs else 0
        UPB = 2 if glu or shared else 4
        block = m.block()

        def expert_list(run):
            def body(eng):
                if TURNS:
                    with eng.Fori(0, TURNS) as i:
                        for j in range(bufs):
                            run(SH + (i * bufs + j) * U, i, j, False)
                for e in range(bufs * TURNS, E):
                    run(SH + e * U, e // bufs, e % bufs, e == E - 1)
            return body

        def ahead(step, lead, base, i, j, is_last, u):
            v = u + lead
            if v < U:
                step(base, i, j, v)
            elif not is_last:
                step(base + U, *((i, j + 1) if j + 1 < bufs else (i + 1, 0)), v - U)

        @block.sync
        def _(sp):
            if shared:
                sp.dma_start(sw[:], d[f"{tag}_sw"]).then_inc(s_sw, 16)

            def fetch(e, j):
                sp.dma_start(w[j][:], d[f"{tag}_wp"][e, :, :]).then_inc(s_w[j], 16)
                sp.dma_start(gate[j][:], gates_dram[e, :, :].to_broadcast([P, TOK])).then_inc(s_w[j], 16)

            fetch(0, 0)
            if b2 is not None:
                sp.dma_start(b2[:], d[f"{tag}_b2"]).then_inc(s_b2, 16)
            for j in range(1, bufs):
                fetch(j, j)
            if TURNS > 1:
                with sp.Fori(1, TURNS) as i:
                    for j in range(bufs):
                        sp.wait_ge(s_down, NT + SH + ((i - 1) * bufs + j + 1) * U)
                        fetch(i * bufs + j, j)
            for e in range(bufs * max(TURNS, 1), E):
                sp.wait_ge(s_down, NT + SH + (e - bufs + 1) * U)
                fetch(e, e % bufs)

        @block.gpsimd
        def _(pool):
            if shared:
                pool.wait_ge(s_sw, 16)
                nc.gpsimd.tensor_copy(swhi[:], sw[:]).then_inc(s_swsplit, 1)
                pool.wait_ge(s_swsplit, 1)
                nc.gpsimd.tensor_tensor(swlo[:], sw[:], swhi[:].bitcast(F32), ALU.subtract).then_inc(s_swsplit, 1)
            if glu:
                pool.wait_ge(s_xsplit, NT + 1)

            def run(base, i, j, is_last):
                n = i * bufs + j
                pool.wait_ge(s_w[j], (i + 1) * 32)
                nc.gpsimd.tensor_tensor(whi[j][:], w[j][:, 0:WMM], S["zero"][:].to_broadcast([P, WMM]), ALU.add).then_inc(s_whi, 1)
                pool.wait_ge(s_whi, n + 1)
                nc.gpsimd.tensor_tensor(wlo[j][:], w[j][:, 0:WMM], whi[j][:].bitcast(F32), ALU.subtract).then_inc(s_wsplit, 1)
                if glu:
                    for tile in range(NT):
                        for dst, src in ((xhi, thi), (xlo, tlo)):
                            nc.gpsimd.tensor_tensor(dst[:, j, tile, :], src[:, tile, :].bitcast(F32),
                                                    gate[j][:, tile * TILE:(tile + 1) * TILE], ALU.mult).then_inc(s_masked, 1)
            expert_list(run)(pool)

        @block.tensor
        def _(pe):
            def product(out, left, right, start, stop):
                nc.tensor.matmul(out, left[0], right[0], start=start, stop=False)
                nc.tensor.matmul(out, left[0], right[1], start=False, stop=False)
                return nc.tensor.matmul(out, left[1], right[0], start=False, stop=stop)

            if b2 is not None:
                pe.wait_ge(s_b2, 16)
            for k in range(NT):
                if b2 is not None:
                    start = nc.tensor.matmul(acc[:, k, :], b2[:], S["gates"][0:E, k * TILE:(k + 1) * TILE], start=True, stop=False)
                else:
                    start = nc.tensor.matmul(acc[:, k, :], S["ident"][:], resid(k), start=True, stop=False)
                start.then_inc(s_down, 1)
            if not glu:
                pe.wait_ge(s_xsplit, NT + 1)
            if shared:
                pe.wait_ge(s_swsplit, 2)
                H = shared["nch"] * P
                for u in range(SH + SKEW):
                    if u < SH:
                        tile, c = u // shared["nch"], u % shared["nch"]
                        if u >= 2:
                            pe.wait_ge(s_mul, u - 1)
                        for bank, col in ((u % 2, c * P), (2 + u % 2, H + c * P)):
                            last = product(up[:, bank, :], (swhi[:, col:col + P], swlo[:, col:col + P]),
                                           (thi[:, tile, :], tlo[:, tile, :]), True, True)
                        last.then_inc(s_up, 1)
                    if u >= SKEW:
                        v = u - SKEW
                        tile, c = v // shared["nch"], v % shared["nch"]
                        col = 2 * H + c * P
                        pe.wait_ge(s_hid, v + 1)
                        product(acc[:, tile, :], (swhi[:, col:col + P], swlo[:, col:col + P]),
                                (hhi[:, v % NB, :], hlo[:, v % NB, :]), False, False).then_inc(s_down, 1)

            def up_step(base, i, j, u):
                tile, c = u // NCH, u % NCH
                f0, fw = chunks[c]
                if u == 0:
                    pe.wait_ge(s_wsplit, i * bufs + j + 1)
                if UPB <= SKEW and not (isinstance(base, int) and base == SH and u < UPB):
                    pe.wait_ge(s_mul if glu else s_act, base + u - UPB + 1)
                if glu:
                    if c == 0:
                        pe.wait_ge(s_masked, ((i * bufs + j) * NT + tile + 1) * 2)
                    rhs = (xhi[:, j, tile, :], xlo[:, j, tile, :])
                    product(up[0:fw, u % 2, :], (whi[j][:, f0:f0 + fw], wlo[j][:, f0:f0 + fw]), rhs, True, True)
                    last = product(up[0:fw, 2 + u % 2, :], (whi[j][:, F + f0:F + f0 + fw], wlo[j][:, F + f0:F + f0 + fw]),
                                   rhs, True, True)
                else:
                    last = product(up[0:fw, u % UPB, :], (whi[j][:, f0:f0 + fw], wlo[j][:, f0:f0 + fw]),
                                   (thi[:, tile, :], tlo[:, tile, :]), True, True)
                last.then_inc(s_up, 1)

            def run(base, i, j, is_last):
                for u in range(U):
                    ahead(up_step, SKEW, base, i, j, is_last, u)
                    tile, c = u // NCH, u % NCH
                    fw, col = chunks[c][1], DOWN + c * P
                    pe.wait_ge(s_hid, base + u + 1)
                    product(acc[:, tile, :], (whi[j][0:fw, col:col + P], wlo[j][0:fw, col:col + P]),
                            (hhi[0:fw, u % NB, :], hlo[0:fw, u % NB, :]), False,
                            is_last and c == NCH - 1).then_inc(s_down, 1)
            for u in range(SKEW):
                up_step(SH, 0, 0, u)
            expert_list(run)(pe)

        @block.scalar
        def _(act):
            def high(n, b, fw):
                act.wait_ge(s_down, NT + n - NB + 1)
                act.wait_ge(s_mul, n + 1)
                nc.scalar.copy(hhi[0:fw, b, :], hb[0:fw, b, :]).then_inc(s_high, 1)

            if shared:
                nc.scalar.activation(warm[:], S["ident"][:, 0:1], ACT.Silu)
                for u in range(SH + 1):
                    if u < SH:
                        act.wait_ge(s_up, u + 1)
                        if u >= NB:
                            act.wait_ge(s_mul, u - NB + 1)
                        nc.scalar.activation(a[:, u % NB, :], up[:, u % 2, :], ACT.Silu).then_inc(s_act, 1)
                    if u >= 1:
                        high(u - 1, (u - 1) % NB, P)
            nc.scalar.activation(warm[:], S["ident"][:, 0:1], act_fn)

            def act_step(base, i, j, u):
                if u == 0 and not glu:
                    act.wait_ge(s_w[j], (i + 1) * 32)
                fw = chunks[u % NCH][1]
                act.wait_ge(s_up, base + u + 1)
                bias = 0.0
                if kind == "gelu" and wcols > WMM:
                    bias = w[j][0:fw, WMM + u % NCH:WMM + u % NCH + 1]
                nc.scalar.activation(a[0:fw, u % NB, :], up[0:fw, u % UPB, :], act_fn, bias=bias).then_inc(s_act, 1)

            def run(base, i, j, is_last):
                for u in range(U):
                    ahead(act_step, 1, base, i, j, is_last, u)
                    high(base + u, u % NB, chunks[u % NCH][1])
            act_step(SH, 0, 0, 0)
            expert_list(run)(act)

        @block.vector
        def _(dve):
            def low(n, b, fw):
                dve.wait_ge(s_high, n + 1)
                nc.vector.tensor_tensor(hlo[0:fw, b, :], hb[0:fw, b, :], hhi[0:fw, b, :].bitcast(F32),
                                        ALU.subtract).then_inc(s_hid, 1)

            for k in range(NT):
                nc.vector.tensor_copy(thi[:, k, :], tokens(k)).then_inc(s_xsplit, 1)
            dve.wait_ge(s_xsplit, NT)
            for k in range(NT):
                last = nc.vector.tensor_tensor(tlo[:, k, :], tokens(k), thi[:, k, :].bitcast(F32), ALU.subtract)
            last.then_inc(s_xsplit, 1)
            if shared:
                for u in range(SH + 1):
                    if u < SH:
                        dve.wait_ge(s_act, u + 1)
                        nc.vector.tensor_tensor(hb[:, u % NB, :], up[:, 2 + u % 2, :], a[:, u % NB, :], ALU.mult).then_inc(s_mul, 1)
                    if u >= 1:
                        low(u - 1, (u - 1) % NB, P)

            def mul_step(base, i, j, u):
                if u == 0 and not glu:
                    dve.wait_ge(s_w[j], (i + 1) * 32)
                tile, fw = u // NCH, chunks[u % NCH][1]
                dve.wait_ge(s_act, base + u + 1)
                other = up[0:fw, 2 + u % 2, :] if glu else gate[j][0:fw, tile * TILE:(tile + 1) * TILE]
                nc.vector.tensor_tensor(hb[0:fw, u % NB, :], a[0:fw, u % NB, :], other, ALU.mult).then_inc(s_mul, 1)

            def run(base, i, j, is_last):
                for u in range(U):
                    ahead(mul_step, 1, base, i, j, is_last, u)
                    low(base + u, u % NB, chunks[u % NCH][1])
            mul_step(SH, 0, 0, 0)
            expert_list(run)(dve)
            dve.wait_ge(s_down, NT + SH + E * U)
            for k in range(NT):
                if result == "scaled":
                    nc.vector.scalar_tensor_tensor(resid(k), acc[:, k, :], L0_SCALE, resid(k), ALU.mult, ALU.add)
                else:
                    nc.vector.tensor_copy(result(k), out_view(acc[:, k, :]))


LAYERS = [0, 1, 2, 3]


def build(nc, d, out, scratch, probs_up, probs_down, layers):
    with ExitStack() as x_ctx, ExitStack() as Memory.semaphores:
        sb = lambda name, shape: x_ctx.enter_context(nc.sbuf_tensor(name, shape, F32))
        x = sb("x", [P, T, N])
        h = sb("h", [P, T + 1, N])
        S = {"cond": sb("cond", [P, N]), "ident": sb("ident", [P, P]), "zero": sb("zero", [P, 1]), "code": sb("code", [P, 8]),
             "gates": sb("gates", [9, TOK])}
        load_state(nc, x, d, S)
        xf = x[:].rearrange("p t n -> p (t n)")
        hf = h[:, 1:, :].rearrange("p t n -> p (t n)")
        x_tile = lambda k: xf[:, k * TILE:(k + 1) * TILE]
        h_tile = lambda k: hf[:, k * TILE:(k + 1) * TILE]
        h_group = lambda g: hf[:, g * P:(g + 1) * P]
        if 0 in layers:
            rnn(nc, x, h, d, S)
            router(nc, "r0", h_group, d, S, scratch[:, 0, :], "softmax", 9)
            experts(nc, "e0", h_tile, x_tile, "scaled", d, S, scratch, E=9,
                    chunks=[(c * P, P) for c in range(4)], kind="gelu", act_fn=ACT.Gelu_apprx_tanh, wcols=8 * P + 4)
        if 1 in layers:
            lstm(nc, x, h, d, S)
            kron_moe(nc, x, h, d, S, (probs_up, probs_down))
        if 2 in layers:
            hid = h[:, 1:, :].rearrange("p t n -> p (t n)").rearrange("p (n t) -> p n t", n=N)
            gated_scan(nc, x, hid, d, S)
            router(nc, "r2", h_group, d, S, scratch[0:8, 0, :], "argmax", 8)
            C = TILE // T
            xn = lambda k: x[:].rearrange("p t n -> p n t")[:, k * C:(k + 1) * C, :]
            experts(nc, "e2", h_tile, xn, xn, d, S, scratch, E=8,
                    chunks=[(0, 128), (128, 128), (256, 96)], kind="glu", act_fn=ACT.Silu, wcols=2 * 352 + 3 * P,
                    out_view=lambda a: a.rearrange("p (n t) -> p n t", t=T))
        if 3 in layers:
            gru(nc, x, h, d, S)
            router(nc, "r3", h_group, d, S, scratch[0:8, 0, :], "sigmoid", 8)
            experts(nc, "e3", h_tile, x_tile, x_tile, d, S, scratch, E=8, chunks=[(0, 128)], kind="gelu",
                    act_fn=ACT.Gelu, wcols=2 * P, shared={"cols": 3 * 2 * P, "nch": 2, "units": 2 * NT}, bufs=4)
        store_state(nc, x, out)


def lay_out(i):
    t = lambda a, *axes: np.ascontiguousarray(np.transpose(a, axes))
    cat, pad = np.concatenate, np.pad
    col = lambda *bs: np.ascontiguousarray(np.stack(bs, 1))
    a = {"xT": t(i["x"], 2, 1, 0), "condT": t(i["cond_1024"], 1, 0)}
    a["l0_wx"], a["l0_wh"], a["l0_b"] = i["L0_cond_Wx"], i["L0_cond_Wh"], i["L0_cond_b"][:, None]
    a["r0_w"] = t(i["L0_ffn_w_router"], 1, 0)
    w1 = t(cat([i["L0_ffn_W1"], i["L0_ffn_Ws1"][None]]), 0, 2, 1)
    w2 = cat([i["L0_ffn_W2"], i["L0_ffn_Ws2"][None]]).reshape(9, P, 4, P).transpose(0, 3, 2, 1).reshape(9, P, 4 * P)
    b1 = cat([i["L0_ffn_b1"], i["L0_ffn_bs1"][None]]).reshape(9, 4, P).transpose(0, 2, 1)
    a["e0_wp"] = np.ascontiguousarray(cat([w1, w2, b1], 2))
    a["e0_b2"] = cat([i["L0_ffn_b2"], i["L0_ffn_bs2"][None]])
    a["l1_wx"] = i["L1_cond_Wx"].reshape(P, 4, P)
    a["l1_wh"] = i["L1_cond_Wh"].reshape(P, 4, P)
    a["l1_b"] = t(i["L1_cond_b"].reshape(4, P), 1, 0)
    a["l2_w"] = col(*(i[f"L2_cond_W_{k}"].T for k in "fih"))
    a["l2_b"] = col(*(i[f"L2_cond_b_{k}"] for k in "fih"))
    a["r2_w"] = t(i["L2_ffn_router_w"], 1, 0)
    dw = pad(t(i["L2_ffn_down_w"], 0, 2, 1), ((0, 0), (0, 32), (0, 0))).reshape(8, 3, P, P).transpose(0, 2, 1, 3)
    a["e2_wp"] = np.ascontiguousarray(cat([t(i["L2_ffn_gate_w"], 0, 2, 1), t(i["L2_ffn_up_w"], 0, 2, 1),
                                           dw.reshape(8, P, 3 * P)], 2))
    a["l3_w"] = col(i["L3_cond_W_z"], i["L3_cond_W_r"], i["L3_cond_W"])
    a["l3_u"] = col(i["L3_cond_U_z"], i["L3_cond_U_r"], i["L3_cond_U"])
    a["l3_c"] = col(i["L3_cond_C_z"], i["L3_cond_C_r"], i["L3_cond_C"])
    a["l3_b"] = col(i["L3_cond_b_z"], i["L3_cond_b_r"], i["L3_cond_b"])
    a["r3_w"] = t(i["L3_ffn_router_w"], 1, 0)
    a["r3_bias"] = np.ascontiguousarray(np.broadcast_to(i["L3_ffn_router_bias"], (P, 8)))
    a["e3_sw"] = cat([i["L3_ffn_sw1"], i["L3_ffn_sw3"],
                      i["L3_ffn_sw2"].reshape(2, P, P).transpose(1, 0, 2).reshape(P, 2 * P)], 1)
    a["e3_wp"] = cat([i["L3_ffn_ew1"], i["L3_ffn_ew2"]], 2)
    tab = (i["L1_ffn_A_up"].reshape(64, 64, 8, 4).transpose(0, 1, 3, 2), i["L1_ffn_B_up"],
           i["L1_ffn_A_down"], i["L1_ffn_B_down"])
    a["k_tab"] = np.stack([cat([v.reshape(64, 2048)] * 2) for v in tab])
    a["k_wup"] = i["L1_ffn_W_up"].reshape(64, 8, P).transpose(2, 1, 0)
    a["k_wdown"] = cat([i["L1_ffn_W_down"].reshape(64, 64, 64).transpose(2, 1, 0)] * 2)
    a["k_bias_up"] = np.tile(i["L1_ffn_bias_up"].reshape(64, 64).T, (2, 2 * BPT))
    a["k_bias_down"] = i["L1_ffn_bias_down"].reshape(8, P).T
    a["k_scale_up"] = np.broadcast_to(i["L1_ffn_scale_up"][None], (P, 1))
    a["k_scale_down"] = np.broadcast_to(i["L1_ffn_scale_down"][None], (P, 1))
    a["k_cst"] = patterns()
    return {k: np.ascontiguousarray(v) for k, v in a.items()}


def patterns():
    p, c = np.arange(P)[:, None], np.arange(P)[None, :]
    parts = [
        p // 32 == c // 8 % 4,
        p // 32 == c // 32,
        p // 64 == c // 64,
        (p // 64 == c // 32 % 2) & (p // 32 % 2 == c // 64),
        np.broadcast_to(c % 64, (P, P)),
        p % 32 == c[:, :32],
        p // 32 % 2 == c[:, :2],
        p // 64 == c[:, :2],
    ]
    return np.concatenate([v.astype(np.float32) for v in parts], 1)


def kernel(**inputs):
    import concourse.bacc as bacc
    from concourse.bass_utils import run_bass_kernel_spmd as run

    arrays = lay_out({k: np.asarray(v) for k, v in inputs.items()})
    nc = bacc.Bacc("TRN2", target_bir_lowering=False, num_devices=1)
    d = {k: nc.dram_tensor("in_" + k, v.shape, mybir.dt.from_np(v.dtype), kind="ExternalInput").ap() for k, v in arrays.items()}
    out = nc.dram_tensor("out_x", (P, T, N), F32, kind="ExternalOutput").ap()
    scratch = nc.dram_tensor("gate_rows", (9, 1, TOK), F32, kind="Internal").ap()
    probs_up = nc.dram_tensor("probs_up", (4, 2 * BLK), F32, kind="Internal").ap()
    probs_down = nc.dram_tensor("probs_down", (2, 4 * BLK), F32, kind="Internal").ap()
    build(nc, d, out, scratch, probs_up, probs_down, LAYERS)
    r = run(nc, [{"in_" + k: v for k, v in arrays.items()}], core_ids=[0])
    return np.ascontiguousarray(np.transpose(r.results[0]["out_x"], (2, 1, 0)))
```

```python
from contextlib import ExitStack

import numpy as np
import concourse.bass as bass
from concourse import mybir

F32 = mybir.dt.float32
F32R = mybir.dt.float32r
BF16 = mybir.dt.bfloat16
U32 = mybir.dt.uint32
ACT = mybir.ActivationFunctionType
ALU = mybir.AluOpType
AX = mybir.AxisListType.X

P = 128
T = 32
N = 64
TOK = T * N
TILE = 512
NT = TOK // TILE
G = TOK // P
BANK = 512
L0_SCALE = 1.0 / float(np.sqrt(1 + 2 / 8))


class Chain:

    def __init__(self, sem):
        self.sem, self.count = sem, 0

    def on(self, eng):
        def link(ins):
            self.count += 1
            ins.then_inc(self.sem, 1)
            eng.wait_ge(self.sem, self.count)

        return link


class Memory:

    semaphores = None

    def __init__(self, nc, tag):
        self.nc, self.tag, self.ctx = nc, tag, ExitStack()

    def __enter__(self):
        self.ctx.__enter__()
        return self

    def __exit__(self, *a):
        return self.ctx.__exit__(*a)

    def sb(self, name, shape, dt=F32):
        return self.ctx.enter_context(self.nc.sbuf_tensor(f"{self.tag}_{name}", shape, dt))

    def ps(self, name, shape, dt=F32):
        return self.ctx.enter_context(self.nc.psum_tensor(f"{self.tag}_{name}", shape, dt))

    def sem(self, name):
        return Memory.semaphores.enter_context(self.nc.semaphore(f"{self.tag}_{name}"))

    def block(self):
        return self.ctx.enter_context(self.nc.Block())


def load_state(nc, x, d, S):
    with Memory(nc, "load") as m:
        s_in, s_const = m.sem("in"), m.sem("const")
        block = m.block()

        @block.sync
        def _(sp):
            sp.dma_start(x[:], d["xT"]).then_inc(s_in, 16)
            sp.dma_start(S["cond"][:], d["condT"]).then_inc(s_in, 16)
            sp.wait_ge(s_in, 32)

        @block.gpsimd
        def _(pool):
            pool.memset(S["ident"][:], 0.0).then_inc(s_const, 1)
            pool.wait_ge(s_const, 1)
            pool.affine_select(out=S["ident"][:], in_=S["ident"][:], compare_op=ALU.not_equal, fill=1.0,
                               base=0, pattern=[[-1, P]], channel_multiplier=1).then_inc(s_const, 1)
            pool.wait_ge(s_const, 2)
            pool.memset(S["zero"][:], 0.0)
            for e in range(8):
                pool.memset(S["code"][:, e:e + 1], float(8 - e))


def store_state(nc, x, out):
    with Memory(nc, "store") as m:
        s_out = m.sem("out")
        block = m.block()

        @block.sync
        def _(sp):
            sp.dma_start(out, x[:]).then_inc(s_out, 16)
            sp.wait_ge(s_out, 16)


H2 = P // 2


def halves_product(nc, out, w, right, start, stop):
    for m in range(2):
        half = slice(m * H2, (m + 1) * H2)
        last = nc.tensor.matmul(out[half], w[:, half], right, start=start, stop=stop)
    return last


def over_steps(eng, step):
    with eng.Fori(0, T // 2 - 1) as i:
        for j in range(2):
            step(i * 2 + j, j, True)
    for j in range(2):
        step(T - 2 + j, j, False)


def rnn(nc, x, h, d, S):
    with Memory(nc, "rnn") as m:
        wx, wh, b, warm = m.sb("wx", [P, P]), m.sb("wh", [P, P]), m.sb("b", [P, 1]), m.sb("warm", [P, 1])
        state, xs = m.sb("state", [P, 2, N]), m.sb("xs", [P, 2, N])
        pre = m.ps("pre", [P, 2, BANK])
        s_w, s_x, s_pre, s_h, s_copied = (m.sem(k) for k in ("w", "x", "pre", "h", "copied"))
        block = m.block()

        @block.sync
        def _(sp):
            sp.dma_start(wx[:], d["l0_wx"]).then_inc(s_w, 16)
            sp.dma_start(wh[:], d["l0_wh"]).then_inc(s_w, 16)
            sp.dma_start(b[:], d["l0_b"]).then_inc(s_w, 16)

        @block.vector
        def _(dve):
            for t in range(2):
                nc.vector.tensor_copy(xs[:, t, :], x[:, t, :]).then_inc(s_x, 1)
            nc.vector.tensor_copy(state[:, 0, :], S["cond"][:]).then_inc(s_copied, 1)

            def step(t, j, more):
                dve.wait_ge(s_h, t + 1)
                if more:
                    nc.vector.tensor_copy(xs[:, j, :], x[:, t + 2, :]).then_inc(s_x, 1)
                nc.vector.tensor_copy(h[:, t + 1, :], state[:, 1 - j, :]).then_inc(s_copied, 1)
            over_steps(dve, step)

        @block.tensor
        def _(pe):
            def input_part(t, j):
                pe.wait_ge(s_x, t + 1)
                halves_product(nc, pre[:, j, 0:N], wx, xs[:, j, :], True, False)

            pe.wait_ge(s_w, 48)
            input_part(0, 0)
            pe.wait_ge(s_copied, 1)
            halves_product(nc, pre[:, 0, 0:N], wh, state[:, 0, :], False, True).then_inc(s_pre, 1)

            def step(t, j, more):
                if more or j == 0:
                    input_part(t + 1, 1 - j)
                    pe.wait_ge(s_h, t + 1)
                    halves_product(nc, pre[:, 1 - j, 0:N], wh, state[:, 1 - j, :], False, True).then_inc(s_pre, 1)
            over_steps(pe, step)

        @block.scalar
        def _(act):
            act.wait_ge(s_w, 48)
            nc.scalar.activation(warm[:], b[:], ACT.Tanh)

            def step(t, j, more):
                act.wait_ge(s_pre, t + 1)
                act.wait_ge(s_copied, t + 1)
                nc.scalar.activation(state[:, 1 - j, :], pre[:, j, 0:N], ACT.Tanh, bias=b[:]).then_inc(s_h, 1)
            over_steps(act, step)


def lstm(nc, x, h, d, S, beside):
    I, FORGET, O, CAND = range(4)
    ORDER = (CAND, I, FORGET, O)
    with Memory(nc, "lstm") as m:
        wx, wh, b = m.sb("wx", [P, 4, P]), m.sb("wh", [P, 4, P]), m.sb("b", [P, 4])
        warm, gates = m.sb("warm", [P, 4]), m.sb("gates", [P, 4, N])
        c, fc, ig, tc = (m.sb(k, [P, N]) for k in ("c", "fc", "ig", "tc"))
        state, xs = m.sb("state", [P, 2, N]), m.sb("xs", [P, 2, N])
        pre = m.ps("pre", [P, 2, 4, BANK])
        s_w, s_x, s_pre, s_gates, s_own, s_c, s_tc, s_h = (
            m.sem(k) for k in ("w", "x", "pre", "gates", "own", "c", "tc", "h"))
        sync_beside, gpsimd_beside, scalar_after, vector_after = beside(m)
        block = m.block()

        @block.sync
        def _(sp):
            sp.dma_start(wx[:], d["l1_wx"]).then_inc(s_w, 16)
            sp.dma_start(wh[:], d["l1_wh"]).then_inc(s_w, 16)
            sp.dma_start(b[:], d["l1_b"]).then_inc(s_w, 16)
            sync_beside(sp)

        @block.gpsimd
        def _(pool):
            gpsimd_beside(pool)

        @block.tensor
        def _(pe):
            pe.wait_ge(s_w, 48)

            def input_part(t, j):
                pe.wait_ge(s_x, t + 1)
                for k in ORDER:
                    halves_product(nc, pre[:, j, k, 0:N], wx[:, k, :], xs[:, j, :], True, False)

            def state_part(j):
                for k in ORDER:
                    halves_product(nc, pre[:, j, k, 0:N], wh[:, k, :], state[:, j, :], False, True).then_inc(s_pre, 1)

            input_part(0, 0)
            pe.wait_ge(s_h, 1)
            state_part(0)

            def step(t, j, more):
                if more or j == 0:
                    input_part(t + 1, 1 - j)
                    pe.wait_ge(s_h, t + 2)
                    state_part(1 - j)
            over_steps(pe, step)

        @block.scalar
        def _(act):
            act.wait_ge(s_w, 48)
            nc.scalar.activation(warm[:], b[:], ACT.Sigmoid)

            def step(t, j, more):
                for n, k in enumerate(ORDER):
                    act.wait_ge(s_pre, t * 4 + n + 1)
                    nc.scalar.activation(gates[:, k, :], pre[:, j, k, 0:N], ACT.Tanh if k == CAND else ACT.Sigmoid,
                                         bias=b[:, k:k + 1]).then_inc(s_gates, 1)
                act.wait_ge(s_c, t + 2)
                nc.scalar.activation(tc[:], c[:], ACT.Tanh).then_inc(s_tc, 1)
            over_steps(act, step)
            scalar_after(act)

        @block.vector
        def _(dve):
            nc.vector.tensor_copy(state[:, 0, :], S["cond"][:]).then_inc(s_h, 1)
            for t in range(2):
                nc.vector.tensor_copy(xs[:, t, :], x[:, t, :]).then_inc(s_x, 1)
            nc.vector.memset(c[:], 0.0).then_inc(s_c, 1)
            dve.wait_ge(s_c, 1)

            def step(t, j, more):
                dve.wait_ge(s_gates, t * 4 + 2)
                nc.vector.tensor_tensor(ig[:], gates[:, I, :], gates[:, CAND, :], ALU.mult).then_inc(s_own, 1)
                dve.wait_ge(s_gates, t * 4 + 3)
                nc.vector.tensor_tensor(fc[:], gates[:, FORGET, :], c[:], ALU.mult).then_inc(s_own, 1)
                dve.wait_ge(s_own, t * 2 + 2)
                nc.vector.tensor_tensor(c[:], fc[:], ig[:], ALU.add).then_inc(s_c, 1)
                dve.wait_ge(s_gates, t * 4 + 4)
                if more:
                    nc.vector.tensor_copy(xs[:, j, :], x[:, t + 2, :]).then_inc(s_x, 1)
                dve.wait_ge(s_tc, t + 1)
                nc.vector.tensor_tensor(state[:, 1 - j, :], gates[:, O, :], tc[:], ALU.mult).then_inc(s_h, 1)
                dve.wait_ge(s_h, t + 2)
                nc.vector.tensor_copy(h[:, t + 1, :], state[:, 1 - j, :])
            over_steps(dve, step)
            vector_after(dve)


E64 = 64
TB = T // 8
BLK = TB * N // 4
BPT = 4


class Turns:

    COUNT = BLK // BPT

    def __init__(self, depth):
        self.depth = depth

    def run(self, eng, step):
        for s in range(4):
            step(s, s % 2)
        with eng.Fori(2, self.COUNT // 2) as i:
            for j in range(2):
                step(i * 2 + j, j)
        for s in range(self.COUNT, self.COUNT + self.depth):
            step(s, s % 2)


def live(v):
    return not isinstance(v, int) or 0 <= v < Turns.COUNT


def freed(eng, sem, v):
    if not isinstance(v, int) or v >= 2:
        eng.wait_ge(sem, v - 1)


def split_tables(m, d, K, space, constants):
    nc = m.nc
    tab = [space[:, i * 2048:(i + 1) * 2048] for i in range(4)]
    mid = [m.sb(f"mid{i}", [P, 2048], BF16) for i in range(2)]
    s_in = [m.sem(f"table{i}") for i in range(2)]
    s_split, s_const = m.sem("split"), m.sem("const")
    s_mid = [m.sem(f"moved{i}") for i in range(2)]

    def sync(sp):
        for i in range(4):
            sp.dma_start(tab[i], d["k_tab"][i]).then_inc(s_in[i // 2], 16)
        for dst, key in constants:
            sp.dma_start(dst, d[key]).then_inc(s_const, 16)
        for i in range(4):
            sp.wait_ge(s_split, 4 * i + 3)
            sp.dma_start(K["hm"][i][E64:P, :], mid[i % 2][E64:P, :]).then_inc(s_mid[i % 2], 16)
        for i in range(2):
            sp.wait_ge(s_mid[i], 32)
        sp.wait_ge(s_const, 16 * len(constants))

    def gpsimd(pool):
        link = Chain(s_split).on(pool)
        for i in range(4):
            pool.wait_ge(s_in[i // 2], 32)
            link(nc.gpsimd.tensor_copy(K["hm"][i][:], tab[i]))
            link(nc.gpsimd.tensor_tensor(tab[i], tab[i], K["hm"][i][:], ALU.subtract))
            if i == 3:
                break
            if i >= 2:
                pool.wait_ge(s_mid[i % 2], 16)
            link(nc.gpsimd.tensor_copy(mid[i % 2][:], tab[i]))
            link(nc.gpsimd.tensor_tensor(K["lo"][i][:], tab[i][0:E64, :], mid[i % 2][0:E64, :], ALU.subtract))

    def scalar(act):
        act.wait_ge(s_split, 4 * 3 + 2)
        act.wait_ge(s_mid[3 % 2], 16)
        nc.scalar.copy(mid[3 % 2][:], tab[3]).then_inc(s_split, 1)

    def vector(dve):
        dve.wait_ge(s_split, 4 * 3 + 3)
        nc.vector.tensor_tensor(K["lo"][3][:], tab[3][0:E64, :], mid[3 % 2][0:E64, :], ALU.subtract)

    return sync, gpsimd, scalar, vector


def pick_two(nc, pick, link, logits, K, halves):
    top, idx, idxf, hot = pick
    for r in range(2):
        link(nc.vector.tensor_copy(halves[:, r, :], logits(r)))
        link(nc.vector.max(top[:, r, :], halves[:, r, :]))
        link(nc.vector.max_index(idx[:, r, :], top[:, r, :], halves[:, r, :]))
    link(nc.vector.tensor_copy(idxf[:], idx[:]))
    for r in range(2):
        for k in range(2):
            link(nc.vector.tensor_scalar(hot[:, r, k, :], K["iota"], idxf[:, r, k:k + 1], None, ALU.is_equal))


def kron_route(nc, tag, mats, d, K, hotT, prob, probs_dram, cls, scale):
    NBK = 8 * BLK // cls
    pr, pb = K["pr"], K["pb"]
    with Memory(nc, tag) as m:
        bankL = m.ps("logits", [P, 2, BANK])
        turned = m.sb("turned", [P, P])
        psT = m.ps("hotT", [P, 2, 2, 2 * BANK], BF16)
        halves = m.sb("halves", [P, 2, E64])
        diff = m.sb("diff", [P, 2, 2])
        top, idx, idxf = m.sb("top", [P, 2, 8]), m.sb("idx", [P, 2, 8], U32), m.sb("idxf", [P, 2, 8])
        hot = m.sb("hot", [P, 2, 2, P], BF16)
        s_logits, s_turned, s_hot, s_T, s_diff, s_pr, s_dram, s_pb, s_hotT = (
            m.sem(k) for k in ("logits", "turned", "hot", "T", "diff", "pr", "dram", "pb", "hotT"))
        block = m.block()

        @block.tensor
        def _(pe):
            if cls == 4:
                for r in range(2):
                    def emit(left, right, **flags):
                        for n in range(2):
                            half = slice(E64 * n, E64 * (n + 1))
                            last = nc.tensor.matmul(bankL[half, r, 0:E64], left(r)[:, half], right, **flags)
                        return last
                    mats(pe, emit).then_inc(s_logits, 1)
            else:
                mats(pe, lambda left, right, **flags: nc.tensor.matmul(bankL[:, 0, 0:P], left, right, **flags)).then_inc(s_logits, 1)
                pe.wait_ge(s_turned, 1)
                nc.tensor.transpose(bankL[:, 1, 0:P], turned[:], K["ident"][:]).then_inc(s_logits, 1)
            pe.wait_ge(s_hot, 1)
            for r in range(2):
                for k in range(2):
                    nc.tensor.transpose(psT[:, r, k, 0:P], hot[:, r, k, :], K["identb"][:]).then_inc(s_T, 1)

        @block.vector
        def _(dve):
            link = K["dve_chain"].on(dve)
            if cls == 2:
                dve.wait_ge(s_logits, 1)
                nc.vector.tensor_copy(turned[:], bankL[:, 0, 0:P]).then_inc(s_turned, 1)
            dve.wait_ge(s_logits, 2)
            pick_two(nc, (top, idx, idxf, hot), link,
                     lambda r: bankL[:, r, 0:E64] if cls == 4 else bankL[:, 1, r * E64:(r + 1) * E64], K, halves)
            nc.vector.tensor_tensor(diff[:, :, 0:1], top[:, :, 0:1], top[:, :, 1:2], ALU.subtract).then_inc(s_hot, 1)
            nc.vector.tensor_tensor(diff[:, :, 1:2], top[:, :, 1:2], top[:, :, 0:1], ALU.subtract).then_inc(s_diff, 1)
            dve.wait_ge(s_T, 4)
            for r in range(2):
                for k in range(2):
                    src = psT[:, r, k, 0:P]
                    if cls == 4:
                        dst = hotT[:].rearrange("p c (b k) -> p k b c", k=2)[:, k, r * BLK // 2:(r + 1) * BLK // 2, :]
                        src = src.rearrange("p (b c) -> p b c", c=4)
                    else:
                        dst = hotT[:].rearrange("p c (b k) -> p c k b", k=2)[:, r, k, :]
                    nc.vector.tensor_copy(dst, src).then_inc(s_hotT, 1)

        @block.scalar
        def _(act):
            act.wait_ge(s_diff, 1)
            act.wait_ge(s_hot, 1)
            nc.scalar.activation(pr[:], diff[:], ACT.Sigmoid).then_inc(s_pr, 1)

    def spread(sp):
        sp.wait_ge(s_pr, 1)
        for r in range(2):
            if cls == 4:
                dst = probs_dram.rearrange("c (b k) -> b c k", k=2)[r * BLK // 2:(r + 1) * BLK // 2, :, :]
            else:
                dst = probs_dram.rearrange("c (b k) -> c b k", k=2)[r, :, :]
            sp.dma_start(dst, pr[:, r, :]).then_inc(s_dram, 16)
        sp.wait_ge(s_dram, 32)
        w = P // cls
        for c in range(cls):
            sp.dma_start(pb[c * w:(c + 1) * w, 0:NBK], probs_dram[c:c + 1, :].to_broadcast([w, NBK])).then_inc(s_pb, 16)

    def scale_and_mask(dve):
        link = K["dve_chain"].on(dve)
        dve.wait_ge(s_pb, 16 * cls)
        link(nc.vector.tensor_scalar(pb[:, 0:NBK] if cls == 4 else prob[:], pb[:, 0:NBK], scale[:], None, ALU.mult))
        if cls == 4:
            for q in range(2):
                link(nc.vector.tensor_scalar(prob[:, :, q], pb[:, 0:NBK], K["half4"][:, q:q + 1], None, ALU.mult))

    return spread, scale_and_mask


def kron_gather(nc, tag, K, tabs, hotT, dst, cls, beside):
    w = P // cls
    PER = P // w
    COLS = BANK // PER
    TURNS = 2048 // P
    with Memory(nc, tag) as m:
        hm = [m.sb(f"hm{j}", [P, 2, P], BF16) for j in range(2)]
        lo = [m.sb(f"lo{j}", [E64, 2, P], BF16) for j in range(2)]
        out = m.ps("out", [P, 2, 2, BANK])
        s_hm, s_lo, s_pick, s_gotA, s_gotB = (m.sem(k) for k in ("hm", "lo", "pick", "gotA", "gotB"))
        block = m.block()
        spread, scale_and_mask = beside

        @block.sync
        def _(sp):
            spread(sp)

        def loop(eng, turn):
            for v in range(2):
                turn(v, v)
            with eng.Fori(1, TURNS // 2 - 1) as i:
                for j in range(2):
                    turn(i * 2 + j, j)
            for j in range(2):
                turn(TURNS - 2 + j, j)

        @block.gpsimd
        def _(pool):
            def turn(v, j):
                freed(pool, s_pick, v)
                for t in range(2):
                    c = bass.ds(v * P, P)
                    nc.gpsimd.tensor_copy(hm[j][:, t, :], K["hm"][tabs[t]][:, c]).then_inc(s_hm, 1)
            loop(pool, turn)

        @block.tensor
        def _(pe):
            def turn(v, j):
                pe.wait_ge(s_hm, v * 2 + 2)
                pe.wait_ge(s_lo, v * 2 + 2)
                freed(pe, s_gotA, v)
                freed(pe, s_gotB, v)
                for t in range(2):
                    for o in range(PER):
                        for c in range(cls):
                            at = out[c * w:(c + 1) * w, j, t, o * COLS:(o + 1) * COLS]
                            nc.tensor.matmul(at, hm[j][:, t, o * w:(o + 1) * w], hotT[:, c, :], start=True, stop=False)
                            last = nc.tensor.matmul(at, lo[j][:, t, o * w:(o + 1) * w], hotT[0:E64, c, :], start=False, stop=True)
                last.then_inc(s_pick, 1)
            loop(pe, turn)

        def put(t, v):
            return dst[t][:].rearrange("p c o -> p o c")[:, bass.ds(v * PER, PER), :]

        @block.scalar
        def _(act):
            def stage(v, j):
                for t in range(2):
                    nc.scalar.copy(lo[j][:, t, :], K["lo"][tabs[t]][:, bass.ds(v * P, P)]).then_inc(s_lo, 1)

            for v in range(2):
                stage(v, v)

            def turn(v, j):
                act.wait_ge(s_pick, v + 1)
                nc.scalar.copy(put(0, v), out[:, j, 0, :].rearrange("p (o c) -> p o c", o=PER)).then_inc(s_gotA, 1)
                if not isinstance(v, int) or v + 2 < TURNS:
                    stage(v + 2, j)
            loop(act, turn)

        @block.vector
        def _(dve):
            def turn(v, j):
                dve.wait_ge(s_pick, v + 1)
                nc.vector.tensor_copy(put(1, v), out[:, j, 1, :].rearrange("p (o c) -> p o c", o=PER)).then_inc(s_gotB, 1)
            loop(dve, turn)
            scale_and_mask(dve)


def kron_up(nc, K, bias, rows, GA, GB, prob, H, fetch):
    with Memory(nc, "up") as m:
        xm = m.sb("xm", [P, 2, BPT, P])
        xd = m.sb("xd", [P, 2, BPT, P])
        vd = m.sb("vd", [P, 2, BPT, 2, P])
        gb = m.sb("gb", [P, 2, BPT, P])
        warm = m.sb("warm", [P, 1])
        px, pv = m.ps("px", [P, 2, BANK]), m.ps("pv", [P, 2, BANK])
        ph = m.ps("ph", [P, 2, BANK])
        s_fetch, s_xm, s_px, s_xd, s_pv, s_vd, s_ph, s_h, s_gb = (
            m.sem(k) for k in ("fetch", "xm", "px", "xd", "pv", "vd", "ph", "h", "gb"))
        block = m.block()
        turns = Turns(2)
        W = 2 * BPT

        @block.sync
        def _(sp):
            sp.dma_start(*fetch).then_inc(s_fetch, 16)
            sp.wait_ge(s_fetch, 16)

        @block.gpsimd
        def _(pool):
            def step(s, j):
                if live(s):
                    freed(pool, s_px, s)
                    nc.gpsimd.tensor_tensor(
                        xm[:, j, :, :].rearrange("p b (n q t) -> p (b n) q t", n=4, q=4),
                        rows[:, bass.ds(s * 32 * BPT, 32 * BPT)].rearrange("p (r o t) -> p r o t", o=1, t=8)
                        .to_broadcast([P, 4 * BPT, 4, 8]),
                        K["mq"][:, 0:32].rearrange("p (o q t) -> p o q t", o=1, q=4).to_broadcast([P, 4 * BPT, 4, 8]),
                        ALU.mult).then_inc(s_xm, 1)
            turns.run(pool, step)

        @block.tensor
        def _(pe):
            def step(s, j):
                if live(s):
                    pe.wait_ge(s_xm, s + 1)
                    freed(pe, s_xd, s)
                    for b in range(BPT):
                        for n in range(4):
                            row = slice(32 * n, 32 * (n + 1))
                            last = nc.tensor.matmul(px[row, j, b * 32:(b + 1) * 32], xm[:, j, b, row], K["fold"], start=True, stop=True)
                    last.then_inc(s_px, 1)
                v, i = s - 1, (j + 1) % 2
                if live(v):
                    pe.wait_ge(s_xd, v + 1)
                    freed(pe, s_vd, v)
                    for b in range(BPT):
                        last = nc.tensor.matmul(pv[:, i, b * P:(b + 1) * P], xd[:, i, b, :],
                                                GA[:, bass.ds(v * W + 2 * b, 2), :].rearrange("p k o -> p (k o)"),
                                                start=True, stop=True)
                    last.then_inc(s_pv, 1)
                v = s - 2
                if live(v):
                    pe.wait_ge(s_vd, v + 1)
                    pe.wait_ge(s_gb, v + 1)
                    freed(pe, s_h, v)
                    nc.tensor.matmul(ph[:, j, :], K["ident"][:], bias[:], start=True, stop=False)
                    for b in range(BPT):
                        for q in range(2):
                            half = slice(E64 * q, E64 * (q + 1))
                            for k in range(2):
                                last = nc.tensor.matmul(ph[half, j, b * P:(b + 1) * P], gb[half, j, b, k * E64:(k + 1) * E64],
                                                        vd[half, j, b, k, :], start=False, stop=(b, k) == (BPT - 1, 1))
                    last.then_inc(s_ph, 1)
            turns.run(pe, step)

        @block.vector
        def _(dve):
            def step(s, j):
                if live(s):
                    dve.wait_ge(s_px, s + 1)
                    freed(dve, s_pv, s)
                    nc.vector.tensor_tensor(
                        xd[:, j, :, :].rearrange("p b (n j) -> p b n j", n=4),
                        px[:, j, 0:32 * BPT].rearrange("p (b o j) -> p b o j", b=BPT, o=1).to_broadcast([P, BPT, 4, 32]),
                        K["mn"].rearrange("p (o n j) -> p o n j", o=1, n=4).to_broadcast([P, BPT, 4, 32]),
                        ALU.mult).then_inc(s_xd, 1)
                v, i = s - 1, (j + 1) % 2
                if live(v):
                    dve.wait_ge(s_pv, v + 1)
                    freed(dve, s_ph, v)
                    nc.vector.tensor_tensor(
                        vd[:, i, :, :, :].rearrange("p b k (m o) -> p (b k) m o", m=2),
                        pv[:, i, :].rearrange("p (w m o) -> p w m o", w=W, m=1).to_broadcast([P, W, 2, E64]),
                        prob[:, bass.ds(v * W, W), :].rearrange("p k (m o) -> p k m o", o=1).to_broadcast([P, W, 2, E64]),
                        ALU.mult).then_inc(s_vd, 1)
            turns.run(dve, step)

        @block.scalar
        def _(act):
            nc.scalar.activation(warm[:], K["ident"][:, 0:1], ACT.Gelu)

            def step(s, j):
                v, i = s - 1, (j + 1) % 2
                if live(v):
                    freed(act, s_ph, v)
                    nc.scalar.copy(gb[:, i, :, :].rearrange("p b c -> p (b c)"),
                                   GB[:, bass.ds(v * W, W), :].rearrange("p c o -> p (c o)")).then_inc(s_gb, 1)
                v = s - 2
                if live(v):
                    act.wait_ge(s_ph, v + 1)
                    nc.scalar.activation(H[:, bass.ds(v * BPT, BPT), :, :].rearrange("p b n o -> p (b n o)"), ph[:, j, :],
                                         ACT.Gelu).then_inc(s_h, 1)
            turns.run(act, step)


def kron_down(nc, K, zero, bias, x, GA, GB, prob, H, y):
    with Memory(nc, "down") as m:
        hs = m.sb("hs", [P, 2, 2 * BPT, E64])
        vs = m.sb("vs", [P, 2, 4 * BPT, 32])
        ym = m.sb("ym", [P, 2, BPT, 4, 32])
        ga = m.sb("ga", [P, 2, 2 * BPT, E64])
        gb = m.sb("gb", [P, 2, 4 * BPT, 32])
        pv, py, pr = m.ps("pv", [P, 2, BANK]), m.ps("py", [P, 2, BANK]), m.ps("pr", [P, 2, BANK])
        s_hs, s_pv, s_vs, s_py, s_ym, s_pr, s_y, s_ga, s_gb = (
            m.sem(k) for k in ("hs", "pv", "vs", "py", "ym", "pr", "y", "ga", "gb"))
        block = m.block()
        turns = Turns(3)
        W = 4 * BPT

        @block.gpsimd
        def _(pool):
            def step(s, j):
                if live(s):
                    freed(pool, s_pv, s)
                    nc.gpsimd.tensor_tensor(
                        hs[:, j, :, :].rearrange("p w o -> p (w o)"),
                        H[:, bass.ds(s * BPT, BPT), :, :].rearrange("p b n o -> p (b n o)"),
                        zero[:].to_broadcast([P, 2 * BPT * E64]), ALU.add).then_inc(s_hs, 1)
            turns.run(pool, step)
            for tb in range(TB):
                xs = x[:, tb * 8:(tb + 1) * 8, :]
                nc.gpsimd.tensor_tensor(xs, xs, bias[:].rearrange("p (t o) -> p t o", o=1).to_broadcast([P, 8, N]),
                                        ALU.add).then_inc(s_hs, 1)

        @block.tensor
        def _(pe):
            def step(s, j):
                first, second, third = s, s - 1, s - 3
                i = (j + 1) % 2
                if live(first):
                    pe.wait_ge(s_hs, s + 1)
                    pe.wait_ge(s_ga, s + 1)
                    freed(pe, s_vs, s)
                if live(second):
                    pe.wait_ge(s_vs, second + 1)
                    pe.wait_ge(s_gb, second + 1)
                    freed(pe, s_ym, second)
                if live(third):
                    freed(pe, s_y, third)
                    pe.wait_ge(s_ym, third + 1)
                    for c in range(4):
                        last = nc.tensor.matmul(pr[c * 32:(c + 1) * 32, i, 0:32 * BPT], K["fold"],
                                                ym[:, i, :, :, :].rearrange("p b n (t c) -> p (b n t) c", c=4)[:, :, c],
                                                start=True, stop=True)
                    last.then_inc(s_pr, 1)
                if live(first):
                    for w in range(2 * BPT):
                        for n in range(2):
                            half = slice(E64 * n, E64 * (n + 1))
                            last = nc.tensor.matmul(pv[half, j, w * E64:(w + 1) * E64], hs[half, j, w, :], ga[half, j, w, :],
                                                    start=True, stop=True)
                    last.then_inc(s_pv, 1)
                if live(second):
                    for b in range(BPT):
                        for n in range(2):
                            for q in range(2):
                                half = slice(E64 * q, E64 * (q + 1))
                                at = E64 * n + 32 * q
                                for k in range(2):
                                    w = 4 * b + 2 * n + k
                                    last = nc.tensor.matmul(py[at:at + 32, i, b * 32:(b + 1) * 32], vs[half, i, w, :],
                                                            gb[half, i, w, :], start=(k == 0), stop=(k == 1))
                    last.then_inc(s_py, 1)
            turns.run(pe, step)

        @block.vector
        def _(dve):
            def step(s, j):
                if live(s):
                    dve.wait_ge(s_pv, s + 1)
                    freed(dve, s_py, s)
                    nc.vector.tensor_tensor(
                        vs[:, j, :, :], pv[:, j, :].rearrange("p (w o) -> p w o", w=W),
                        prob[:, bass.ds(s * W, W)].rearrange("p (k o) -> p k o", o=1).to_broadcast([P, W, 32]),
                        ALU.mult).then_inc(s_vs, 1)
                v, i = s - 1, (j + 1) % 2
                if live(v):
                    dve.wait_ge(s_py, v + 1)
                    freed(dve, s_pr, v)
                    nc.vector.tensor_tensor(
                        ym[:, i, :, :, :],
                        py[:, i, 0:32 * BPT].rearrange("p (b o j) -> p b o j", b=BPT, o=1).to_broadcast([P, BPT, 4, 32]),
                        K["mns"].rearrange("p (o c j) -> p o c j", o=1, c=4).to_broadcast([P, BPT, 4, 32]),
                        ALU.mult).then_inc(s_ym, 1)
            turns.run(dve, step)
            dve.wait_ge(s_y, Turns.COUNT)
            dve.wait_ge(s_hs, Turns.COUNT + TB)
            link = K["dve_chain"].on(dve)
            for tb in range(TB):
                v = y[:, tb * BANK:(tb + 1) * BANK].rearrange("p (n t) -> p t n", t=8)
                xs = x[:, tb * 8:(tb + 1) * 8, :]
                link(nc.vector.tensor_tensor(xs, xs, v, ALU.add))

        @block.scalar
        def _(act):
            def step(s, j):
                if live(s):
                    freed(act, s_pv, s)
                    nc.scalar.copy(ga[:, j, :, :].rearrange("p w o -> p (w o)"),
                                   GA[:, bass.ds(s * W, W), :].rearrange("p c o -> p (c o)")).then_inc(s_ga, 1)
                    freed(act, s_py, s)
                    nc.scalar.copy(gb[:, j, :, :].rearrange("p w o -> p (w o)"),
                                   GB[:, bass.ds(s * W, W), :].rearrange("p c o -> p (c o)")).then_inc(s_gb, 1)
                v, i = s - 3, (j + 1) % 2
                if live(v):
                    act.wait_ge(s_pr, v + 1)
                    nc.scalar.copy(y[:, bass.ds(v * 32 * BPT, 32 * BPT)], pr[:, i, 0:32 * BPT]).then_inc(s_y, 1)
            turns.run(act, step)


def kron_moe(nc, x, h, d, S, scratch):
    with Memory(nc, "kron") as m:
        cst = m.sb("cst", [P, 800])
        K = {"ident": S["ident"], "dve_chain": S["dve_chain"], "pr": m.sb("pr", [P, 2, 2]), "pb": m.sb("pb", [P, 4 * BLK]),
             "identb": m.sb("identb", [P, P], BF16)}
        at = 0
        for k, n in (("mq", P), ("mn", P), ("mns", P), ("iota", P), ("fold", 32),
                     ("half4", 2)):
            K[k] = cst[:, at:at + n]
            at += n
        rows = m.sb("rows", [P, TOK])
        H = m.sb("H", [P, BLK, 2, E64])
        GA, GB = m.sb("GA", [P, 2 * BLK, E64]), m.sb("GB", [P, 2 * BLK, E64])
        hotT = m.sb("hotT4", [P, 4, 2 * BLK], BF16)
        hotT2 = m.sb("hotT2", [P, 2, 4 * BLK], BF16)
        prob = m.sb("prob4", [P, 2 * BLK, 2])
        prob2 = m.sb("prob2", [P, 4 * BLK])
        scale_up, scale_down = m.sb("scale_up", [P, 1]), m.sb("scale_down", [P, 1])
        bias_up, bias_down = m.sb("bias_up", [P, BPT * P]), m.sb("bias_down", [P, 8])
        down = [(m.sb(f"hm{i}", [P, 2048], BF16), m.sb(f"lo{i}", [E64, 2048], BF16)) for i in (2, 3)]

        with Memory(nc, "kup") as q:
            up = [(q.sb(f"hm{i}", [P, 2048], BF16), q.sb(f"lo{i}", [E64, 2048], BF16)) for i in (0, 1)]
            K["hm"], K["lo"] = zip(*(up + down))
            wup = q.sb("wup", [P, 8, E64])
            lstm(nc, x, h, d, S, lambda m: split_tables(
                m, d, K, H[:].rearrange("p b q o -> p (b q o)"),
                ((cst[:, 0:at], "k_cst"), (wup[:], "k_wup"),
                 (bias_up[:], "k_bias_up"), (bias_down[:], "k_bias_down"),
                 (scale_up[:], "k_scale_up"), (scale_down[:], "k_scale_down"))))
            kron_start(nc, K, S, h, rows)

            def mats_up(pe, emit):
                for t8 in range(8):
                    last = emit(lambda r: rows[:].rearrange("p (r t) -> p r t", t=8)[:, r * P:(r + 1) * P, t8],
                                wup[:, t8, :], start=(t8 == 0), stop=(t8 == 7))
                return last

            finish = kron_route(nc, "ru", mats_up, d, K, hotT, prob, scratch[0], 4, scale_up)
            kron_gather(nc, "gu", K, (0, 1), hotT, (GA, GB), 4, finish)
        with Memory(nc, "kdn") as q:
            wdown = q.sb("wdown", [P, E64, P])
            kron_up(nc, K, bias_up, rows, GA, GB, prob, H, (wdown[:], d["k_wdown"]))

            def mats_down(pe, emit):
                for o in range(E64):
                    last = emit(wdown[:, o, :], H[:, :, :, o].rearrange("p b n -> p (b n)"), start=(o == 0), stop=(o == E64 - 1))
                return last

            finish = kron_route(nc, "rd", mats_down, d, K, hotT2, prob2, scratch[1], 2, scale_down)
        GAd = GA[:].rearrange("p c o -> p (c o)").rearrange("p (c o) -> p c o", o=32)
        GBd = GB[:].rearrange("p c o -> p (c o)").rearrange("p (c o) -> p c o", o=32)
        kron_gather(nc, "gd", K, (3, 2), hotT2, (GAd, GBd), 2, finish)
        kron_down(nc, K, S["zero"], bias_down, x, GAd, GBd, prob2, H, rows)


def kron_start(nc, K, S, h, rows):
    with Memory(nc, "kstart") as q:
        block = q.block()

        @block.vector
        def _(dve):
            nc.vector.tensor_copy(K["identb"][:], S["ident"][:])
            for tb in range(TB):
                nc.vector.tensor_copy(rows[:, tb * BANK:(tb + 1) * BANK].rearrange("p (n t) -> p t n", t=8),
                                      h[:, 1 + tb * 8:1 + (tb + 1) * 8, :])


def gated_scan(nc, x, hid, d, S):
    C = TILE // T
    with Memory(nc, "scan") as m:
        w, b = m.sb("w", [P, 3, P]), m.sb("b", [P, 3])
        keep = m.sb("keep", [P, C, T])
        eps = m.sb("eps", [P, 1])
        f, i_, cand, r, log, till, grown = (m.sb(k, [P, N, T]) for k in ("f", "i", "cand", "r", "log", "till", "grown"))
        pre = m.ps("pre", [P, 3, 2, BANK])
        s_w, s_keep, s_pre, s_act, s_ratio, s_info, s_log, s_scan, s_till, s_exp = (
            m.sem(k) for k in ("w", "keep", "pre", "act", "ratio", "info", "log", "scan", "till", "exp"))
        block = m.block()
        tile_of = lambda a, k: a[:, k * C:(k + 1) * C, :]
        flat = lambda a, k: tile_of(a, k).rearrange("p n t -> p (n t)")

        @block.sync
        def _(sp):
            sp.dma_start(w[:], d["l2_w"]).then_inc(s_w, 16)
            sp.dma_start(b[:], d["l2_b"]).then_inc(s_w, 16)

        @block.tensor
        def _(pe):
            pe.wait_ge(s_w, 32)
            for tile in range(NT):
                if tile >= 2:
                    pe.wait_ge(s_act, 3 * (tile - 1))
                for k in range(3):
                    nc.tensor.matmul(pre[:, k, tile % 2, :], w[:, k, :],
                                     x[:].rearrange("p t n -> p n t")[:, tile * C:(tile + 1) * C, :],
                                     start=True, stop=True).then_inc(s_pre, 1)

        @block.scalar
        def _(act):
            act.wait_ge(s_w, 32)
            for tile in range(NT):
                for k, (dst, fn) in enumerate(((f, ACT.Sigmoid), (i_, ACT.Sigmoid), (cand, ACT.Identity))):
                    act.wait_ge(s_pre, 3 * tile + k + 1)
                    nc.scalar.activation(flat(dst, tile), pre[:, k, tile % 2, :], fn, bias=b[:, k:k + 1]).then_inc(s_act, 1)
            act.wait_ge(s_keep, 3)
            for tile in range(NT):
                act.wait_ge(s_ratio, 2 * tile + 2)
                nc.scalar.activation(flat(f, tile), flat(f, tile), ACT.Ln, bias=eps[:]).then_inc(s_log, 1)
            for tile in range(NT):
                act.wait_ge(s_scan, tile + 1)
                nc.scalar.activation(flat(grown, tile), flat(log, tile), ACT.Exp).then_inc(s_exp, 1)
                act.wait_ge(s_till, 2 * tile + 2)
                nc.scalar.activation(flat(till, tile), flat(till, tile), ACT.Exp).then_inc(s_exp, 1)

        @block.gpsimd
        def _(pool):
            pool.memset(keep[:], 1.0).then_inc(s_keep, 1)
            pool.wait_ge(s_keep, 1)
            pool.memset(keep[:, :, 0:1], 0.0).then_inc(s_keep, 1)
            pool.memset(eps[:], 1e-8).then_inc(s_keep, 1)
            for tile in range(NT):
                pool.wait_ge(s_ratio, 2 * tile + 1)
                nc.gpsimd.tensor_tensor(flat(i_, tile), flat(i_, tile), flat(r, tile), ALU.mult).then_inc(s_info, 1)
                pool.wait_ge(s_info, 2 * tile + 1)
                pool.wait_ge(s_act, 3 * tile + 3)
                nc.gpsimd.tensor_tensor(flat(cand, tile), flat(cand, tile), flat(i_, tile), ALU.mult).then_inc(s_info, 1)
            for tile in range(NT):
                pool.wait_ge(s_scan, tile + 1)
                last = tile_of(log, tile)[:, :, T - 1:T]
                nc.gpsimd.tensor_copy(tile_of(till, tile)[:, :, 0:1], last).then_inc(s_till, 1)
                nc.gpsimd.tensor_tensor(tile_of(till, tile)[:, :, 1:T], last.to_broadcast([P, C, T - 1]),
                                        tile_of(log, tile)[:, :, 0:T - 1], ALU.subtract).then_inc(s_till, 1)
            for tile in range(NT):
                pool.wait_ge(s_exp, 2 * tile + 1)
                nc.gpsimd.tensor_tensor(tile_of(grown, tile), tile_of(grown, tile), S["cond"][:, tile * C:(tile + 1) * C]
                                        .rearrange("p (n o) -> p n o", o=1).to_broadcast([P, C, T]), ALU.mult).then_inc(s_till, 1)

        @block.vector
        def _(dve):
            link = S["dve_chain"].on(dve)
            for tile in range(NT):
                dve.wait_ge(s_act, 3 * tile + 2)
                link(nc.vector.scalar_tensor_tensor(flat(r, tile), flat(f, tile), 1e-8, flat(i_, tile), ALU.add, ALU.add))
                nc.vector.reciprocal(flat(r, tile), flat(r, tile)).then_inc(s_ratio, 1)
                dve.wait_ge(s_ratio, 2 * tile + 1)
                nc.vector.tensor_tensor(flat(f, tile), flat(f, tile), flat(r, tile), ALU.mult).then_inc(s_ratio, 1)
            dve.wait_ge(s_keep, 2)
            flat_keep = keep[:].rearrange("p n t -> p (n t)")
            for tile in range(NT):
                dve.wait_ge(s_log, tile + 1)
                nc.vector.tensor_tensor_scan(flat(log, tile), flat_keep, flat(f, tile), 0.0, ALU.mult, ALU.add).then_inc(s_scan, 1)
            for tile in range(NT):
                dve.wait_ge(s_info, 2 * tile + 2)
                dve.wait_ge(s_exp, 2 * tile + 2)
                link(nc.vector.tensor_tensor(flat(cand, tile), flat(cand, tile), flat(till, tile), ALU.mult))
                link(nc.vector.tensor_tensor_scan(flat(r, tile), flat_keep, flat(cand, tile), 0.0, ALU.mult, ALU.add))
                dve.wait_ge(s_till, 2 * NT + tile + 1)
                nc.vector.tensor_tensor(tile_of(hid, tile), tile_of(grown, tile), tile_of(r, tile), ALU.add)


def gru(nc, x, h, d, S):
    ZRC = ((1,), (0,), (2,))
    with Memory(nc, "gru") as m:
        w, u, cv, b = m.sb("w", [P, 3, P]), m.sb("u", [P, 3, P]), m.sb("cv", [P, 3, P]), m.sb("b", [P, 3])
        vid = m.sb("vid", [P, 3, N])
        z, keep, r, rh, hh, kept, new = (m.sb(k, [P, N]) for k in ("z", "keep", "r", "rh", "hh", "kept", "new"))
        warm, state, xs = m.sb("warm", [P, 3]), m.sb("state", [P, 2, N]), m.sb("xs", [P, 2, 3, N])
        inputs = m.sb("inputs", [P, T, 3, N])
        pre = m.ps("pre", [P, 2, 3, BANK])
        BANKS = 6
        bank = lambda n: pre[:, n % BANKS // 3, n % 3, :]
        s_w, s_v, s_vid, s_x, s_pre, s_gate, s_rh, s_hh, s_own, s_h = (
            m.sem(k) for k in ("w", "v", "vid", "x", "pre", "gate", "rh", "hh", "own", "h"))
        block = m.block()

        @block.sync
        def _(sp):
            for dst, src in ((w, "l3_w"), (u, "l3_u"), (cv, "l3_c"), (b, "l3_b")):
                sp.dma_start(dst[:], d[src]).then_inc(s_w, 16)

        @block.tensor
        def _(pe):
            pe.wait_ge(s_w, 64)
            for k in range(3):
                nc.tensor.matmul(pre[:, 1, 2, k * N:(k + 1) * N], cv[:, k, :], S["cond"][:], start=True, stop=True).then_inc(s_v, 1)
            for n in range(3 * NT):
                if n >= BANKS - 1:
                    pe.wait_ge(s_vid, 3 + max(n - BANKS + 1, 0))
                nc.tensor.matmul(bank(n), w[:, n % 3, :], x[:].rearrange("p t n -> p (t n)")[:, n // 3 * TILE:(n // 3 + 1) * TILE],
                                 start=True, stop=True).then_inc(s_v, 1)
            pe.wait_ge(s_vid, 3 + 3 * NT)

            def input_part(t, j, banks):
                for bank in banks:
                    halves_product(nc, pre[:, j, bank, 0:N], S["ident"], xs[:, j, ZRC[bank][0], :], True, False)

            def gate_part(j):
                for bank in range(2):
                    halves_product(nc, pre[:, j, bank, 0:N], u[:, ZRC[bank][0], :], state[:, j, :], False, True).then_inc(s_pre, 1)

            pe.wait_ge(s_x, 1)
            input_part(0, 0, range(3))
            pe.wait_ge(s_h, 1)
            gate_part(0)

            def step(t, j, more):
                if more or j == 0:
                    pe.wait_ge(s_x, t + 2)
                    input_part(t + 1, 1 - j, (0,))
                pe.wait_ge(s_rh, t + 1)
                halves_product(nc, pre[:, j, 2, 0:N], u[:, 2, :], rh[:], False, True).then_inc(s_pre, 1)
                if more or j == 0:
                    input_part(t + 1, 1 - j, (1, 2))
                    pe.wait_ge(s_h, t + 2)
                    gate_part(1 - j)
            over_steps(pe, step)

        @block.scalar
        def _(act):
            act.wait_ge(s_w, 64)
            nc.scalar.activation(warm[:], b[:], ACT.Sigmoid)

            def step(t, j, more):
                act.wait_ge(s_pre, t * 3 + 1)
                nc.scalar.activation(r[:], pre[:, j, 0, 0:N], ACT.Sigmoid).then_inc(s_gate, 1)
                act.wait_ge(s_pre, t * 3 + 2)
                nc.scalar.activation(keep[:], pre[:, j, 1, 0:N], ACT.Sigmoid, scale=-1.0).then_inc(s_gate, 1)
                nc.scalar.activation(z[:], pre[:, j, 1, 0:N], ACT.Sigmoid).then_inc(s_gate, 1)
                act.wait_ge(s_pre, t * 3 + 3)
                nc.scalar.activation(hh[:], pre[:, j, 2, 0:N], ACT.Tanh).then_inc(s_hh, 1)
            over_steps(act, step)

        @block.vector
        def _(dve):
            nc.vector.memset(state[:, 0, :], 0.0).then_inc(s_h, 1)
            dve.wait_ge(s_w, 64)
            dve.wait_ge(s_v, 3)
            for k in range(3):
                nc.vector.tensor_scalar(vid[:, k, :], pre[:, 1, 2, k * N:(k + 1) * N], b[:, k:k + 1], None, ALU.add).then_inc(s_vid, 1)
            dve.wait_ge(s_vid, 3)
            for n in range(3 * NT):
                k, tile = n % 3, n // 3
                dve.wait_ge(s_v, 3 + n + 1)
                nc.vector.tensor_tensor(inputs[:, tile * 8:(tile + 1) * 8, k, :], bank(n).rearrange("p (t n) -> p t n", n=N),
                                        vid[:, k, :].rearrange("p (o n) -> p o n", o=1).to_broadcast([P, 8, N]),
                                        ALU.add).then_inc(s_vid, 1)
            dve.wait_ge(s_vid, 3 + 3 * NT)
            for t in range(2):
                nc.vector.tensor_copy(xs[:, t, :, :], inputs[:, t, :, :]).then_inc(s_x, 1)
            dve.wait_ge(s_h, 1)

            def step(t, j, more):
                dve.wait_ge(s_gate, t * 3 + 1)
                nc.vector.tensor_tensor(rh[:], r[:], state[:, j, :], ALU.mult).then_inc(s_rh, 1)
                dve.wait_ge(s_gate, t * 3 + 2)
                nc.vector.tensor_tensor(kept[:], keep[:], state[:, j, :], ALU.mult).then_inc(s_own, 1)
                dve.wait_ge(s_gate, t * 3 + 3)
                dve.wait_ge(s_hh, t + 1)
                nc.vector.tensor_tensor(new[:], z[:], hh[:], ALU.mult).then_inc(s_own, 1)
                dve.wait_ge(s_own, t * 2 + 2)
                nc.vector.tensor_tensor(state[:, 1 - j, :], new[:], kept[:], ALU.add).then_inc(s_h, 1)
                if more:
                    nc.vector.tensor_copy(xs[:, j, :, :], inputs[:, t + 2, :, :]).then_inc(s_x, 1)
                dve.wait_ge(s_h, t + 2)
                nc.vector.tensor_copy(h[:, t + 1, :], state[:, 1 - j, :])
            over_steps(dve, step)


def router(m, tag, tokens, d, S, gates_dram, mode, EG, logits, gT, rows, s_w, loads):
    E = 8
    nc = m.nc
    w, code = m.sb("router_w", [P, E]), S["code"]
    bias = m.sb("router_bias", [P, E])
    v = {k: m.sb(k, [P, G, E]) for k in ("score", "value", "eq", "one", "two", "tmp")}
    red = {k: m.sb(k, [P, G]) for k in ("mx", "sum", "rec")}
    gates = m.sb("gates", [P, G, EG])
    GT = min(G, P // EG // 8 * 8)
    NTR = G // GT
    turned = m.sb("turned", [GT * EG, NTR, P])
    s_logits, s_gates, s_gT, s_rows, s_out = (m.sem(k) for k in ("logits", "gates", "gT", "rows", "out"))
    s_in, s_exp = (m.sem("in"), m.sem("exp")) if mode != "argmax" else (None, None)
    wide = lambda a: a[:].rearrange("p (g o) -> p g o", o=1).to_broadcast([P, G, E])
    per = lambda a: a[:].rearrange("p (o e) -> p o e", o=1).to_broadcast([P, G, E])

    def load(sp):
        sp.dma_start(w[:], d[f"{tag}_w"]).then_inc(s_w, 16)
        if mode == "sigmoid":
            sp.dma_start(bias[:], d[f"{tag}_bias"]).then_inc(s_w, 16)

    def write_rows(sp):
        for n in range(NTR):
            sp.wait_ge(s_rows, n + 1)
            sp.dma_start(gates_dram.rearrange("e (n g t) -> n g e t", n=NTR, t=P)[n], turned[:, n, :]).then_inc(s_out, 16)
        sp.wait_ge(s_out, 16 * NTR)
        if rows is not None:
            sp.dma_start(rows[:], gates_dram).then_inc(s_out, 16)

    def wait_rows(pe):
        pe.wait_ge(s_out, 16 * NTR + 16)

    def tensor(pe, meanwhile):
        pe.wait_ge(s_w, 16 * loads)
        for g in range(G):
            for n in range(4):
                part = slice(32 * n, 32 * (n + 1))
                last = nc.tensor.matmul(logits[part, g * E:(g + 1) * E], tokens(g)[:, part], w[:], start=True, stop=True)
        last.then_inc(s_logits, 1)
        meanwhile()
        pe.wait_ge(s_gates, 1)
        for n in range(NTR):
            nc.tensor.transpose(gT[0:GT * EG, n, 0:P], gates[:, n * GT:(n + 1) * GT, :].rearrange("p g e -> p (g e)"),
                                S["ident"][:]).then_inc(s_gT, 1)
        pe.wait_ge(s_rows, NTR)

    def scalar(act):
        if mode == "softmax":
            act.wait_ge(s_in, 1)
            nc.scalar.activation(v["value"][:], v["value"][:], ACT.Exp).then_inc(s_exp, 1)
        if mode == "sigmoid":
            act.wait_ge(s_in, 1)
            nc.scalar.activation(v["value"][:], v["value"][:], ACT.Sigmoid).then_inc(s_exp, 1)
        for n in range(NTR):
            act.wait_ge(s_gT, n + 1)
            nc.scalar.activation(turned[:, n, :], gT[0:GT * EG, n, 0:P], ACT.Copy).then_inc(s_rows, 1)

    def vector(dve):
        link = S["dve_chain"].on(dve)
        tt = nc.vector.tensor_tensor
        lg = logits[:].rearrange("p (g e) -> p g e", e=E)
        value, score, eq, tmp = v["value"], v["score"], v["eq"], v["tmp"]

        def pick(one, src):
            link(nc.vector.tensor_reduce(red["mx"][:], src, AX, ALU.max))
            link(tt(eq[:], src, wide(red["mx"]), ALU.is_ge))
            link(tt(eq[:], eq[:], per(code), ALU.mult))
            link(nc.vector.tensor_reduce(red["mx"][:], eq[:], AX, ALU.max))
            link(tt(one[:], eq[:], wide(red["mx"]), ALU.is_equal))

        dve.wait_ge(s_logits, 1)
        if mode == "softmax":
            link(nc.vector.tensor_reduce(red["mx"][:], lg, AX, ALU.max))
            tt(value[:], lg, wide(red["mx"]), ALU.subtract).then_inc(s_in, 1)
            dve.wait_ge(s_exp, 1)
            link(nc.vector.tensor_reduce(red["sum"][:], value[:], AX, ALU.add))
            link(nc.vector.reciprocal(red["rec"][:], red["sum"][:]))
            link(tt(value[:], value[:], wide(red["rec"]), ALU.mult))
            link(nc.vector.tensor_copy(score[:], value[:]))
        elif mode == "sigmoid":
            nc.vector.tensor_copy(value[:], lg).then_inc(s_in, 1)
            dve.wait_ge(s_exp, 1)
            link(tt(score[:], value[:], per(bias), ALU.add))
        else:
            link(nc.vector.tensor_copy(score[:], lg))
        pick(v["one"], score[:])
        out = gates[:, :, 0:E]
        if mode != "argmax":
            link(nc.vector.scalar_tensor_tensor(tmp[:], v["one"][:], -1e30, score[:], ALU.mult, ALU.add))
            pick(v["two"], tmp[:])
            link(tt(v["one"][:], v["one"][:], v["two"][:], ALU.add))
        if mode == "argmax":
            last = nc.vector.tensor_copy(out, v["one"][:])
        elif mode == "softmax":
            last = tt(out, v["one"][:], value[:], ALU.mult)
        else:
            link(tt(value[:], v["one"][:], value[:], ALU.mult))
            link(nc.vector.tensor_reduce(red["sum"][:], value[:], AX, ALU.add))
            link(nc.vector.tensor_scalar(red["mx"][:], red["sum"][:], 1e-9, None, ALU.is_gt))
            link(nc.vector.tensor_scalar(red["sum"][:], red["sum"][:], 1e-9, None, ALU.add))
            link(nc.vector.reciprocal(red["rec"][:], red["sum"][:]))
            link(tt(value[:], value[:], wide(red["rec"]), ALU.mult))
            link(nc.vector.tensor_scalar(v["two"][:], v["one"][:], 0.5, None, ALU.mult))
            link(tt(value[:], value[:], v["two"][:], ALU.subtract))
            link(tt(value[:], value[:], wide(red["mx"]), ALU.mult))
            last = tt(out, value[:], v["two"][:], ALU.add)
        if EG > E:
            link(last)
            last = nc.vector.memset(gates[:, :, E:EG], 1.0)
        last.then_inc(s_gates, 1)

    return load, write_rows, wait_rows, tensor, scalar, vector


def experts(nc, tag, tokens, resid, result, d, S, gates_dram, *, route, E, chunks, kind, act_fn, wcols,
            shared=None, bufs=2, out_view=lambda a: a, out=None):
    glu = kind == "glu"
    NCH = len(chunks)
    F = sum(w for _, w in chunks)
    DOWN = F * (2 if glu else 1)
    WMM = DOWN + NCH * P
    U = NT * NCH
    NB = NT
    SKEW = 3 if glu else 4
    with Memory(nc, tag) as m:
        w = [m.sb(f"w{i}", [P, wcols]) for i in range(bufs)]
        whi, wlo = ([m.sb(f"{k}{i}", [P, WMM], F32R) for i in range(bufs)] for k in ("whi", "wlo"))
        gate = [m.sb(f"gate{i}", [P, TOK]) for i in range(bufs)]
        thi, tlo = m.sb("thi", [P, NT, TILE], F32R), m.sb("tlo", [P, NT, TILE], F32R)
        if glu:
            xhi, xlo = m.sb("xhi", [P, bufs, NT, TILE], F32R), m.sb("xlo", [P, bufs, NT, TILE], F32R)
        a = m.sb("a", [P, NB, TILE])
        hb = m.sb("h", [P, NB, TILE])
        hhi, hlo = m.sb("hhi", [P, NB, TILE], F32R), m.sb("hlo", [P, NB, TILE], F32R)
        if shared:
            sw = m.sb("sw", [P, shared["cols"]])
            swhi, swlo = m.sb("swhi", [P, shared["cols"]], F32R), m.sb("swlo", [P, shared["cols"]], F32R)
        b2 = m.sb("b2", [E, P]) if result == "scaled" else None
        warm = m.sb("warm", [P, 1])
        acc = m.ps("acc", [P, NT, BANK])
        up = m.ps("up", [P, 4, BANK])
        router_tag, mode, groups = route
        rows = m.sb("gate_rows", [E, TOK]) if b2 is not None else None
        s_param = m.sem("param")
        loads = 1 + (mode == "sigmoid") + (b2 is not None) + bool(shared)
        load_router, write_rows, wait_rows, route_pe, route_act, route_dve = router(
            m, router_tag, groups, d, S, gates_dram[0:E, 0, :], mode, E, acc[:, 0, 0:G * 8], acc, rows, s_param, loads)
        s_up, s_act, s_mul, s_high, s_hid, s_down, s_whi, s_wsplit, s_xsplit = (
            m.sem(k) for k in ("up", "act", "mul", "high", "hid", "down", "whi", "wsplit", "xsplit"))
        s_swsplit = m.sem("swsplit") if shared else None
        s_masked = m.sem("masked") if glu else None
        s_result, s_out = (m.sem("result"), m.sem("stored")) if out is not None else (None, None)
        s_w = [m.sem(f"w{i}") for i in range(bufs)]
        s_gate = [m.sem(f"gate{i}") for i in range(bufs)]
        SH = shared["units"] if shared else 0
        TURNS = (E - 1) // bufs if E > 2 * bufs else 0
        UPB = 2 if glu or shared else 4
        block = m.block()

        def expert_list(run):
            def body(eng):
                if TURNS:
                    with eng.Fori(0, TURNS) as i:
                        for j in range(bufs):
                            run(SH + (i * bufs + j) * U, i, j, False)
                for e in range(bufs * TURNS, E):
                    run(SH + e * U, e // bufs, e % bufs, e == E - 1)
            return body

        def ahead(step, lead, base, i, j, is_last, u):
            v = u + lead
            if v < U:
                step(base, i, j, v)
            elif not is_last:
                step(base + U, *((i, j + 1) if j + 1 < bufs else (i + 1, 0)), v - U)

        @block.sync
        def _(sp):
            load_router(sp)
            if shared:
                sp.dma_start(sw[:], d[f"{tag}_sw"]).then_inc(s_param, 16)
            if b2 is not None:
                sp.dma_start(b2[:], d[f"{tag}_b2"]).then_inc(s_param, 16)

            def fetch(e, j):
                sp.dma_start(w[j][:], d[f"{tag}_wp"][e, :, :]).then_inc(s_w[j], 16)

            def fetch_gate(e, j):
                sp.dma_start(gate[j][:], gates_dram[e, :, :].to_broadcast([P, TOK])).then_inc(s_gate[j], 16)

            for j in range(bufs):
                fetch(j, j)
            write_rows(sp)
            for j in range(bufs):
                fetch_gate(j, j)
            if TURNS > 1:
                with sp.Fori(1, TURNS) as i:
                    for j in range(bufs):
                        sp.wait_ge(s_down, NT + SH + ((i - 1) * bufs + j + 1) * U)
                        fetch(i * bufs + j, j)
                        fetch_gate(i * bufs + j, j)
            for e in range(bufs * max(TURNS, 1), E):
                sp.wait_ge(s_down, NT + SH + (e - bufs + 1) * U)
                fetch(e, e % bufs)
                fetch_gate(e, e % bufs)
            if out is not None:
                for k in range(NT):
                    sp.wait_ge(s_result, k + 1)
                    sp.dma_start(out(k), result(k)).then_inc(s_out, 16)
                sp.wait_ge(s_out, 16 * NT)

        @block.gpsimd
        def _(pool):
            if shared:
                pool.wait_ge(s_param, 16 * loads)
                nc.gpsimd.tensor_copy(swhi[:], sw[:]).then_inc(s_swsplit, 1)
                pool.wait_ge(s_swsplit, 1)
                nc.gpsimd.tensor_tensor(swlo[:], sw[:], swhi[:].bitcast(F32), ALU.subtract).then_inc(s_swsplit, 1)
            if glu:
                pool.wait_ge(s_xsplit, NT + 1)

            def run(base, i, j, is_last):
                n = i * bufs + j
                pool.wait_ge(s_w[j], (i + 1) * 16)
                nc.gpsimd.tensor_tensor(whi[j][:], w[j][:, 0:WMM], S["zero"][:].to_broadcast([P, WMM]), ALU.add).then_inc(s_whi, 1)
                pool.wait_ge(s_whi, n + 1)
                nc.gpsimd.tensor_tensor(wlo[j][:], w[j][:, 0:WMM], whi[j][:].bitcast(F32), ALU.subtract).then_inc(s_wsplit, 1)
                if glu:
                    pool.wait_ge(s_gate[j], (i + 1) * 16)
                    for tile in range(NT):
                        for dst, src in ((xhi, thi), (xlo, tlo)):
                            nc.gpsimd.tensor_tensor(dst[:, j, tile, :], src[:, tile, :].bitcast(F32),
                                                    gate[j][:, tile * TILE:(tile + 1) * TILE], ALU.mult).then_inc(s_masked, 1)
            expert_list(run)(pool)

        @block.tensor
        def _(pe):
            def product(out, left, right, start, stop):
                nc.tensor.matmul(out, left[0], right[0], start=start, stop=False)
                nc.tensor.matmul(out, left[0], right[1], start=False, stop=False)
                return nc.tensor.matmul(out, left[1], right[0], start=False, stop=stop)

            H = shared["nch"] * P if shared else 0

            def shared_up(u):
                tile, c = u // shared["nch"], u % shared["nch"]
                if u >= 2:
                    pe.wait_ge(s_mul, u - 1)
                for bank, col in ((u % 2, c * P), (2 + u % 2, H + c * P)):
                    last = product(up[:, bank, :], (swhi[:, col:col + P], swlo[:, col:col + P]),
                                   (thi[:, tile, :], tlo[:, tile, :]), True, True)
                last.then_inc(s_up, 1)

            def before_gates():
                if not glu:
                    pe.wait_ge(s_xsplit, NT + 1)
                if shared:
                    pe.wait_ge(s_swsplit, 2)
                    for u in range(2):
                        shared_up(u)
                elif not glu:
                    for u in range(SKEW):
                        up_step(SH, 0, 0, u)

            def up_step(base, i, j, u):
                tile, c = u // NCH, u % NCH
                f0, fw = chunks[c]
                if u == 0:
                    pe.wait_ge(s_wsplit, i * bufs + j + 1)
                if UPB <= SKEW and not (isinstance(base, int) and base == SH and u < UPB):
                    pe.wait_ge(s_mul if glu else s_act, base + u - UPB + 1)
                if glu:
                    if c == 0:
                        pe.wait_ge(s_masked, ((i * bufs + j) * NT + tile + 1) * 2)
                    rhs = (xhi[:, j, tile, :], xlo[:, j, tile, :])
                    product(up[0:fw, u % 2, :], (whi[j][:, f0:f0 + fw], wlo[j][:, f0:f0 + fw]), rhs, True, True)
                    last = product(up[0:fw, 2 + u % 2, :], (whi[j][:, F + f0:F + f0 + fw], wlo[j][:, F + f0:F + f0 + fw]),
                                   rhs, True, True)
                else:
                    last = product(up[0:fw, u % UPB, :], (whi[j][:, f0:f0 + fw], wlo[j][:, f0:f0 + fw]),
                                   (thi[:, tile, :], tlo[:, tile, :]), True, True)
                last.then_inc(s_up, 1)

            def run(base, i, j, is_last):
                for u in range(U):
                    ahead(up_step, SKEW, base, i, j, is_last, u)
                    tile, c = u // NCH, u % NCH
                    fw, col = chunks[c][1], DOWN + c * P
                    pe.wait_ge(s_hid, base + u + 1)
                    product(acc[:, tile, :], (whi[j][0:fw, col:col + P], wlo[j][0:fw, col:col + P]),
                            (hhi[0:fw, u % NB, :], hlo[0:fw, u % NB, :]), False,
                            is_last and c == NCH - 1).then_inc(s_down, 1)
            route_pe(pe, before_gates)
            if b2 is not None:
                wait_rows(pe)
            for k in range(NT):
                if b2 is not None:
                    start = nc.tensor.matmul(acc[:, k, :], b2[:], rows[:, k * TILE:(k + 1) * TILE], start=True, stop=False)
                else:
                    start = nc.tensor.matmul(acc[:, k, :], S["ident"][:], resid(k), start=True, stop=False)
                start.then_inc(s_down, 1)
            if shared:
                for u in range(SH + SKEW):
                    if 2 <= u < SH:
                        shared_up(u)
                    if u >= SKEW:
                        v = u - SKEW
                        tile, c = v // shared["nch"], v % shared["nch"]
                        col = 2 * H + c * P
                        pe.wait_ge(s_hid, v + 1)
                        product(acc[:, tile, :], (swhi[:, col:col + P], swlo[:, col:col + P]),
                                (hhi[:, v % NB, :], hlo[:, v % NB, :]), False, False).then_inc(s_down, 1)
            if glu or shared:
                for u in range(SKEW):
                    up_step(SH, 0, 0, u)
            expert_list(run)(pe)

        @block.scalar
        def _(act):
            route_act(act)

            def high(n, b, fw):
                act.wait_ge(s_down, NT + n - NB + 1)
                act.wait_ge(s_mul, n + 1)
                nc.scalar.copy(hhi[0:fw, b, :], hb[0:fw, b, :]).then_inc(s_high, 1)

            if shared:
                nc.scalar.activation(warm[:], S["ident"][:, 0:1], ACT.Silu)
                for u in range(SH + 1):
                    if u < SH:
                        act.wait_ge(s_up, u + 1)
                        if u >= NB:
                            act.wait_ge(s_mul, u - NB + 1)
                        nc.scalar.activation(a[:, u % NB, :], up[:, u % 2, :], ACT.Silu).then_inc(s_act, 1)
                    if u >= 1:
                        high(u - 1, (u - 1) % NB, P)
            nc.scalar.activation(warm[:], S["ident"][:, 0:1], act_fn)

            def act_step(base, i, j, u):
                if u == 0 and not glu:
                    act.wait_ge(s_w[j], (i + 1) * 16)
                fw = chunks[u % NCH][1]
                act.wait_ge(s_up, base + u + 1)
                bias = 0.0
                if kind == "gelu" and wcols > WMM:
                    bias = w[j][0:fw, WMM + u % NCH:WMM + u % NCH + 1]
                nc.scalar.activation(a[0:fw, u % NB, :], up[0:fw, u % UPB, :], act_fn, bias=bias).then_inc(s_act, 1)

            def run(base, i, j, is_last):
                for u in range(U):
                    ahead(act_step, 1, base, i, j, is_last, u)
                    high(base + u, u % NB, chunks[u % NCH][1])
            act_step(SH, 0, 0, 0)
            expert_list(run)(act)

        @block.vector
        def _(dve):
            def low(n, b, fw):
                dve.wait_ge(s_high, n + 1)
                nc.vector.tensor_tensor(hlo[0:fw, b, :], hb[0:fw, b, :], hhi[0:fw, b, :].bitcast(F32),
                                        ALU.subtract).then_inc(s_hid, 1)

            for k in range(NT):
                nc.vector.tensor_copy(thi[:, k, :], tokens(k)).then_inc(s_xsplit, 1)
            dve.wait_ge(s_xsplit, NT)
            for k in range(NT):
                last = nc.vector.tensor_tensor(tlo[:, k, :], tokens(k), thi[:, k, :].bitcast(F32), ALU.subtract)
            last.then_inc(s_xsplit, 1)
            route_dve(dve)
            if shared:
                for u in range(SH + 1):
                    if u < SH:
                        dve.wait_ge(s_act, u + 1)
                        nc.vector.tensor_tensor(hb[:, u % NB, :], up[:, 2 + u % 2, :], a[:, u % NB, :], ALU.mult).then_inc(s_mul, 1)
                    if u >= 1:
                        low(u - 1, (u - 1) % NB, P)

            def mul_step(base, i, j, u):
                if u == 0 and not glu:
                    dve.wait_ge(s_gate[j], (i + 1) * 16)
                tile, fw = u // NCH, chunks[u % NCH][1]
                dve.wait_ge(s_act, base + u + 1)
                other = up[0:fw, 2 + u % 2, :] if glu else gate[j][0:fw, tile * TILE:(tile + 1) * TILE]
                nc.vector.tensor_tensor(hb[0:fw, u % NB, :], a[0:fw, u % NB, :], other, ALU.mult).then_inc(s_mul, 1)

            def run(base, i, j, is_last):
                for u in range(U):
                    ahead(mul_step, 1, base, i, j, is_last, u)
                    low(base + u, u % NB, chunks[u % NCH][1])
            mul_step(SH, 0, 0, 0)
            expert_list(run)(dve)
            for k in range(NT):
                dve.wait_ge(s_down, NT + SH + (E - 1) * U + (k + 1) * NCH)
                if result == "scaled":
                    last = nc.vector.scalar_tensor_tensor(resid(k), acc[:, k, :], L0_SCALE, resid(k), ALU.mult, ALU.add)
                else:
                    last = nc.vector.tensor_copy(result(k), out_view(acc[:, k, :]))
                if out is not None:
                    last.then_inc(s_result, 1)


LAYERS = [0, 1, 2, 3]


def build(nc, d, out, scratch, probs_up, probs_down, layers):
    with ExitStack() as x_ctx, ExitStack() as Memory.semaphores:
        sb = lambda name, shape: x_ctx.enter_context(nc.sbuf_tensor(name, shape, F32))
        x = sb("x", [P, T, N])
        h = sb("h", [P, T + 1, N])
        S = {"cond": sb("cond", [P, N]), "ident": sb("ident", [P, P]), "zero": sb("zero", [P, 1]), "code": sb("code", [P, 8])}
        S["dve_chain"] = Chain(Memory.semaphores.enter_context(nc.semaphore("dve_chain")))
        load_state(nc, x, d, S)
        xf = x[:].rearrange("p t n -> p (t n)")
        hf = h[:, 1:, :].rearrange("p t n -> p (t n)")
        x_tile = lambda k: xf[:, k * TILE:(k + 1) * TILE]
        h_tile = lambda k: hf[:, k * TILE:(k + 1) * TILE]
        h_group = lambda g: hf[:, g * P:(g + 1) * P]
        if 0 in layers:
            rnn(nc, x, h, d, S)
            experts(nc, "e0", h_tile, x_tile, "scaled", d, S, scratch, route=("r0", "softmax", h_group), E=9,
                    chunks=[(c * P, P) for c in range(4)], kind="gelu", act_fn=ACT.Gelu_apprx_tanh, wcols=8 * P + 4)
        if 1 in layers:
            kron_moe(nc, x, h, d, S, (probs_up, probs_down))
        if 2 in layers:
            hid = h[:, 1:, :].rearrange("p t n -> p (t n)").rearrange("p (n t) -> p n t", n=N)
            gated_scan(nc, x, hid, d, S)
            C = TILE // T
            xn = lambda k: x[:].rearrange("p t n -> p n t")[:, k * C:(k + 1) * C, :]
            experts(nc, "e2", h_tile, xn, xn, d, S, scratch, route=("r2", "argmax", h_group), E=8,
                    chunks=[(0, 128), (128, 128), (256, 96)], kind="glu", act_fn=ACT.Silu, wcols=2 * 352 + 3 * P,
                    out_view=lambda a: a.rearrange("p (n t) -> p n t", t=T))
        if 3 in layers:
            gru(nc, x, h, d, S)
            experts(nc, "e3", h_tile, x_tile, x_tile, d, S, scratch, route=("r3", "sigmoid", h_group), E=8, chunks=[(0, 128)], kind="gelu",
                    act_fn=ACT.Gelu, wcols=2 * P, shared={"cols": 3 * 2 * P, "nch": 2, "units": 2 * NT}, bufs=4,
                    out=lambda k: out.rearrange("p t n -> p (t n)")[:, k * TILE:(k + 1) * TILE])
        else:
            store_state(nc, x, out)


def lay_out(i):
    t = lambda a, *axes: np.ascontiguousarray(np.transpose(a, axes))
    cat, pad = np.concatenate, np.pad
    col = lambda *bs: np.ascontiguousarray(np.stack(bs, 1))
    a = {"xT": t(i["x"], 2, 1, 0), "condT": t(i["cond_1024"], 1, 0)}
    a["l0_wx"], a["l0_wh"], a["l0_b"] = i["L0_cond_Wx"], i["L0_cond_Wh"], i["L0_cond_b"][:, None]
    a["r0_w"] = t(i["L0_ffn_w_router"], 1, 0)
    w1 = t(cat([i["L0_ffn_W1"], i["L0_ffn_Ws1"][None]]), 0, 2, 1)
    w2 = cat([i["L0_ffn_W2"], i["L0_ffn_Ws2"][None]]).reshape(9, P, 4, P).transpose(0, 3, 2, 1).reshape(9, P, 4 * P)
    b1 = cat([i["L0_ffn_b1"], i["L0_ffn_bs1"][None]]).reshape(9, 4, P).transpose(0, 2, 1)
    a["e0_wp"] = np.ascontiguousarray(cat([w1, w2, b1], 2))
    a["e0_b2"] = cat([i["L0_ffn_b2"], i["L0_ffn_bs2"][None]])
    a["l1_wx"] = i["L1_cond_Wx"].reshape(P, 4, P)
    a["l1_wh"] = i["L1_cond_Wh"].reshape(P, 4, P)
    a["l1_b"] = t(i["L1_cond_b"].reshape(4, P), 1, 0)
    a["l2_w"] = col(*(i[f"L2_cond_W_{k}"].T for k in "fih"))
    a["l2_b"] = col(*(i[f"L2_cond_b_{k}"] for k in "fih"))
    a["r2_w"] = t(i["L2_ffn_router_w"], 1, 0)
    dw = pad(t(i["L2_ffn_down_w"], 0, 2, 1), ((0, 0), (0, 32), (0, 0))).reshape(8, 3, P, P).transpose(0, 2, 1, 3)
    a["e2_wp"] = np.ascontiguousarray(cat([t(i["L2_ffn_gate_w"], 0, 2, 1), t(i["L2_ffn_up_w"], 0, 2, 1),
                                           dw.reshape(8, P, 3 * P)], 2))
    a["l3_w"] = col(i["L3_cond_W_z"], i["L3_cond_W_r"], i["L3_cond_W"])
    a["l3_u"] = col(i["L3_cond_U_z"], i["L3_cond_U_r"], i["L3_cond_U"])
    a["l3_c"] = col(i["L3_cond_C_z"], i["L3_cond_C_r"], i["L3_cond_C"])
    a["l3_b"] = col(i["L3_cond_b_z"], i["L3_cond_b_r"], i["L3_cond_b"])
    a["r3_w"] = t(i["L3_ffn_router_w"], 1, 0)
    a["r3_bias"] = np.ascontiguousarray(np.broadcast_to(i["L3_ffn_router_bias"], (P, 8)))
    a["e3_sw"] = cat([i["L3_ffn_sw1"], i["L3_ffn_sw3"],
                      i["L3_ffn_sw2"].reshape(2, P, P).transpose(1, 0, 2).reshape(P, 2 * P)], 1)
    a["e3_wp"] = cat([i["L3_ffn_ew1"], i["L3_ffn_ew2"]], 2)
    tab = (i["L1_ffn_A_up"].reshape(64, 64, 8, 4).transpose(0, 1, 3, 2), i["L1_ffn_B_up"],
           i["L1_ffn_A_down"], i["L1_ffn_B_down"])
    a["k_tab"] = np.stack([cat([v.reshape(64, 2048)] * 2) for v in tab])
    a["k_wup"] = i["L1_ffn_W_up"].reshape(64, 8, P).transpose(2, 1, 0)
    wd = i["L1_ffn_W_down"].reshape(64, 64, 64).transpose(2, 1, 0)
    a["k_wdown"] = cat([pad(wd, ((0, 0), (0, 0), (0, 64))), pad(wd, ((0, 0), (0, 0), (64, 0)))])
    a["k_bias_up"] = np.tile(i["L1_ffn_bias_up"].reshape(64, 64).T, (2, 2 * BPT))
    a["k_bias_down"] = i["L1_ffn_bias_down"].reshape(8, P).T
    a["k_scale_up"] = np.broadcast_to(i["L1_ffn_scale_up"][None], (P, 1))
    a["k_scale_down"] = np.broadcast_to(i["L1_ffn_scale_down"][None], (P, 1))
    a["k_cst"] = patterns()
    return {k: np.ascontiguousarray(v) for k, v in a.items()}


def patterns():
    p, c = np.arange(P)[:, None], np.arange(P)[None, :]
    parts = [
        p // 32 == c // 8 % 4,
        p // 32 == c // 32,
        (p // 64 == c // 32 % 2) & (p // 32 % 2 == c // 64),
        np.broadcast_to(c % 64, (P, P)),
        p % 32 == c[:, :32],
        p // 32 % 2 == c[:, :2],
    ]
    return np.concatenate([v.astype(np.float32) for v in parts], 1)


def kernel(**inputs):
    import concourse.bacc as bacc
    from concourse.bass_utils import run_bass_kernel_spmd as run

    arrays = lay_out({k: np.asarray(v) for k, v in inputs.items()})
    nc = bacc.Bacc("TRN2", target_bir_lowering=False, num_devices=1)
    d = {k: nc.dram_tensor("in_" + k, v.shape, mybir.dt.from_np(v.dtype), kind="ExternalInput").ap() for k, v in arrays.items()}
    out = nc.dram_tensor("out_x", (P, T, N), F32, kind="ExternalOutput").ap()
    scratch = nc.dram_tensor("gate_rows", (9, 1, TOK), F32, kind="Internal").ap()
    probs_up = nc.dram_tensor("probs_up", (4, 2 * BLK), F32, kind="Internal").ap()
    probs_down = nc.dram_tensor("probs_down", (2, 4 * BLK), F32, kind="Internal").ap()
    build(nc, d, out, scratch, probs_up, probs_down, LAYERS)
    r = run(nc, [{"in_" + k: v for k, v in arrays.items()}], core_ids=[0])
    return np.ascontiguousarray(np.transpose(r.results[0]["out_x"], (2, 1, 0)))
```
